# Optimizing a Trainium2 kernel written in Bass

```python
import numpy as np
import jax
import jax.numpy as jnp

def _softmax(x, axis=-1):
    return jax.nn.softmax(x, axis=axis)

def _gelu(x):
    return jax.nn.gelu(x, approximate=True)

def _silu(x):
    return jax.nn.silu(x)

def _sigmoid(x):
    return jax.nn.sigmoid(x)

def _layernorm(x, axis=-1, eps=1e-05):
    m = jnp.mean(x, axis=axis, keepdims=True)
    v = jnp.var(x, axis=axis, keepdims=True)
    return (x - m) / jnp.sqrt(v + eps)

def _scatter_add(tgt, idx, src, axis=0):
    return tgt.at[idx].add(src)

def _segment_sum(src, seg, n):
    return jax.ops.segment_sum(src, seg, n)
kernel_name = 'mk_sandwich_d1_jaxref_r8_c75906'

def setup_inputs(seed: int=0):
    np.random.seed(seed)
    _w = jnp.asarray

    def _L0_attn_setup():
        import jax, jax.numpy as jnp
        import numpy as np
        H = 128
        D = 32
        CHUNK = 64
        LR = 0.1
        GRAD_SCALE = 0.1
        MAX_GRAD_NORM = 1.0
        EPS = 1e-06
        P = 2 * D * D

        def _xavier(k, shape, gain=0.1):
            fan_out, fan_in = shape
            a = gain * np.sqrt(6.0 / (fan_in + fan_out))
            return jax.random.uniform(k, shape, jnp.float32, -a, a)

        def _causal_dwconv(x, w, b):
            T = x.shape[1]
            xp = jnp.pad(x, ((0, 0), (3, 0), (0, 0)))
            y = b
            for j in range(4):
                y = y + xp[:, j:j + T, :] * w[:, j]
            return y

        def _mem_loss(p, k_t, v_t):
            W1 = p[:D * D].reshape(D, D)
            W2 = p[D * D:].reshape(D, D)
            pred = jax.nn.silu(k_t @ W1.T) @ W2.T
            return jnp.sum((pred - v_t) ** 2)
        _grad_fn = jax.vmap(jax.vmap(jax.grad(_mem_loss), in_axes=(None, 0, 0)), in_axes=(0, 0, 0))

        def _forward(hidden, Wk, Wv, Wq, Wo, ckw, ckb, cvw, cvb, cqw, cqb, mW1, mW2, aW, ab, eW, eb, tW, tb, norm_g, gW, gb):
            B, S, _ = hidden.shape
            k = _causal_dwconv(hidden @ Wk.T, ckw, ckb)
            v = _causal_dwconv(hidden @ Wv.T, cvw, cvb)
            q = _causal_dwconv(hidden @ Wq.T, cqw, cqb)
            alpha = (jax.nn.sigmoid(hidden @ aW.T + ab) * 0.1).mean(-1)
            eta = (jax.nn.sigmoid(hidden @ eW.T + eb) * 0.9 + 0.05).mean(-1)
            theta = (jax.nn.softplus(hidden @ tW.T + tb) * LR).mean(-1)
            W_state = jnp.tile(jnp.concatenate([mW1.ravel(), mW2.ravel()])[None], (B, 1))
            S_state = jnp.zeros_like(W_state)

            def step(carry, xs):
                Sm, Wm = carry
                gt, et, tt, at = xs
                Sm = et[:, None] * Sm - tt[:, None] * gt
                Wm = (1.0 - at[:, None]) * Wm + Sm
                return ((Sm, Wm), Wm)
            outs = []
            for c0 in range(0, S, CHUNK):
                sl = slice(c0, c0 + CHUNK)
                g = _grad_fn(W_state, k[:, sl], v[:, sl]) * GRAD_SCALE
                gn = jnp.maximum(jnp.linalg.norm(g, axis=-1, keepdims=True), EPS)
                g = g * jnp.minimum(MAX_GRAD_NORM / gn, 1.0)
                g = jax.lax.stop_gradient(g)
                xs = (jnp.swapaxes(g, 0, 1), eta[:, sl].T, theta[:, sl].T, alpha[:, sl].T)
                (S_state, W_state), Wtraj = jax.lax.scan(step, (S_state, W_state), xs)
                Wtraj = jnp.swapaxes(Wtraj, 0, 1)
                T = Wtraj.shape[1]
                W1t = Wtraj[..., :D * D].reshape(B, T, D, D)
                W2t = Wtraj[..., D * D:].reshape(B, T, D, D)
                h = jax.nn.silu(jnp.einsum('btd,btod->bto', q[:, sl], W1t))
                outs.append(jnp.einsum('bto,btpo->btp', h, W2t))
            retrieved = jnp.concatenate(outs, axis=1)
            out = retrieved @ Wo.T
            out = out * jax.lax.rsqrt(jnp.mean(out * out, -1, keepdims=True) + EPS) * norm_g
            gate = hidden @ gW.T + gb
            return out * gate
        key = jax.random.key(seed)
        ks = jax.random.split(key, 24)
        B, S = (1, 128)
        return {'hidden': jax.random.normal(ks[0], (B, S, H), jnp.float32), 'Wk': _xavier(ks[1], (D, H)), 'Wv': _xavier(ks[2], (D, H)), 'Wq': _xavier(ks[3], (D, H)), 'Wo': _xavier(ks[4], (H, D)), 'ckw': jax.random.normal(ks[5], (D, 4), jnp.float32) * 0.05, 'ckb': jnp.zeros((D,), jnp.float32), 'cvw': jax.random.normal(ks[6], (D, 4), jnp.float32) * 0.05, 'cvb': jnp.zeros((D,), jnp.float32), 'cqw': jax.random.normal(ks[7], (D, 4), jnp.float32) * 0.05, 'cqb': jnp.zeros((D,), jnp.float32), 'mW1': _xavier(ks[8], (D, D)), 'mW2': _xavier(ks[9], (D, D)), 'aW': jax.random.normal(ks[10], (D, H), jnp.float32) * 0.02, 'ab': jnp.zeros((D,), jnp.float32), 'eW': jax.random.normal(ks[11], (D, H), jnp.float32) * 0.02, 'eb': jnp.zeros((D,), jnp.float32), 'tW': jax.random.normal(ks[12], (D, H), jnp.float32) * 0.02, 'tb': jnp.zeros((D,), jnp.float32), 'norm_g': jnp.ones((H,), jnp.float32), 'gW': jnp.zeros((H, H), jnp.float32), 'gb': jnp.ones((H,), jnp.float32)}
    _L0_attn_in = _L0_attn_setup()

    def _L0_ffn_setup():
        import jax, jax.numpy as jnp
        import numpy as np
        DIM = 128
        DEPTH = 6
        HEADS = 16
        DIM_HEAD = 64
        WINDOW = 32
        INNER = HEADS * DIM_HEAD
        DIM_INNER = int(DIM * 4 * 2 / 3)
        QK_SCALE = 8.0

        def shift_tokens(t):
            a, s = jnp.split(t, 2, -1)
            s = jnp.pad(s, ((0, 0), (1, 0), (0, 0)))[:, :-1]
            return jnp.concatenate([a, s], -1)

        def l2norm(t):
            return t / jnp.maximum(jnp.linalg.norm(t, axis=-1, keepdims=True), 1e-12)

        def rotate_half(x):
            x1, x2 = jnp.split(x, 2, -1)
            return jnp.concatenate([-x2, x1], -1)

        def rotary_tables(n):
            half = jnp.arange(0, DIM_HEAD, 2, dtype=jnp.float32)
            inv_freq = 1.0 / 10000.0 ** (half / DIM_HEAD)
            t = jnp.arange(n, dtype=jnp.float32)
            freqs = t[:, None] * inv_freq[None, :]
            freqs = jnp.concatenate([freqs, freqs], -1)
            base_scale = (half + 0.4 * DIM_HEAD) / (1.4 * DIM_HEAD)
            power = (t - n // 2) / (WINDOW // 2)
            scale = base_scale[None, :] ** power[:, None]
            scale = jnp.concatenate([scale, scale], -1)
            return (freqs, scale)

        def local_attention(q, k, v):
            b, h, n, d = q.shape
            w = WINDOW
            nw = n // w
            bq = q.reshape(b, h, nw, w, d)
            bk = k.reshape(b, h, nw, w, d)
            bv = v.reshape(b, h, nw, w, d)

            def look(t):
                p = jnp.pad(t, ((0, 0), (0, 0), (1, 0), (0, 0), (0, 0)))
                return jnp.concatenate([p[:, :, :nw], p[:, :, 1:]], axis=3)
            bk2, bv2 = (look(bk), look(bv))
            seq = jnp.arange(n).reshape(nw, w)
            seq_p = jnp.pad(seq, ((1, 0), (0, 0)), constant_values=-1)
            jt = jnp.concatenate([seq_p[:nw], seq_p[1:]], axis=1)
            it = seq[:, :, None]
            jb = jt[:, None, :]
            mask = (it < jb) | (it > jb + w) | (jb == -1)
            sim = jnp.einsum('bhwie,bhwje->bhwij', bq, bk2) * QK_SCALE
            sim = jnp.where(mask, -jnp.finfo(sim.dtype).max, sim)
            attn = jax.nn.softmax(sim, -1)
            out = jnp.einsum('bhwij,bhwje->bhwie', attn, bv2)
            return out.reshape(b, h, n, d)

        def attn_layer(x, Wqkv, qs, ksc, Wo):
            b, n, _ = x.shape
            qkv = x @ Wqkv
            q, k, v = jnp.split(qkv, 3, -1)
            sh = lambda t: t.reshape(b, n, HEADS, DIM_HEAD).transpose(0, 2, 1, 3)
            q, k, v = (sh(q), sh(k), sh(v))
            q = l2norm(q) * qs
            k = l2norm(k) * ksc
            freqs, scale = rotary_tables(n)
            cos, sin = (jnp.cos(freqs), jnp.sin(freqs))
            q = q * cos * scale + rotate_half(q) * sin * scale
            inv = 1.0 / scale
            k = k * cos * inv + rotate_half(k) * sin * inv
            out = local_attention(q, k, v)
            out = out.transpose(0, 2, 1, 3).reshape(b, n, INNER)
            return out @ Wo

        def ffn_layer(x, g, bln, W1, b1, W2, b2):
            mu = x.mean(-1, keepdims=True)
            var = ((x - mu) ** 2).mean(-1, keepdims=True)
            xn = (x - mu) / jnp.sqrt(var + 1e-05) * g + bln
            hg = xn @ W1 + b1
            a, gate = jnp.split(hg, 2, -1)
            return a * jax.nn.gelu(gate, approximate=False) @ W2 + b2
        key = jax.random.key(seed)
        ks = jax.random.split(key, 8)
        B, N = (2, 256)
        init = lambda k, shape: jax.random.normal(k, shape, jnp.float32) * 0.02
        return {'x': jax.random.normal(ks[0], (B, N, DIM), jnp.float32), 'Wqkv': init(ks[1], (DEPTH, DIM, 3 * INNER)), 'q_scale': jnp.ones((DEPTH, DIM_HEAD), jnp.float32), 'k_scale': jnp.ones((DEPTH, DIM_HEAD), jnp.float32), 'Wo': init(ks[2], (DEPTH, INNER, DIM)), 'ln_g': jnp.ones((DEPTH, DIM), jnp.float32), 'ln_b': jnp.zeros((DEPTH, DIM), jnp.float32), 'W1': init(ks[3], (DEPTH, DIM, 2 * DIM_INNER)), 'b1': jnp.zeros((DEPTH, 2 * DIM_INNER), jnp.float32), 'W2': init(ks[4], (DEPTH, DIM_INNER, DIM)), 'b2': jnp.zeros((DEPTH, DIM), jnp.float32)}
    _L0_ffn_in = _L0_ffn_setup()
    _d = {'L0_attn_hidden': _L0_attn_in['hidden'], 'L0_attn_Wk': _L0_attn_in['Wk'], 'L0_attn_Wv': _L0_attn_in['Wv'], 'L0_attn_Wq': _L0_attn_in['Wq'], 'L0_attn_Wo': _L0_attn_in['Wo'], 'L0_attn_ckw': _L0_attn_in['ckw'], 'L0_attn_ckb': _L0_attn_in['ckb'], 'L0_attn_cvw': _L0_attn_in['cvw'], 'L0_attn_cvb': _L0_attn_in['cvb'], 'L0_attn_cqw': _L0_attn_in['cqw'], 'L0_attn_cqb': _L0_attn_in['cqb'], 'L0_attn_mW1': _L0_attn_in['mW1'], 'L0_attn_mW2': _L0_attn_in['mW2'], 'L0_attn_aW': _L0_attn_in['aW'], 'L0_attn_ab': _L0_attn_in['ab'], 'L0_attn_eW': _L0_attn_in['eW'], 'L0_attn_eb': _L0_attn_in['eb'], 'L0_attn_tW': _L0_attn_in['tW'], 'L0_attn_tb': _L0_attn_in['tb'], 'L0_attn_norm_g': _L0_attn_in['norm_g'], 'L0_attn_gW': _L0_attn_in['gW'], 'L0_attn_gb': _L0_attn_in['gb'], 'L0_ffn_Wqkv': _L0_ffn_in['Wqkv'], 'L0_ffn_q_scale': _L0_ffn_in['q_scale'], 'L0_ffn_k_scale': _L0_ffn_in['k_scale'], 'L0_ffn_Wo': _L0_ffn_in['Wo'], 'L0_ffn_ln_g': _L0_ffn_in['ln_g'], 'L0_ffn_ln_b': _L0_ffn_in['ln_b'], 'L0_ffn_W1': _L0_ffn_in['W1'], 'L0_ffn_b1': _L0_ffn_in['b1'], 'L0_ffn_W2': _L0_ffn_in['W2'], 'L0_ffn_b2': _L0_ffn_in['b2']}
    _x0 = _d['L0_attn_hidden']
    _d['L0_attn_hidden'] = jax.random.normal(jax.random.fold_in(jax.random.key(seed), 1), (4, 1024, 128), dtype=_x0.dtype)
    del _x0
    return _d

def reference(L0_attn_hidden, L0_attn_Wk, L0_attn_Wv, L0_attn_Wq, L0_attn_Wo, L0_attn_ckw, L0_attn_ckb, L0_attn_cvw, L0_attn_cvb, L0_attn_cqw, L0_attn_cqb, L0_attn_mW1, L0_attn_mW2, L0_attn_aW, L0_attn_ab, L0_attn_eW, L0_attn_eb, L0_attn_tW, L0_attn_tb, L0_attn_norm_g, L0_attn_gW, L0_attn_gb, L0_ffn_Wqkv, L0_ffn_q_scale, L0_ffn_k_scale, L0_ffn_Wo, L0_ffn_ln_g, L0_ffn_ln_b, L0_ffn_W1, L0_ffn_b1, L0_ffn_W2, L0_ffn_b2):

    def _L0_attn_ref(hidden, Wk, Wv, Wq, Wo, ckw, ckb, cvw, cvb, cqw, cqb, mW1, mW2, aW, ab, eW, eb, tW, tb, norm_g, gW, gb):
        import jax, jax.numpy as jnp
        import numpy as np
        H = 128
        D = 32
        CHUNK = 64
        LR = 0.1
        GRAD_SCALE = 0.1
        MAX_GRAD_NORM = 1.0
        EPS = 1e-06
        P = 2 * D * D

        def _xavier(k, shape, gain=0.1):
            fan_out, fan_in = shape
            a = gain * np.sqrt(6.0 / (fan_in + fan_out))
            return jax.random.uniform(k, shape, jnp.float32, -a, a)

        def _causal_dwconv(x, w, b):
            T = x.shape[1]
            xp = jnp.pad(x, ((0, 0), (3, 0), (0, 0)))
            y = b
            for j in range(4):
                y = y + xp[:, j:j + T, :] * w[:, j]
            return y

        def _mem_loss(p, k_t, v_t):
            W1 = p[:D * D].reshape(D, D)
            W2 = p[D * D:].reshape(D, D)
            pred = jax.nn.silu(k_t @ W1.T) @ W2.T
            return jnp.sum((pred - v_t) ** 2)
        _grad_fn = jax.vmap(jax.vmap(jax.grad(_mem_loss), in_axes=(None, 0, 0)), in_axes=(0, 0, 0))

        def _forward(hidden, Wk, Wv, Wq, Wo, ckw, ckb, cvw, cvb, cqw, cqb, mW1, mW2, aW, ab, eW, eb, tW, tb, norm_g, gW, gb):
            B, S, _ = hidden.shape
            k = _causal_dwconv(hidden @ Wk.T, ckw, ckb)
            v = _causal_dwconv(hidden @ Wv.T, cvw, cvb)
            q = _causal_dwconv(hidden @ Wq.T, cqw, cqb)
            alpha = (jax.nn.sigmoid(hidden @ aW.T + ab) * 0.1).mean(-1)
            eta = (jax.nn.sigmoid(hidden @ eW.T + eb) * 0.9 + 0.05).mean(-1)
            theta = (jax.nn.softplus(hidden @ tW.T + tb) * LR).mean(-1)
            W_state = jnp.tile(jnp.concatenate([mW1.ravel(), mW2.ravel()])[None], (B, 1))
            S_state = jnp.zeros_like(W_state)

            def step(carry, xs):
                Sm, Wm = carry
                gt, et, tt, at = xs
                Sm = et[:, None] * Sm - tt[:, None] * gt
                Wm = (1.0 - at[:, None]) * Wm + Sm
                return ((Sm, Wm), Wm)
            outs = []
            for c0 in range(0, S, CHUNK):
                sl = slice(c0, c0 + CHUNK)
                g = _grad_fn(W_state, k[:, sl], v[:, sl]) * GRAD_SCALE
                gn = jnp.maximum(jnp.linalg.norm(g, axis=-1, keepdims=True), EPS)
                g = g * jnp.minimum(MAX_GRAD_NORM / gn, 1.0)
                g = jax.lax.stop_gradient(g)
                xs = (jnp.swapaxes(g, 0, 1), eta[:, sl].T, theta[:, sl].T, alpha[:, sl].T)
                (S_state, W_state), Wtraj = jax.lax.scan(step, (S_state, W_state), xs)
                Wtraj = jnp.swapaxes(Wtraj, 0, 1)
                T = Wtraj.shape[1]
                W1t = Wtraj[..., :D * D].reshape(B, T, D, D)
                W2t = Wtraj[..., D * D:].reshape(B, T, D, D)
                h = jax.nn.silu(jnp.einsum('btd,btod->bto', q[:, sl], W1t))
                outs.append(jnp.einsum('bto,btpo->btp', h, W2t))
            retrieved = jnp.concatenate(outs, axis=1)
            out = retrieved @ Wo.T
            out = out * jax.lax.rsqrt(jnp.mean(out * out, -1, keepdims=True) + EPS) * norm_g
            gate = hidden @ gW.T + gb
            return out * gate
        return _forward(hidden, Wk, Wv, Wq, Wo, ckw, ckb, cvw, cvb, cqw, cqb, mW1, mW2, aW, ab, eW, eb, tW, tb, norm_g, gW, gb)

    def _L0_ffn_ref(x, Wqkv, q_scale, k_scale, Wo, ln_g, ln_b, W1, b1, W2, b2):
        import jax, jax.numpy as jnp
        import numpy as np
        DIM = 128
        DEPTH = 6
        HEADS = 16
        DIM_HEAD = 64
        WINDOW = 32
        INNER = HEADS * DIM_HEAD
        DIM_INNER = int(DIM * 4 * 2 / 3)
        QK_SCALE = 8.0

        def shift_tokens(t):
            a, s = jnp.split(t, 2, -1)
            s = jnp.pad(s, ((0, 0), (1, 0), (0, 0)))[:, :-1]
            return jnp.concatenate([a, s], -1)

        def l2norm(t):
            return t / jnp.maximum(jnp.linalg.norm(t, axis=-1, keepdims=True), 1e-12)

        def rotate_half(x):
            x1, x2 = jnp.split(x, 2, -1)
            return jnp.concatenate([-x2, x1], -1)

        def rotary_tables(n):
            half = jnp.arange(0, DIM_HEAD, 2, dtype=jnp.float32)
            inv_freq = 1.0 / 10000.0 ** (half / DIM_HEAD)
            t = jnp.arange(n, dtype=jnp.float32)
            freqs = t[:, None] * inv_freq[None, :]
            freqs = jnp.concatenate([freqs, freqs], -1)
            base_scale = (half + 0.4 * DIM_HEAD) / (1.4 * DIM_HEAD)
            power = (t - n // 2) / (WINDOW // 2)
            scale = base_scale[None, :] ** power[:, None]
            scale = jnp.concatenate([scale, scale], -1)
            return (freqs, scale)

        def local_attention(q, k, v):
            b, h, n, d = q.shape
            w = WINDOW
            nw = n // w
            bq = q.reshape(b, h, nw, w, d)
            bk = k.reshape(b, h, nw, w, d)
            bv = v.reshape(b, h, nw, w, d)

            def look(t):
                p = jnp.pad(t, ((0, 0), (0, 0), (1, 0), (0, 0), (0, 0)))
                return jnp.concatenate([p[:, :, :nw], p[:, :, 1:]], axis=3)
            bk2, bv2 = (look(bk), look(bv))
            seq = jnp.arange(n).reshape(nw, w)
            seq_p = jnp.pad(seq, ((1, 0), (0, 0)), constant_values=-1)
            jt = jnp.concatenate([seq_p[:nw], seq_p[1:]], axis=1)
            it = seq[:, :, None]
            jb = jt[:, None, :]
            mask = (it < jb) | (it > jb + w) | (jb == -1)
            sim = jnp.einsum('bhwie,bhwje->bhwij', bq, bk2) * QK_SCALE
            sim = jnp.where(mask, -jnp.finfo(sim.dtype).max, sim)
            attn = jax.nn.softmax(sim, -1)
            out = jnp.einsum('bhwij,bhwje->bhwie', attn, bv2)
            return out.reshape(b, h, n, d)

        def attn_layer(x, Wqkv, qs, ksc, Wo):
            b, n, _ = x.shape
            qkv = x @ Wqkv
            q, k, v = jnp.split(qkv, 3, -1)
            sh = lambda t: t.reshape(b, n, HEADS, DIM_HEAD).transpose(0, 2, 1, 3)
            q, k, v = (sh(q), sh(k), sh(v))
            q = l2norm(q) * qs
            k = l2norm(k) * ksc
            freqs, scale = rotary_tables(n)
            cos, sin = (jnp.cos(freqs), jnp.sin(freqs))
            q = q * cos * scale + rotate_half(q) * sin * scale
            inv = 1.0 / scale
            k = k * cos * inv + rotate_half(k) * sin * inv
            out = local_attention(q, k, v)
            out = out.transpose(0, 2, 1, 3).reshape(b, n, INNER)
            return out @ Wo

        def ffn_layer(x, g, bln, W1, b1, W2, b2):
            mu = x.mean(-1, keepdims=True)
            var = ((x - mu) ** 2).mean(-1, keepdims=True)
            xn = (x - mu) / jnp.sqrt(var + 1e-05) * g + bln
            hg = xn @ W1 + b1
            a, gate = jnp.split(hg, 2, -1)
            return a * jax.nn.gelu(gate, approximate=False) @ W2 + b2
        for i in range(DEPTH):
            x = attn_layer(shift_tokens(x), Wqkv[i], q_scale[i], k_scale[i], Wo[i]) + x
            x = ffn_layer(shift_tokens(x), ln_g[i], ln_b[i], W1[i], b1[i], W2[i], b2[i]) + x
        return x
    x = L0_attn_hidden
    x = x + _layernorm(_L0_attn_ref(_layernorm(x, axis=-1), L0_attn_Wk, L0_attn_Wv, L0_attn_Wq, L0_attn_Wo, L0_attn_ckw, L0_attn_ckb, L0_attn_cvw, L0_attn_cvb, L0_attn_cqw, L0_attn_cqb, L0_attn_mW1, L0_attn_mW2, L0_attn_aW, L0_attn_ab, L0_attn_eW, L0_attn_eb, L0_attn_tW, L0_attn_tb, L0_attn_norm_g, L0_attn_gW, L0_attn_gb), axis=-1)
    x = x + _layernorm(_L0_ffn_ref(_layernorm(x, axis=-1), L0_ffn_Wqkv, L0_ffn_q_scale, L0_ffn_k_scale, L0_ffn_Wo, L0_ffn_ln_g, L0_ffn_ln_b, L0_ffn_W1, L0_ffn_b1, L0_ffn_W2, L0_ffn_b2), axis=-1)
    return x

_drawn_inputs = setup_inputs


def setup_inputs(seed=0):
    import zlib

    import numpy as np

    out = dict(_drawn_inputs(seed))
    spreads = {'L0_attn_ckb': (0.0, 0.404),
     'L0_attn_cvb': (0.0, 0.399),
     'L0_attn_cqb': (0.0, 0.1),
     'L0_attn_ab': (0.0, 0.8),
     'L0_attn_eb': (0.0, 0.8),
     'L0_attn_tb': (0.0, 0.8),
     'L0_attn_norm_g': (1.0, 0.576),
     'L0_attn_gW': (0.0, 0.1),
     'L0_attn_gb': (1.0, 0.6),
     'L0_ffn_q_scale': (1.0, 0.6),
     'L0_ffn_k_scale': (1.0, 0.6),
     'L0_ffn_ln_g': (1.0, 0.6),
     'L0_ffn_ln_b': (0.0, 0.8),
     'L0_ffn_b1': (0.0, 0.8),
     'L0_ffn_b2': (0.0, 0.1)}
    factors = {'L0_attn_Wk': 8.0,
     'L0_attn_Wv': 8.0,
     'L0_attn_Wq': 4.633,
     'L0_attn_ckw': 8.0,
     'L0_attn_cvw': 8.0,
     'L0_attn_cqw': 4.421,
     'L0_attn_aW': 8.0,
     'L0_attn_eW': 8.0,
     'L0_attn_tW': 8.0,
     'L0_ffn_W1': 3.757,
     'L0_ffn_W2': 3.688}
    for name, (base, spread) in spreads.items():
        noise = np.random.default_rng([zlib.crc32(name.encode()), seed]).standard_normal(out[name].shape)
        drawn = base * np.exp(spread * noise) if base else spread * noise
        out[name] = jnp.asarray(drawn.astype(out[name].dtype))
    for name, factor in factors.items():
        out[name] = (out[name] * factor).astype(out[name].dtype)
    return out
```

```python
from contextlib import ExitStack

import numpy as np

import concourse.bass as bass
from concourse import mybir

ALU = mybir.AluOpType
ACT = mybir.ActivationFunctionType
AX = mybir.AxisListType
F32 = mybir.dt.float32
BF16 = mybir.dt.bfloat16

P = 128
LN_EXP = "natural_log_exp_and_others"
SIGMOID = "sigmoid_and_others"


def transformer(nc, x_mid, Wqkv, q_scale, k_scale, Wo, ln_g, ln_b, W1, b1, W2, b2,
                rotary, masks, ident_in, center_in, out, DEPTH=6):
    DIM = Wqkv.shape[1]
    INNER = Wo.shape[1]
    DH = q_scale.shape[1]
    HEADS = INNER // DH
    PAIRS = HEADS // 2
    HALF = DH // 2
    B = 4
    WIN = P // B
    NW = x_mid.shape[1] // DIM
    HID = W2.shape[1]
    HC = -(-HID // P)
    LAYERS = DEPTH
    TILES = LAYERS * NW
    QKS = 8.0
    LOG2_SHIFT = 20
    assert DIM == P and HEADS == 16 and DH == 64 and WIN == 32

    with ExitStack() as ctx:
        def sb(name, shape, dt=F32):
            return ctx.enter_context(nc.sbuf_tensor(name, shape, dt))

        def sem(name):
            return nc.alloc_semaphore(name)

        X = sb("X", [P, NW * DIM])
        tab = sb("tab", [P, NW * 4 * HALF])
        wqkv = sb("wqkv", [P, 2, 3 * INNER])
        wo = sb("wo", [P, 2, PAIRS * DIM])
        w1 = sb("w1", [P, LAYERS, 2 * HID])
        b1b = sb("b1b", [P, LAYERS, 2 * HID])
        w2 = sb("w2", [P, LAYERS, HC * DIM])
        b2b = sb("b2b", [P, LAYERS, DIM])
        qks = sb("qks", [P, LAYERS, 4 * DH])
        ident = sb("ident", [P, P])
        center = sb("center", [P, P])
        identb = sb("identb", [P, P], BF16)
        maskb = sb("maskb", [P, 3 * PAIRS * 2 * WIN], BF16)
        first = sb("first", [P, NW])

        R0 = ctx.enter_context(nc.psum_tensor("R0", [P, 1024], F32))
        R1 = ctx.enter_context(nc.psum_tensor("R1", [P, 1024], F32))
        R2 = ctx.enter_context(nc.psum_tensor("R2", [P, 1024], F32))
        b6 = ctx.enter_context(nc.psum_tensor("b6", [P, 512], F32))
        b7 = ctx.enter_context(nc.psum_tensor("b7", [P, 512], F32))

        wqkv_in = sem("wqkv_in")
        wo_in = sem("wo_in")
        x_ready = sem("x_ready")
        prep(nc, ctx, locals())
        stream(nc, ctx, locals())
        finish(nc, ctx, locals())


def prep(nc, ctx0, e):
    (X, tab, wqkv, wo, w1, b1b, w2, b2b, qks, ident, center, identb, maskb, first, R0, R1) = (e[k] for k in (
        "X", "tab", "wqkv", "wo", "w1", "b1b", "w2", "b2b", "qks", "ident", "center", "identb", "maskb", "first", "R0", "R1"))
    DIM, DH, HALF, NW, HID, HC, LAYERS, PAIRS, WIN = (e[k] for k in ("DIM", "DH", "HALF", "NW", "HID", "HC", "LAYERS", "PAIRS", "WIN"))
    G = 4
    GROUPS = NW // G
    with ExitStack() as ctx:
        def sb(name, shape, dt=F32):
            return ctx.enter_context(nc.sbuf_tensor(name, shape, dt))

        def sem(name):
            return nc.alloc_semaphore(name)

        w1r = sb("w1r", [P, 2, 2 * HID])
        lng = sb("lng", [P, LAYERS])
        lnb = sb("lnb", [P, LAYERS])
        ones = sb("ones", [P, P])
        brep = sb("brep", [P, LAYERS, P])
        maskf = sb("maskf", [P, 3, 2 * WIN])
        m_in = sem("m_in"); s_in = sem("s_in"); x_in = sem("x_in"); w1_in = [sem("w1_in0"), sem("w1_in1")]
        v = sem("v_step"); w1_mm = sem("w1_mm"); b1_mm = sem("b1_mm"); w1_ev = sem("w1_ev"); pad_done = sem("pad_done")
        w1g_ready = sem("w1g_ready"); brep_ready = sem("brep_ready")
        block = ctx.enter_context(nc.Block())
        wi, wo_s = e["wqkv_in"], e["wo_in"]

        @block.sync
        def _(sp):
            sp.dma_start(X[:, :], e["x_mid"]).then_inc(x_in, 16)
            sp.dma_start(ident[:, :], e["ident_in"]).then_inc(s_in, 16)
            sp.dma_start(center[:, :], e["center_in"]).then_inc(s_in, 16)
            sp.dma_start(maskf[:, :, :], e["masks"]).then_inc(s_in, 16)
            sp.dma_start(lng[:, :], e["ln_g"]).then_inc(s_in, 16)
            sp.dma_start(lnb[:, :], e["ln_b"]).then_inc(s_in, 16)
            sp.dma_start(b1b[:, :, :], e["b1"].unsqueeze(0).to_broadcast([P, LAYERS, 2 * HID])).then_inc(s_in, 16)
            sp.dma_start(b2b[:, :, :], e["b2"].unsqueeze(0).to_broadcast([P, LAYERS, DIM])).then_inc(s_in, 16)
            sp.dma_start(wqkv[:, 0, :], e["Wqkv"][0]).then_inc(wi, 16)
            sp.dma_start(wo[:, 0, :].rearrange("p (c n) -> p c n", n=DIM),
                         e["Wo"][0].rearrange("(c p) n -> p c n", p=P)).then_inc(wo_s, 16)

        @block.scalar
        def _(act):
            for l in range(LAYERS):
                if l >= 2:
                    act.wait_ge(w1g_ready, l - 1)
                    act.wait_ge(b1_mm, l - 1)
                act.dma_start(w1r[:, l % 2, :], e["W1"][l]).then_inc(w1_in[l % 2], 16)
            act.dma_start(tab[:, :], e["rotary"]).then_inc(m_in, 16)
            qv = qks[:, :, :].rearrange("p l (c d) -> p l c d", d=DH)
            for c, s in ((0, e["q_scale"]), (2, e["k_scale"])):
                s = s.unsqueeze(0).to_broadcast([P, LAYERS, DH])
                act.dma_start(qv[:, :, c, :], s).then_inc(m_in, 16)
                act.dma_start(qv[:, :, c + 1, 0:HALF], s[:, :, HALF:DH]).then_inc(m_in, 16)
                act.dma_start(qv[:, :, c + 1, HALF:DH], s[:, :, 0:HALF]).then_inc(m_in, 16)
            act.wait_ge(pad_done, 1)
            w2v = w2[:, :, :].rearrange("p l (c n) -> p l c n", n=DIM)
            for c in range(HC):
                n = min(P, HID - c * P)
                act.dma_start(w2v[0:n, :, c, :], e["W2"][0:LAYERS, c * P:c * P + n, :].rearrange("l p n -> p l n")).then_inc(m_in, 16)
            act.wait_ge(m_in, 16 * (7 + HC))

        @block.tensor
        def _(pe):
            pe.wait_ge(s_in, 16 * 7)
            for l in range(LAYERS):
                pe.wait_ge(brep_ready, l + 1)
                pe.wait_ge(w1_in[l % 2], 16 * (l // 2 + 1))
                if l >= 1:
                    pe.wait_ge(w1_ev, 2 * l)
                for h in range(2):
                    mm = pe.matmul(R0[:, 512 * h:512 * h + HID], brep[:, l, :], w1r[:, l % 2, h * HID:(h + 1) * HID],
                                   start=True, stop=True)
                mm.then_inc(b1_mm, 1)
                pe.wait_ge(w1g_ready, l + 1)
                for h in range(2):
                    mm = pe.matmul(R1[:, 512 * h:512 * h + HID], center[:, :], w1[:, l, h * HID:(h + 1) * HID],
                                   start=True, stop=True)
                mm.then_inc(w1_mm, 1)

        @block.vector
        def _(dve):
            steps = [0]

            def link(ins):
                steps[0] += 1
                ins.then_inc(v, 1)
                dve.wait_ge(v, steps[0])

            dve.memset(w2[:, :, :], 0.0).then_inc(pad_done, 1)
            dve.memset(ones[:, :], 1.0).then_inc(v, 1)
            dve.memset(first[:, :], 1.0).then_inc(v, 1)
            steps[0] = 2
            dve.wait_ge(v, 2)
            link(dve.memset(first[:, 0:1], 0.0))
            dve.wait_ge(s_in, 16 * 7)
            link(dve.tensor_copy(identb[:, :], ident[:, :]))
            link(dve.tensor_copy(maskb[:, :].rearrange("p (m c k) -> p m c k", m=3, c=PAIRS),
                                 maskf[:, :, :].unsqueeze(2).to_broadcast([P, 3, PAIRS, 2 * WIN])))
            for l in range(LAYERS):
                dve.tensor_scalar(brep[:, l, :], ones[:, :], lnb[:, l:l + 1], None, ALU.mult).then_inc(brep_ready, 1)
            for l in range(LAYERS):
                dve.wait_ge(w1_in[l % 2], 16 * (l // 2 + 1))
                dve.tensor_scalar(w1[:, l, :], w1r[:, l % 2, :], lng[:, l:l + 1], None, ALU.mult).then_inc(w1g_ready, 1)
                dve.wait_ge(b1_mm, l + 1)
                bv = b1b[:, l, :].rearrange("p (h n) -> p h n", h=2)
                dve.tensor_tensor(bv, R0[:, :].rearrange("p (h n) -> p h n", h=2)[:, :, 0:HID], bv, ALU.add).then_inc(w1_ev, 1)
                dve.wait_ge(w1_mm, l + 1)
                dve.tensor_copy(w1[:, l, :].rearrange("p (h n) -> p h n", h=2),
                                R1[:, :].rearrange("p (h n) -> p h n", h=2)[:, :, 0:HID]).then_inc(w1_ev, 1)
            dve.wait_ge(m_in, 16 * (7 + HC))
            qv = qks[:, :, :].rearrange("p l (c d) -> p l c d", d=DH)
            for c in (1, 3):
                link(dve.tensor_scalar(qv[:, :, c, 0:HALF], qv[:, :, c, 0:HALF], -1.0, None, ALU.mult))
            dve.wait_ge(x_in, 16)
    layer_norm(nc, e, X, None, "mid")


def layer_norm(nc, e, X, resid, tag):
    DIM, NW = e["DIM"], e["NW"]
    G = 4
    GROUPS = NW // G
    N = G * DIM
    with ExitStack() as ctx:
        def sb(name, shape, dt=F32):
            return ctx.enter_context(nc.sbuf_tensor(name, shape, dt))

        def sem(name):
            return nc.alloc_semaphore(name)

        sq = sb(tag + "_sq", [P, 2, N])
        su = sb(tag + "_su", [P, GROUPS, G])
        va = sb(tag + "_va", [P, GROUPS, G])
        lg = sb(tag + "_lg", [P, GROUPS, G])
        rs = sb(tag + "_rs", [P, GROUPS, G])
        eps = sb(tag + "_eps", [P, 1])
        res = sb(tag + "_res", [P, 2, N])
        v = sem(tag + "_v"); cen = sem(tag + "_cen"); sqd = sem(tag + "_sq"); vard = sem(tag + "_var"); rsd = sem(tag + "_rs"); lgd = sem(tag + "_lg")
        r_in = [sem(tag + "_rin0"), sem(tag + "_rin1")]; done = sem(tag + "_done"); st = sem(tag + "_store")
        block = ctx.enter_context(nc.Block())

        def grp(t, g):
            return t[:, g * N:(g + 1) * N].rearrange("p (w n) -> p w n", n=DIM)

        @block.sync
        def _(sp):
            if resid is None:
                return
            for g in range(GROUPS):
                if g >= 2:
                    sp.wait_ge(done, g - 1)
                sp.dma_start(res[:, g % 2, :], resid[:, g * N:(g + 1) * N]).then_inc(r_in[g % 2], 16)
                if g >= 1:
                    sp.wait_ge(done, g)
                    sp.dma_start(e["out"][:, (g - 1) * N:g * N], X[:, (g - 1) * N:g * N]).then_inc(st, 16)
            sp.wait_ge(done, GROUPS)
            sp.dma_start(e["out"][:, (GROUPS - 1) * N:GROUPS * N], X[:, (GROUPS - 1) * N:GROUPS * N]).then_inc(st, 16)
            sp.wait_ge(st, 16 * GROUPS)

        def rstd(act, g):
            act.wait_ge(vard, g + 1)
            act.activation(lg[:, g, :], va[:, g, :], ACT.Ln, bias=eps[:, 0:1], scale=1.0 / DIM).then_inc(lgd, 1)
            act.wait_ge(lgd, g + 1)
            act.activation(rs[:, g, :], lg[:, g, :], ACT.Exp, scale=-0.5).then_inc(rsd, 1)

        @block.scalar
        def _(act):
            act.preload_act_table_set(LN_EXP)
            act.wait_ge(v, 1)
            for g in range(GROUPS):
                act.wait_ge(cen, g + 1)
                if g >= 2:
                    act.wait_ge(vard, g - 1)
                act.activation(sq[:, g % 2, :], X[:, g * N:(g + 1) * N], ACT.Square).then_inc(sqd, 1)
                if g >= 1:
                    rstd(act, g - 1)
            rstd(act, GROUPS - 1)

        @block.vector
        def _(dve):
            steps = [1]

            def link(ins):
                steps[0] += 1
                ins.then_inc(v, 1)
                dve.wait_ge(v, steps[0])

            dve.memset(eps[:, :], 1e-5).then_inc(v, 1)

            def centre(g):
                link(dve.tensor_reduce(su[:, g, :], grp(X, g), AX.X, ALU.add))
                link(dve.tensor_scalar(su[:, g, :], su[:, g, :], 1.0 / DIM, None, ALU.mult))
                dve.tensor_tensor(grp(X, g), grp(X, g), su[:, g, :].unsqueeze(2).to_broadcast([P, G, DIM]),
                                  ALU.subtract).then_inc(cen, 1)

            def variance(g):
                dve.wait_ge(sqd, g + 1)
                dve.tensor_reduce(va[:, g, :], sq[:, g % 2, :].rearrange("p (w n) -> p w n", n=DIM), AX.X,
                                  ALU.add).then_inc(vard, 1)

            def scale(g):
                dve.wait_ge(rsd, g + 1)
                ins = dve.tensor_tensor(grp(X, g), grp(X, g), rs[:, g, :].unsqueeze(2).to_broadcast([P, G, DIM]), ALU.mult)
                if resid is None:
                    ins.then_inc(done, 1)
                    return
                link(ins)
                dve.wait_ge(r_in[g % 2], 16 * (g // 2 + 1))
                dve.tensor_tensor(X[:, g * N:(g + 1) * N], X[:, g * N:(g + 1) * N], res[:, g % 2, :], ALU.add).then_inc(done, 1)

            for g in range(GROUPS + 2):
                if g < GROUPS:
                    centre(g)
                if 1 <= g <= GROUPS:
                    variance(g - 1)
                if g >= 2:
                    scale(g - 2)

        if resid is None and e["x_ready"] is not None:
            @block.gpsimd
            def _(pool):
                pool.wait_ge(done, GROUPS)
                pool.sem_inc(e["x_ready"], NW)


def finish(nc, ctx0, e):
    layer_norm(nc, e, e["X"], e["x_mid"], "last")


def stream(nc, ctx0, e):
    (X, tab, wqkv, wo, w1, b1b, w2, b2b, qks, ident, center, identb, maskb, first, R0, R1, R2, b6, b7) = (e[k] for k in (
        "X", "tab", "wqkv", "wo", "w1", "b1b", "w2", "b2b", "qks", "ident", "center", "identb", "maskb", "first",
        "R0", "R1", "R2", "b6", "b7"))
    DIM, DH, HALF, NW, HID, HC, LAYERS, PAIRS, WIN, HEADS, INNER, TILES, B = (e[k] for k in (
        "DIM", "DH", "HALF", "NW", "HID", "HC", "LAYERS", "PAIRS", "WIN", "HEADS", "INNER", "TILES", "B"))
    QKS, SHIFT = e["QKS"], e["LOG2_SHIFT"]
    wqkv_in, wo_in, x_ready = e["wqkv_in"], e["wo_in"], e["x_ready"]
    K2 = 2 * WIN
    HS = PAIRS * K2
    with ExitStack() as ctx:
        def sb(name, shape, dt=F32):
            return ctx.enter_context(nc.sbuf_tensor(name, shape, dt))

        def sem(name):
            return nc.alloc_semaphore(name)

        xs = sb("xs", [P, DIM])
        XS = sb("XS", [P, B, WIN])
        XS2 = sb("XS2", [P, B, WIN])
        cx = sb("cx", [P, B])
        cx2 = sb("cx2", [P, B])
        sq = sb("sq", [P, 2 * INNER])
        ss = sb("ss", [P, 2 * HEADS])
        lss = sb("lss", [P, 2 * HEADS])
        rn = sb("rn", [P, 2 * HEADS])
        nqk = sb("nqk", [P, 2 * INNER])
        t1 = sb("t1", [P, 2 * INNER])
        t2 = sb("t2", [P, 2 * INNER])
        tb = sb("tb", [P, 4 * DH])
        QT = sb("QT", [P, PAIRS, P])
        KT = sb("KT", [P, 2, PAIRS, P])
        mx = sb("mx", [P, HEADS])
        pr = sb("pr", [P, PAIRS, 2, K2])
        sm = sb("sm", [P, PAIRS, 2])
        rc = sb("rc", [P, HEADS])
        On = sb("On", [P, INNER])
        PT = sb("PT", [P, PAIRS, P])
        Vn = sb("Vn", [P, 2, PAIRS * DH])
        V2 = sb("V2", [P, B, PAIRS * DH])
        OT = sb("OT", [P, PAIRS, P])
        x1 = sb("x1", [P, DIM])
        x1b = sb("x1b", [P, 2, DIM])
        sqx = sb("sqx", [P, DIM])
        vx = sb("vx", [P, 1])
        lvx = sb("lvx", [P, 1])
        rx = sb("rx", [P, 1])
        ha = sb("ha", [P, HID])
        hg = sb("hg", [P, HID])
        hgl = sb("hgl", [P, HID])
        ac = sb("ac", [P, HC * P])
        AT = sb("AT", [P, HC, P])
        eps = sb("eps", [P, 1])
        lsh = sb("lsh", [P, 1])

        names = ("init xs_in xt_mm xs_ev xs_ev_s v_mm q_mm k_mm v_ev v2_in sqq_d sqk_d ssq_d ssk_d clq_d clk_d lnq_d lnk_d rnq_d rnk_d "
                 "nq_d nk_d tb_d t1q_d t1k_d t2q_d t2k_d qt_mm kt_mm qt_ev kt_ev sim_mm max_d sub_d exp_d sum_d rc_d on_d ot_mm "
                 "pt_mm pt_ev pv_mm ot_ev y_mm x1_d x1b_d xt2_mm xs2_ev xs2_s xcsq_d lvx_d rx_d hga_mm hgg_mm ha_d hg_d "
                 "kz_d pv_go w_ready gelu_d act_d at_mm at_ev y2_mm").split()
        s = {n: sem("s_" + n) for n in names}
        block = ctx.enter_context(nc.Block())

        Q4 = lambda t: t.rearrange("p (h s d) -> p h s d", s=2, d=HALF)
        swapped = lambda t: Q4(t)[:, :, ::-1, :]
        def table(i):
            return tb[:, i * DH:(i + 1) * DH].rearrange("p (s d) -> p s d", s=2).unsqueeze(1).to_broadcast([P, HEADS, 2, HALF])

        def win(t):
            return t % NW

        def lay(t):
            return t // NW

        def drive(eng, body):
            for n in range(-1, 4):
                body(n, n % 2)
            with eng.Fori(4, TILES - 2, 2) as n:
                body(n, 0, True)
                body(n + 1, 1, True)
            for n in range(TILES - 2, TILES + 3):
                body(n, n % 2)

        def has(t, loop):
            return loop or 0 <= t < TILES

        def above(n, loop, c):
            return loop or n - c > 0

        @block.tensor
        def _(pe):
            def body(n, par, loop=False):
                A, Bt, C, Cp = n, n - 1, n - 2, n - 3
                if has(A, loop):
                    pe.wait_ge(s["xs_ev"], n + 1)
                    pe.wait_ge(s["w_ready"], lay(n) + 1)
                    woff = (lay(n) % 2) * (3 * INNER)
                    wf = wqkv[:, :, :].rearrange("p l n -> p (l n)")
                    def proj(region, part, sig):
                        for h in range(2):
                            o = woff + (part * INNER + 512 * h)
                            mm = pe.matmul(region[:, 512 * h:512 * h + 512], XS[:, :, :].rearrange("p b i -> p (b i)"),
                                           wf[:, bass.ds(o, 512)], start=True, stop=True)
                        mm.then_inc(s[sig], 1)
                    if above(n, loop, 0):
                        pe.wait_ge(s["qt_ev"], n)
                    proj(R0, 0, "q_mm")
                    if above(n, loop, 1):
                        pe.wait_ge(s["ot_ev"], n - 1)
                    proj(R2, 2, "v_mm")
                    if above(n, loop, 0):
                        pe.wait_ge(s["sub_d"], 2 * n)
                    proj(R1, 1, "k_mm")
                if has(Cp, loop):
                    pe.wait_ge(s["act_d"], Cp + 1)
                    pe.wait_ge(s["ha_d"], Cp + 1)
                    pe.wait_ge(s["xcsq_d"], Cp + 1)
                    if has(C, loop):
                        pe.wait_ge(s["xs2_ev"], C + 1)
                    for c in range(HC):
                        mm = pe.transpose(b6[:, c * P:(c + 1) * P], ac[:, c * P:(c + 1) * P], ident[:, :])
                    mm.then_inc(s["at_mm"], 1)
                if has(Bt, loop):
                    pe.wait_ge(s["exp_d"], 2 * Bt + 2)
                    if has(A, loop):
                        pe.wait_ge(s["v_ev"], n + 1)
                    for p in range(PAIRS):
                        mm = pe.transpose(R2[:, p * P:(p + 1) * P], pr[:, p, :, :].rearrange("p a k -> p (a k)"), ident[:, :])
                    mm.then_inc(s["pt_mm"], 1)
                if has(C, loop):
                    pe.wait_ge(s["x1_d"], C + 1)
                    pe.wait_ge(s["xs2_ev"], C + 1)
                    lx = XS2[:, :, :].rearrange("p b i -> p (b i)")
                    w1f = w1[:, :, :].rearrange("p l n -> p (l n)")
                    o = lay(C) * (2 * HID)
                    pe.matmul(b7[:, 0:HID], lx, w1f[:, bass.ds(o + HID, HID)], start=True, stop=True).then_inc(s["hgg_mm"], 1)
                if has(Cp, loop):
                    pe.wait_ge(s["at_ev"], Cp + 1)
                    w2f = w2[:, :, :].rearrange("p l n -> p (l n)")
                    for c in range(HC):
                        o = lay(Cp) * (HC * DIM) + c * DIM
                        mm = pe.matmul(b6[:, 0:DIM], AT[:, c, :], w2f[:, bass.ds(o, DIM)], start=(c == 0), stop=(c == HC - 1))
                    mm.then_inc(s["y2_mm"], 1)
                if has(Bt, loop):
                    pe.wait_ge(s["pt_ev"], Bt + 1)
                    pe.wait_ge(s["v2_in"], (Bt + 1) * (16 * 2 * B))
                    pe.sem_inc(s["pv_go"], 1)
                    for p in range(PAIRS):
                        for a in range(2):
                            q = slice(64 * a, 64 * a + 64)
                            o = a * (INNER // 2) + p * DH
                            for b in range(B):
                                mm = pe.matmul(R2[b * WIN:(b + 1) * WIN, o:o + DH], PT[q, p, b * WIN:(b + 1) * WIN],
                                               V2[q, b, p * DH:(p + 1) * DH], start=True, stop=True)
                    mm.then_inc(s["pv_mm"], 1)

                if has(C, loop):
                    pe.wait_ge(s["xs2_ev"], C + 1)
                    if has(Cp, loop):
                        pe.wait_ge(x_ready, Cp + (NW + 1))
                    lx = XS2[:, :, :].rearrange("p b i -> p (b i)")
                    w1f = w1[:, :, :].rearrange("p l n -> p (l n)")
                    o = lay(C) * (2 * HID)
                    pe.matmul(b6[:, 512 - DIM:512], lx, center[:, :], start=True, stop=True)
                    pe.matmul(b6[:, 0:HID], lx, w1f[:, bass.ds(o, HID)], start=True, stop=True).then_inc(s["hga_mm"], 1)

                def rotated(reg, o, a, c, sig):
                    pe.wait_ge(s[a], n + 1)
                    pe.wait_ge(s[c], n + 1)
                    for p in range(PAIRS):
                        c0 = o + p * P
                        pe.matmul(reg[:, p * P:(p + 1) * P], t1[:, c0:c0 + P], ident[:, :], is_transpose=True,
                                  start=True, stop=False)
                        mm = pe.matmul(reg[:, p * P:(p + 1) * P], t2[:, c0:c0 + P], ident[:, :], is_transpose=True,
                                       start=False, stop=True)
                    mm.then_inc(s[sig], 1)

                if has(A, loop):
                    rotated(R0, 0, "t1q_d", "t2q_d", "qt_mm")
                if has(Bt, loop):
                    pe.wait_ge(s["on_d"], Bt + 1)
                    for p in range(PAIRS):
                        mm = pe.transpose(R2[:, p * P:(p + 1) * P], On[:, p * P:(p + 1) * P], ident[:, :])
                    mm.then_inc(s["ot_mm"], 1)
                if loop or 0 <= n + 1 < TILES:
                    pe.wait_ge(s["xs_in"], n + 2)
                    if has(C, loop):
                        pe.wait_ge(s["ha_d"], C + 1)
                        pe.wait_ge(s["xcsq_d"], C + 1)
                    pe.transpose(b6[:, 0:P], xs[:, :], ident[:, :]).then_inc(s["xt_mm"], 1)
                if has(A, loop):
                    rotated(R1, INNER, "t1k_d", "t2k_d", "kt_mm")
                if has(Bt, loop):
                    pe.wait_ge(s["ot_ev"], Bt + 1)
                    pe.wait_ge(s["w_ready"], lay(Bt) + 1)
                    if has(C, loop):
                        pe.wait_ge(s["hg_d"], C + 1)
                    wof = wo[:, :, :].rearrange("p l n -> p (l n)")
                    for p in range(PAIRS):
                        o = (lay(Bt) % 2) * (PAIRS * DIM) + p * DIM
                        mm = pe.matmul(b7[:, 0:DIM], OT[:, p, :], wof[:, bass.ds(o, DIM)], start=(p == 0), stop=(p == PAIRS - 1))
                    mm.then_inc(s["y_mm"], 1)
                for a in range(2):
                    if has(A, loop):
                        if a == 0:
                            pe.wait_ge(s["qt_ev"], n + 1)
                            pe.wait_ge(s["kt_ev"], n + 1)
                            if par == 0:
                                pe.wait_ge(s["kz_d"], n // 2 + 1)
                        m = ((win(n) + (NW - 1)) // NW) if par == 0 else 2
                        pe.matmul(R1[:, a * HS:(a + 1) * HS], identb[:, :], maskb[:, bass.ds(m * HS, HS)],
                                  start=True, stop=False, skip_group_check=True)
                        q = slice(64 * a, 64 * a + 64)
                        for p in range(PAIRS):
                            for b in range(B):
                                mm = pe.matmul(R1[b * WIN:(b + 1) * WIN, a * HS + p * K2:a * HS + (p + 1) * K2],
                                               QT[q, p, b * WIN:(b + 1) * WIN], KT[q, :, p, b * WIN:(b + 1) * WIN],
                                               start=False, stop=True, skip_group_check=True)
                        mm.then_inc(s["sim_mm"], 1)
                    if a == 0 and has(Bt, loop):
                        pe.wait_ge(s["x1_d"], Bt + 1)
                        if has(C, loop):
                            pe.wait_ge(s["ha_d"], C + 1)
                            pe.wait_ge(s["xcsq_d"], C + 1)
                        if loop or n + 1 < TILES:
                            pe.wait_ge(s["xs_ev"], n + 2)
                        pe.transpose(b6[:, 0:P], x1[:, :], ident[:, :]).then_inc(s["xt2_mm"], 1)

            pe.wait_ge(s["init"], 6)
            drive(pe, body)

        @block.scalar
        def _(act):
            def body(n, par, loop=False):
                A, Bt, C, Cp = n, n - 1, n - 2, n - 3
                def softmax_exp(a):
                    act.wait_ge(s["sub_d"], 2 * Bt + 1 + a)
                    act.activation(pr[:, :, a, :], pr[:, :, a, :], ACT.Exp, scale=QKS).then_inc(s["exp_d"], 1)
                def squares(reg, o, mm, prev, sig):
                    act.wait_ge(s[mm], n + 1)
                    if above(n, loop, 0):
                        act.wait_ge(s[prev], n)
                    act.activation(sq[:, o:o + INNER], reg[:, :], ACT.Square).then_inc(s[sig], 1)

                def norms(h, c, l, r):
                    hs = slice(h * HEADS, (h + 1) * HEADS)
                    act.wait_ge(s[c], n + 1)
                    act.activation(lss[:, hs], ss[:, hs], ACT.Ln, scale=float(2 ** SHIFT)).then_inc(s[l], 1)
                    act.wait_ge(s[l], n + 1)
                    if above(n, loop, 0):
                        act.wait_ge(s["nk_d"], n)
                        act.wait_ge(s["nq_d"], n)
                    act.activation(rn[:, hs], lss[:, hs], ACT.Exp, bias=lsh[:, 0:1], scale=-0.5).then_inc(s[r], 1)

                act.preload_act_table_set(LN_EXP)
                if has(Bt, loop):
                    softmax_exp(0)
                    softmax_exp(1)
                if has(A, loop):
                    squares(R0, 0, "q_mm", "ssq_d", "sqq_d")
                    act.wait_ge(s["v_mm"], n + 1)
                    if above(n, loop, 0):
                        act.wait_ge(s["v2_in"], n * (16 * 2 * B))
                    act.activation(Vn[:, :, :].rearrange("p a (c d) -> p c a d", d=DH),
                                   R2[:, :].rearrange("p (c a d) -> p c a d", a=2, d=DH), ACT.Copy).then_inc(s["v_ev"], 1)
                    norms(0, "clq_d", "lnq_d", "rnq_d")
                if has(Cp, loop):
                    act.wait_ge(s["at_mm"], Cp + 1)
                    act.activation(AT[:, :, :].rearrange("p c k -> p (c k)"), b6[:, 0:HC * P], ACT.Copy).then_inc(s["at_ev"], 1)
                if has(Bt, loop):
                    act.wait_ge(s["pt_mm"], Bt + 1)
                    act.activation(PT[:, :, :].rearrange("p c k -> p (c k)"), R2[:, :], ACT.Copy).then_inc(s["pt_ev"], 1)
                if has(A, loop):
                    squares(R1, INNER, "k_mm", "ssk_d", "sqk_d")
                    norms(1, "clk_d", "lnk_d", "rnk_d")
                if has(C, loop):
                    act.wait_ge(s["hga_mm"], C + 1)
                    act.activation(sqx[:, :], b6[:, 512 - DIM:512], ACT.Square, accum_out=vx[:, 0:1]).then_inc(s["xcsq_d"], 1)
                    act.wait_ge(s["xcsq_d"], C + 1)
                    act.activation(lvx[:, :], vx[:, :], ACT.Ln, bias=eps[:, 0:1], scale=1.0 / DIM).then_inc(s["lvx_d"], 1)
                    act.wait_ge(s["lvx_d"], C + 1)
                    act.activation(rx[:, :], lvx[:, :], ACT.Exp, scale=-0.5).then_inc(s["rx_d"], 1)
                if has(A, loop):
                    act.wait_ge(s["qt_mm"], n + 1)
                    act.activation(QT[:, :, :].rearrange("p c k -> p (c k)"), R0[:, :], ACT.Copy).then_inc(s["qt_ev"], 1)
                if has(Bt, loop):
                    act.wait_ge(s["ot_mm"], Bt + 1)
                    act.activation(OT[:, :, :].rearrange("p c k -> p (c k)"), R2[:, :], ACT.Copy).then_inc(s["ot_ev"], 1)
                if has(A, loop):
                    act.wait_ge(s["kt_mm"], n + 1)
                    act.activation(KT[:, par, :, :].rearrange("p c k -> p (c k)"), R1[:, :], ACT.Copy).then_inc(s["kt_ev"], 1)
                if has(C, loop):
                    act.wait_ge(s["hg_d"], C + 1)
                    act.activation(hgl[:, :], hg[:, :], ACT.Gelu).then_inc(s["gelu_d"], 1)

            act.wait_ge(s["init"], 6)
            drive(act, body)

        @block.vector
        def _(dve):
            dve.memset(KT[:, :, :, :], 0.0).then_inc(s["init"], 1)
            dve.memset(V2[:, :, :], 0.0).then_inc(s["init"], 1)
            dve.memset(cx[:, :], 0.0).then_inc(s["init"], 1)
            dve.memset(cx2[:, :], 0.0).then_inc(s["init"], 1)
            dve.memset(ac[:, :], 0.0).then_inc(s["init"], 1)
            dve.memset(eps[:, :], 1e-5).then_inc(s["init"], 1)
            dve.memset(lsh[:, :], 0.5 * SHIFT * float(np.log(2.0))).then_inc(s["init"], 1)

            def shifted(t, loop, src, dst, carry, step, done):
                up = slice(DIM // 2, DIM)
                lo = slice(0, DIM // 2)
                sv = src[:, 0:P].rearrange("p (b i) -> p b i", b=B)
                dve.tensor_copy(dst[lo, :, :], sv[lo, :, :]).then_inc(s[step], 1)
                dve.tensor_copy(dst[up, :, 1:WIN], sv[up, :, 0:WIN - 1]).then_inc(s[step], 1)
                dve.tensor_scalar(dst[up, :, 0], carry[up, :], first[up, bass.ds(win(t), 1)], None, ALU.mult).then_inc(s[step], 1)
                dve.wait_ge(s[step], t * 3 + 3)
                dve.tensor_copy(carry[up, :], sv[up, :, WIN - 1]).then_inc(s[done], 1)

            def body(n, par, loop=False):
                A, Bt, C, Cp = n, n - 1, n - 2, n - 3
                if has(Bt, loop):
                    for a in range(2):
                        dve.wait_ge(s["exp_d"], 2 * Bt + 1 + a)
                        if above(Bt, loop, 0):
                            dve.wait_ge(s["rc_d"], Bt)
                        dve.tensor_reduce(sm[:, :, a], pr[:, :, a, :], AX.X, ALU.add).then_inc(s["sum_d"], 1)
                    dve.wait_ge(s["sum_d"], 2 * Bt + 2)
                    if above(Bt, loop, 0):
                        dve.wait_ge(s["on_d"], Bt)
                    dve.reciprocal(rc[:, :], sm[:, :, :].rearrange("p c a -> p (c a)")).then_inc(s["rc_d"], 1)
                def square_sums(h, a, b_, c):
                    hs = slice(h * HEADS, (h + 1) * HEADS)
                    dve.wait_ge(s[a], n + 1)
                    if above(n, loop, 0):
                        dve.wait_ge(s["lnk_d"], n)
                    dve.tensor_reduce(ss[:, hs], sq[:, h * INNER:(h + 1) * INNER].rearrange("p (h d) -> p h d", d=DH),
                                      AX.X, ALU.add).then_inc(s[b_], 1)
                    dve.wait_ge(s[b_], n + 1)
                    dve.tensor_scalar(ss[:, hs], ss[:, hs], 1e-24, None, ALU.max).then_inc(s[c], 1)

                def normed(h, reg, r, d, prev):
                    dve.wait_ge(s[r], n + 1)
                    if above(n, loop, 0):
                        dve.wait_ge(s[prev], n)
                    dve.tensor_tensor(nqk[:, h * INNER:(h + 1) * INNER].rearrange("p (h d) -> p h d", d=DH),
                                      reg[:, :].rearrange("p (h d) -> p h d", d=DH),
                                      rn[:, h * HEADS:(h + 1) * HEADS].unsqueeze(2).to_broadcast([P, HEADS, DH]),
                                      ALU.mult).then_inc(s[d], 1)

                def cosines(h, d, t, prev):
                    hs = slice(h * INNER, (h + 1) * INNER)
                    dve.wait_ge(s[d], n + 1)
                    dve.wait_ge(s["tb_d"], n + 1)
                    if above(n, loop, 0):
                        dve.wait_ge(s[prev], n)
                    dve.tensor_tensor(Q4(t1[:, hs]), Q4(nqk[:, hs]), table(2 * h), ALU.mult).then_inc(s[t], 1)

                if has(A, loop):
                    square_sums(0, "sqq_d", "ssq_d", "clq_d")
                    normed(0, R0, "rnq_d", "nq_d", "t2q_d")
                    cosines(0, "nq_d", "t1q_d", "qt_mm")
                    square_sums(1, "sqk_d", "ssk_d", "clk_d")
                if has(Cp, loop):
                    dve.wait_ge(s["y2_mm"], Cp + 1)
                    dve.wait_ge(s["x1b_d"], Cp + 1)
                    dve.tensor_tensor(X[:, bass.ds(win(Cp) * DIM, DIM)], b6[:, 0:DIM], x1b[:, 1 - par, :], ALU.add).then_inc(x_ready, 1)
                if has(A, loop):
                    normed(1, R1, "rnk_d", "nk_d", "t2k_d")
                if has(Bt, loop):
                    dve.wait_ge(s["pv_mm"], Bt + 1)
                    dve.wait_ge(s["rc_d"], Bt + 1)
                    if above(Bt, loop, 0):
                        dve.wait_ge(s["ot_mm"], Bt)
                    dve.tensor_tensor(On[:, :].rearrange("p (c a d) -> p c a d", a=2, d=DH),
                                      R2[:, :].rearrange("p (a c d) -> p c a d", a=2, d=DH),
                                      rc[:, :].rearrange("p (c a) -> p c a", a=2).unsqueeze(3).to_broadcast([P, PAIRS, 2, DH]),
                                      ALU.mult).then_inc(s["on_d"], 1)
                if has(A, loop):
                    cosines(1, "nk_d", "t1k_d", "kt_mm")
                if has(C, loop):
                    b1f = b1b[:, :, :].rearrange("p l n -> p (l n)")
                    o = lay(C) * (2 * HID)
                    dve.wait_ge(s["rx_d"], C + 1)
                    dve.wait_ge(s["hga_mm"], C + 1)
                    dve.scalar_tensor_tensor(out=ha[:, :], in0=b6[:, 0:HID], scalar=rx[:, 0:1], in1=b1f[:, bass.ds(o, HID)],
                                             op0=ALU.mult, op1=ALU.add).then_inc(s["ha_d"], 1)
                    dve.wait_ge(s["hgg_mm"], C + 1)
                    dve.scalar_tensor_tensor(out=hg[:, :], in0=b7[:, 0:HID], scalar=rx[:, 0:1], in1=b1f[:, bass.ds(o + HID, HID)],
                                             op0=ALU.mult, op1=ALU.add).then_inc(s["hg_d"], 1)
                if has(A, loop) and par == 0:
                    if above(n, loop, 0):
                        dve.wait_ge(s["sim_mm"], 2 * n)
                        dve.wait_ge(s["kt_ev"], n)
                    kz = KT[:, 1, :, :].rearrange("p c k -> p (c k)")
                    dve.tensor_scalar(kz, kz, first[:, bass.ds(win(n), 1)], None, ALU.mult).then_inc(s["kz_d"], 1)
                if loop or 0 <= n + 1 < TILES:
                    t = n + 1
                    dve.wait_ge(s["xt_mm"], t + 1)
                    if above(t, loop, 0):
                        dve.wait_ge(s["k_mm"], t)
                        dve.wait_ge(s["xs_ev"], t)
                    shifted(t, loop, b6, XS, cx, "xs_ev_s", "xs_ev")
                if has(Bt, loop):
                    dve.wait_ge(s["y_mm"], Bt + 1)
                    if above(Bt, loop, 0):
                        dve.wait_ge(s["x1b_d"], Bt)
                        dve.wait_ge(s["xt2_mm"], Bt)
                    dve.tensor_tensor(x1[:, :], b7[:, 0:DIM], X[:, bass.ds(win(Bt) * DIM, DIM)], ALU.add).then_inc(s["x1_d"], 1)
                    dve.wait_ge(s["xt2_mm"], Bt + 1)
                    if above(Bt, loop, 0):
                        dve.wait_ge(s["hgg_mm"], Bt)
                        dve.wait_ge(s["xs2_ev"], Bt)
                    shifted(Bt, loop, b6, XS2, cx2, "xs2_s", "xs2_ev")
                if has(C, loop):
                    dve.wait_ge(s["gelu_d"], C + 1)
                    if above(C, loop, 0):
                        dve.wait_ge(s["at_mm"], C)
                    dve.tensor_tensor(ac[:, 0:HID], ha[:, :], hgl[:, :], ALU.mult).then_inc(s["act_d"], 1)
                if has(A, loop):
                    for a in range(2):
                        hs = slice(a * PAIRS, (a + 1) * PAIRS)
                        sv = R1[:, a * HS:(a + 1) * HS].rearrange("p (c k) -> p c k", k=K2)
                        dve.wait_ge(s["sim_mm"], 2 * n + 1 + a)
                        dve.tensor_reduce(mx[:, hs], sv, AX.X, ALU.max).then_inc(s["max_d"], 1)
                        dve.wait_ge(s["max_d"], 2 * n + 1 + a)
                        if above(n, loop, 0):
                            dve.wait_ge(s["pt_mm"], n)
                            dve.wait_ge(s["sum_d"], 2 * n)
                        dve.tensor_tensor(pr[:, :, a, :], sv,
                                          mx[:, hs].unsqueeze(2).to_broadcast([P, PAIRS, K2]), ALU.subtract).then_inc(s["sub_d"], 1)

            dve.wait_ge(s["init"], 7)
            drive(dve, body)

        @block.gpsimd
        def _(pool):
            def body(n, par, loop=False):
                A, Bt, C, Cp = n, n - 1, n - 2, n - 3
                if has(A, loop):
                    if above(n, loop, 0):
                        pool.wait_ge(s["t1k_d"], n)
                        pool.wait_ge(s["t2k_d"], n)
                    qf = qks[:, :, :].rearrange("p l n -> p (l n)")
                    pool.tensor_tensor(tb[:, :].rearrange("p (c s d) -> p c s d", s=2, d=HALF),
                                       qf[:, bass.ds(lay(n) * (4 * DH), 4 * DH)].rearrange("p (c s d) -> p c s d", s=2, d=HALF),
                                       tab[:, bass.ds(win(n) * (4 * HALF), 4 * HALF)].rearrange("p (c d) -> p c d", d=HALF)
                                       .unsqueeze(2).to_broadcast([P, 4, 2, HALF]), ALU.mult).then_inc(s["tb_d"], 1)
                if loop or 0 <= n + 1 < TILES:
                    t = n + 1
                    pool.wait_ge(x_ready, t + 1)
                    if above(t, loop, 0):
                        pool.wait_ge(s["xt_mm"], t)
                    pool.tensor_copy(xs[:, :], X[:, bass.ds(win(t) * DIM, DIM)]).then_inc(s["xs_in"], 1)
                if has(A, loop):
                    pool.wait_ge(s["tb_d"], n + 1)
                    for h, d, t, prev in ((0, "nq_d", "t2q_d", "qt_mm"), (1, "nk_d", "t2k_d", "kt_mm")):
                        hs = slice(h * INNER, (h + 1) * INNER)
                        pool.wait_ge(s[d], n + 1)
                        if above(n, loop, 0):
                            pool.wait_ge(s[prev], n)
                        pool.tensor_tensor(Q4(t2[:, hs]), swapped(nqk[:, hs]), table(2 * h + 1), ALU.mult).then_inc(s[t], 1)
                if has(Bt, loop):
                    pool.wait_ge(s["x1_d"], Bt + 1)
                    if above(Bt, loop, 1):
                        pool.wait_ge(x_ready, Bt + (NW - 1))
                    b2f = b2b[:, :, :].rearrange("p l n -> p (l n)")
                    pool.tensor_tensor(x1b[:, 1 - par, :], x1[:, :], b2f[:, bass.ds(lay(Bt) * DIM, DIM)], ALU.add).then_inc(s["x1b_d"], 1)

            pool.wait_ge(s["init"], 7)
            drive(pool, body)

        @block.sync
        def _(sp):
            def values(t, par, loop=False):
                sp.wait_ge(s["v_ev"], t + 1)
                if above(t, loop, 0):
                    sp.wait_ge(s["pv_mm"], t)
                for a in range(2):
                    for b in range(B):
                        q = 64 * a + WIN * par
                        sp.dma_start(V2[q:q + WIN, b, :], Vn[b * WIN:(b + 1) * WIN, a, :]).then_inc(s["v2_in"], 16)

            sp.wait_ge(s["init"], 7)
            sp.wait_ge(wqkv_in, 16)
            sp.wait_ge(wo_in, 16)
            sp.sem_inc(s["w_ready"], 1)
            for l in range(LAYERS):
                t0 = l * NW
                values(t0, 0)
                values(t0 + 1, 1)
                if l + 1 < LAYERS:
                    sl = (l + 1) % 2
                    if l >= 1:
                        sp.wait_ge(s["k_mm"], t0)
                    sp.dma_start(wqkv[:, sl, :], e["Wqkv"][l + 1]).then_inc(wqkv_in, 16)
                    if l >= 1:
                        sp.wait_ge(s["y_mm"], t0)
                    sp.dma_start(wo[:, sl, :].rearrange("p (c n) -> p c n", n=DIM),
                                 e["Wo"][l + 1].rearrange("(c p) n -> p c n", p=P)).then_inc(wo_in, 16)
                with sp.Fori(t0 + 2, t0 + NW - 2, 2) as t:
                    values(t, 0, True)
                    values(t + 1, 1, True)
                if l + 1 < LAYERS:
                    sp.wait_ge(wqkv_in, 16 * (l + 2))
                    sp.wait_ge(wo_in, 16 * (l + 2))
                    sp.sem_inc(s["w_ready"], 1)
                values(t0 + NW - 2, 0)
                values(t0 + NW - 1, 1)
            sp.wait_ge(s["v2_in"], TILES * 16 * 2 * B)


def memory(nc, hidden, proj, cols, mW1T, mW2T, mW2, WoT, gWT, norm_g, gb, mean_in, ident_in, x_mid):
    B, WIN = 4, P // 4
    DIM = gWT.shape[0]
    D = mW1T.shape[0]
    NW = hidden.shape[1] // DIM
    S = NW * WIN
    C = 64
    NC = S // C
    with ExitStack() as ctx:
        def sb(name, shape, dt=F32):
            return ctx.enter_context(nc.sbuf_tensor(name, shape, dt))

        Y = sb("Y", [P, NW * DIM])
        hT = sb("hT", [P, NW, P])
        big = sb("big", [P, 9, S])
        ident = sb("m_ident", [P, P])
        MT = sb("MT", [C, B, S])
        E = sb("E", [C, B, S])
        banks = [ctx.enter_context(nc.psum_tensor(f"bank{i}", [P, 512], F32)) for i in range(8)]
        e = dict(locals())
        e.update(x_ready=None, out=x_mid)
        load_and_norm(nc, e)
        gates(nc, e)
        read = chunks(nc, ctx, e)
        e["RT"] = read
        output(nc, e)
        layer_norm(nc, dict(DIM=DIM, NW=NW, out=x_mid), Y, hidden, "memory")


def load_and_norm(nc, e):
    with ExitStack() as ctx:
        x_in = nc.alloc_semaphore("y_in")
        block = ctx.enter_context(nc.Block())

        @block.sync
        def _(sp):
            sp.dma_start(e["Y"][:, :], e["hidden"]).then_inc(x_in, 16)
            sp.dma_start(e["ident"][:, :], e["ident_in"]).then_inc(x_in, 16)
            sp.wait_ge(x_in, 32)
    layer_norm(nc, dict(DIM=e["DIM"], NW=e["NW"], x_ready=None), e["Y"], None, "start")


V_, TH, K_, A_, B_, Q_, AQ, BQ, EB = range(9)


def gates(nc, e):
    Y, hT, big, ident, MT, E, banks = (e[k] for k in ("Y", "hT", "big", "ident", "MT", "E", "banks"))
    B, WIN, DIM, D, NW, S, C, NC = (e[k] for k in ("B", "WIN", "DIM", "D", "NW", "S", "C", "NC"))
    H2 = S // 512
    with ExitStack() as ctx:
        def sb(name, shape, dt=F32):
            return ctx.enter_context(nc.sbuf_tensor(name, shape, dt))

        def sem(name):
            return nc.alloc_semaphore(name)

        pw = sb("pw", [P, 6, D])
        cl = sb("cl", [P, 18])
        mean = sb("mean", [P, P])
        sel = sb("sel", [P, B, C])
        PAD = 3
        cin = sb("cin", [P, 3, PAD + S])
        cacc = sb("cacc", [P, 2, S])
        sg = sb("sg", [P, 3, S])
        gm = sb("gm", [P, 3, S])
        inj = sb("inj", [P, 2, S])
        aM = sb("aM", [C, B, S])
        eM = sb("eM", [C, B, S])
        ab = sb("ab", [P, 512])
        ex = sb("ex", [P, 512])
        s = {n: sem("g_" + n) for n in (
            "w_in pad t_mm t_ev p_mm p_ev m_mm m_ev v abs ex sp conv".split())}
        block = ctx.enter_context(nc.Block())
        ORDER = (3, 4, 5, 0, 1, 2)
        cw = lambda i, j: cl[:, 5 * i + j:5 * i + j + 1]

        @block.sync
        def _(sp):
            sp.dma_start(pw[:, :, :], e["proj"]).then_inc(s["w_in"], 16)
            sp.dma_start(cl[:, :], e["cols"]).then_inc(s["w_in"], 16)
            sp.dma_start(mean[:, :], e["mean_in"]).then_inc(s["w_in"], 16)

        @block.gpsimd
        def _(pool):
            pool.wait_ge(s["w_in"], 48)
            for b in range(B):
                pool.tensor_copy(sel[:, b, :].rearrange("p (r c) -> p r c", r=2),
                                 mean[:, b * WIN:(b + 1) * WIN].unsqueeze(1).to_broadcast([P, 2, WIN])).then_inc(s["pad"], 1)
            pool.memset(cin[:, :, 0:PAD], 0.0).then_inc(s["pad"], 1)
            pool.memset(inj[:, :, :], 0.0).then_inc(s["pad"], 1)
            pool.tensor_copy(MT[:, :, :].rearrange("p b (c t) -> p (b c) t", t=C),
                             ident[0:C, 0:C].unsqueeze(1).to_broadcast([C, B * NC, C])).then_inc(s["pad"], 1)

        @block.tensor
        def _(pe):
            for g in range(NW // 4):
                if g >= 2:
                    pe.wait_ge(s["t_ev"], g - 1)
                for j in range(4):
                    w = 4 * g + j
                    mm = pe.transpose(banks[g % 2][:, j * P:(j + 1) * P], Y[:, w * DIM:(w + 1) * DIM], ident[:, :])
                mm.then_inc(s["t_mm"], 1)
            pe.wait_ge(s["w_in"], 48)
            pe.wait_ge(s["t_ev"], NW // 4)
            n = 0
            for i in ORDER:
                for h in range(H2):
                    if n >= 3:
                        pe.wait_ge(s["p_ev"], n - 2)
                    for b in range(B):
                        mm = pe.matmul(banks[2 + n % 3][b * D:(b + 1) * D, :], pw[:, i, :],
                                       hT[:, h * (512 // WIN):(h + 1) * (512 // WIN), b * WIN:(b + 1) * WIN], start=True, stop=True)
                    mm.then_inc(s["p_mm"], 1)
                    n += 1
            pe.wait_ge(s["pad"], B)
            n = 0
            for i in range(3):
                pe.wait_ge(s["p_ev"], 2 * H2) if i < 2 else pe.wait_ge(s["sp"], H2)
                for h in range(H2):
                    if n >= 3:
                        pe.wait_ge(s["m_ev"], n - 2)
                    pe.matmul(banks[5 + n % 3][:, :], mean[:, :], sg[:, i, 512 * h:512 * h + 512],
                              start=True, stop=True).then_inc(s["m_mm"], 1)
                    n += 1
            for i in range(2):
                for b in range(B):
                    for h in range(H2):
                        pe.wait_ge(s["m_ev"], n - 2)
                        pe.matmul(banks[5 + n % 3][0:C, :], sel[:, b, :], sg[:, i, 512 * h:512 * h + 512],
                                  start=True, stop=True).then_inc(s["m_mm"], 1)
                        n += 1

        @block.scalar
        def _(act):
            act.preload_act_table_set(SIGMOID)
            act.wait_ge(s["w_in"], 48)
            n = 0
            for i in ORDER:
                if i == 5:
                    act.preload_act_table_set(LN_EXP)
                for h in range(H2):
                    src = banks[2 + n % 3][:, :]
                    hs = slice(512 * h, 512 * h + 512)
                    act.wait_ge(s["p_mm"], n + 1)
                    if i in (3, 4):
                        act.activation(sg[:, i - 3, hs], src, ACT.Sigmoid, bias=cl[:, 12 + i:13 + i]).then_inc(s["p_ev"], 1)
                    elif i == 5:
                        act.activation(sg[:, 2, hs], src, ACT.Identity, bias=cl[:, 17:18]).then_inc(s["p_ev"], 1)
                        act.wait_ge(s["p_ev"], n + 1)
                        if h:
                            act.wait_ge(s["ex"], 2 * h)
                        act.activation(ab[:, :], sg[:, 2, hs], ACT.Abs).then_inc(s["abs"], 1)
                        act.wait_ge(s["abs"], h + 1)
                        if h:
                            act.wait_ge(s["sp"], h)
                        act.activation(ex[:, :], ab[:, :], ACT.Exp, scale=-1.0).then_inc(s["ex"], 1)
                        act.wait_ge(s["ex"], 2 * h + 1)
                        act.activation(ex[:, :], ex[:, :], ACT.Ln, bias=1.0).then_inc(s["ex"], 1)
                    else:
                        act.activation(cin[:, i, PAD + 512 * h:PAD + 512 * h + 512], src, ACT.Copy).then_inc(s["p_ev"], 1)
                    n += 1

        @block.vector
        def _(dve):
            steps = [0]

            def link(ins):
                steps[0] += 1
                ins.then_inc(s["v"], 1)
                dve.wait_ge(s["v"], steps[0])

            for g in range(NW // 4):
                dve.wait_ge(s["t_mm"], g + 1)
                dve.tensor_copy(hT[:, 4 * g:4 * (g + 1), :].rearrange("p w n -> p (w n)"), banks[g % 2][:, :]).then_inc(s["t_ev"], 1)
            for h in range(H2):
                hs = slice(512 * h, 512 * h + 512)
                dve.wait_ge(s["ex"], 2 * h + 2)
                dve.scalar_tensor_tensor(out=sg[:, 2, hs], in0=sg[:, 2, hs], scalar=0.0, in1=ex[:, :],
                                         op0=ALU.max, op1=ALU.add).then_inc(s["sp"], 1)
            n = 0
            aff = ((-0.1, 1.0), (0.9, 0.05), (-0.1, 0.0))
            for i in range(3):
                for h in range(H2):
                    dve.wait_ge(s["m_mm"], n + 1)
                    dve.tensor_scalar(gm[:, i, 512 * h:512 * h + 512], banks[5 + n % 3][:, :], *aff[i],
                                      ALU.mult, ALU.add).then_inc(s["m_ev"], 1)
                    n += 1
            for i, dst in ((0, aM), (1, eM)):
                for b in range(B):
                    for h in range(H2):
                        dve.wait_ge(s["m_mm"], n + 1)
                        dve.tensor_scalar(dst[:, b, 512 * h:512 * h + 512], banks[5 + n % 3][0:C, :], *aff[i],
                                          ALU.mult, ALU.add).then_inc(s["m_ev"], 1)
                        n += 1
            dve.wait_ge(s["m_ev"], n)
            dve.wait_ge(s["pad"], B + 3)
            starts = lambda t: t.rearrange("p (c t) -> p c t", t=C)[:, :, 0:1]
            for i in range(2):
                link(dve.tensor_copy(starts(inj[:, i, :]), starts(gm[:, i, :])))
                link(dve.memset(starts(gm[:, i, :]), 0.0))
            link(dve.memset(starts(aM[:, :, :].rearrange("p b t -> p (b t)")), 0.0))
            link(dve.memset(starts(eM[:, :, :].rearrange("p b t -> p (b t)")), 0.0))
            link(dve.tensor_tensor_scan(big[:, A_, :], gm[:, 0, :], inj[:, 0, :], 0.0, ALU.mult, ALU.add))
            link(dve.tensor_tensor_scan(big[:, EB, :], gm[:, 1, :], inj[:, 1, :], 0.0, ALU.mult, ALU.add))
            link(dve.tensor_tensor_scan(big[:, B_, :], gm[:, 0, :], big[:, EB, :], 0.0, ALU.mult, ALU.add))
            link(dve.tensor_copy(big[:, TH, :], gm[:, 2, :]))
            fl = lambda t: t.rearrange("p b t -> p (b t)")
            link(dve.tensor_tensor_scan(fl(E[:, :, :]), fl(eM[:, :, :]), fl(MT[:, :, :]), 0.0, ALU.mult, ALU.add))
            link(dve.tensor_tensor_scan(fl(MT[:, :, :]), fl(aM[:, :, :]), fl(E[:, :, :]), 0.0, ALU.mult, ALU.add))
            dve.wait_ge(s["p_ev"], 6 * H2)
            for i, item in ((0, K_), (1, V_), (2, Q_)):
                link(dve.tensor_scalar(cacc[:, 0, :], cin[:, i, 0:S], cw(i, 0), cw(i, 4), ALU.mult, ALU.add))
                for j in (1, 2, 3):
                    dst = big[:, item, :] if j == 3 else cacc[:, j % 2, :]
                    link(dve.scalar_tensor_tensor(out=dst, in0=cin[:, i, j:j + S], scalar=cw(i, j),
                                                  in1=cacc[:, (j + 1) % 2, :], op0=ALU.mult, op1=ALU.add))
            link(dve.tensor_tensor(big[:, AQ, :], big[:, Q_, :], big[:, A_, :], ALU.mult))
            link(dve.tensor_tensor(big[:, BQ, :], big[:, Q_, :], big[:, B_, :], ALU.mult))

    release(nc, s)


def release(nc, semaphores):
    nc.clear_and_free_semaphores(list(semaphores.values()))
    nc.all_engine_barrier()


def chunks(nc, ctx0, e):
    big, ident, MT, E, banks = (e[k] for k in ("big", "ident", "MT", "E", "banks"))
    B, WIN, DIM, D, NW, S, C, NC = (e[k] for k in ("B", "WIN", "DIM", "D", "NW", "S", "C", "NC"))
    RT = ctx0.enter_context(nc.sbuf_tensor("RT", [D, NW, P], F32))
    BD = B * D
    with ExitStack() as ctx:
        def sb(name, shape, dt=F32):
            return ctx.enter_context(nc.sbuf_tensor(name, shape, dt))

        def sem(name):
            return nc.alloc_semaphore(name)

        st_n = sb("st_n", [P, 5, C])
        zero = sb("zero", [D, 2, B, 7, C])
        mt = sb("mt", [C, 2, B, C])
        ee = sb("ee", [C, 2, B])
        nat = sb("nat", [C, 2, 5, BD])
        v02 = sb("v02", [C, BD])
        state = sb("state", [D, 2, 3, B, 2, D])
        sa = sb("sa", [D, 3, B, D])
        sbb = sb("sbb", [D, 3, B, D])
        sc = sb("sc", [D, 3, B, D])
        zz, ez, e1, sig, ds, dt1, dt2, dz = (sb(n, [C, BD]) for n in ("zz", "ez", "e1", "sig", "ds", "dt1", "dt2", "dz"))
        hh = sb("hh", [C, 2, BD])
        ev = sb("ev", [C, BD])
        hmT = sb("hmT", [D, 2, B, C])
        eT = sb("eT", [D, B, C])
        sqs = sb("sqs", [C, 4, BD])
        nr = sb("nr", [C, 4, B])
        pd = sb("pd", [C, 2, B])
        gn, gl, gf, ww = (sb(n, [C, B]) for n in ("gn", "gl", "gf", "ww"))
        wme = sb("wme", [C, B, 2])
        r1 = sb("r1", [C, B, 2, D])
        r2 = sb("r2", [C, B, 2, D])
        dzw = sb("dzw", [C, 2, BD])
        ew = sb("ew", [C, 2, BD])
        g1 = sb("g1", [C, B, C])
        g2 = sb("g2", [C, B, C])
        zq, eq, e1q, sgq = (sb(n, [C, BD]) for n in ("zq", "eq", "e1q", "sgq"))
        hq = sb("hq", [C, 3, BD])
        hqT = sb("hqT", [D, 3, B, C])
        names = ("init go st_in z_in0 z_in1 st_n mt ee nat_mm nat_ev v02 zk_mm z ez e1 sig h ds1 ds2 ds hT_mm hT_ev pr_mm ev eT_mm eT_ev dh_mm dz "
                 "sq_h sq_k sq_e sq_z nr3 nrz pd gn0 gn gl gf ww wm we r1 r2 dzw ew up_mm sa sbb sab sc state stateS "
                 "kq_mm g1 zq_mm zq eq e1q sgq hq hqa hqb hqT_mm hqT_ev HQ_mm g2 rt_mm rt_ev").split()
        s = {n: sem("c_" + n) for n in names}
        block = ctx.enter_context(nc.Block())
        b4 = lambda t: t.rearrange("p (b d) -> p b d", b=B)
        pN, pZ, pR, pT, pQ0, pQ1, pU0, pU1 = banks
        TAIL = NC - 2

        def drive(eng, body):
            body(-1, 1)
            body(0, 0)
            body(1, 1)
            with eng.Fori(2, TAIL, 2) as c:
                body(c, 0, True)
                body(c + 1, 1, True)
            for c in range(TAIL, NC + 1):
                body(c, c % 2)

        def wait(eng, name, c, loop=True):
            if loop or c >= 0:
                eng.wait_ge(s[name], c + 1)

        def settled(eng):
            eng.wait_ge(s["init"], 1)

        def here(c, loop):
            return loop or 0 <= c < NC

        @block.sync
        def _(sp):
            for m, src in ((0, e["mW1T"]), (1, e["mW2T"]), (2, e["mW2"])):
                for b in range(B):
                    sp.dma_start(state[:, 0, m, b, 0, :], src).then_inc(s["st_in"], 16)

            def body(c, par, loop=False):
                n = c + 1
                if not here(n, loop):
                    return
                wait(sp, "up_mm", n - 2, loop)
                wait(sp, "zq_mm", n - 2, loop)
                wait(sp, "kq_mm", n - 2, loop)
                wait(sp, "sc", n - 2, loop)
                for b in range(B):
                    sp.dma_start(zero[:, 1 - par, b, :, :], big[b * D:(b + 1) * D, K_:EB + 1, bass.ds(n * C, C)]
                                 ).then_inc(s["z_in%d" % (1 - par)], 16)
            drive(sp, body)

        @block.gpsimd
        def _(pool):
            pool.memset(state[:, 0, :, :, 1, :], 0.0).then_inc(s["init"], 1)

            def body(c, par, loop=False):
                n, R = c + 1, c - 1
                if here(n, loop):
                    wait(pool, "nat_mm", n - 1, loop)
                    pool.tensor_copy(st_n[:, :, :], big[:, 0:5, bass.ds(n * C, C)]).then_inc(s["st_n"], 1)
                if here(c, loop):
                    wait(pool, "h", c)
                    wait(pool, "dz", c - 1, loop)
                    pool.tensor_tensor(dt1[:, :], hh[:, par, :], sig[:, :], ALU.mult).then_inc(s["ds1"], 1)
                    pool.tensor_tensor(dt2[:, :], hh[:, par, :], sig[:, :], ALU.add).then_inc(s["ds2"], 1)
                    wait(pool, "ds1", c)
                    wait(pool, "ds2", c)
                    pool.tensor_tensor(ds[:, :], dt2[:, :], dt1[:, :], ALU.subtract).then_inc(s["ds"], 1)
                    wait(pool, "nr3", 2 * c - 1, loop)
                    pool.tensor_tensor(sqs[:, 2, :], hh[:, par, :], hh[:, par, :], ALU.mult).then_inc(s["sq_h"], 1)
                    wait(pool, "nat_ev", c)
                    pool.tensor_tensor(sqs[:, 3, :], nat[:, par, 2, :], nat[:, par, 2, :], ALU.mult).then_inc(s["sq_k"], 1)
                    wait(pool, "ev", c)
                    pool.tensor_tensor(sqs[:, 0, :], ev[:, :], ev[:, :], ALU.mult).then_inc(s["sq_e"], 1)
                if here(R, loop):
                    wait(pool, "hq", R)
                    wait(pool, "hqT_mm", R - 1, loop)
                    pool.tensor_tensor(hq[:, 1, :], hq[:, 0, :], nat[:, 1 - par, 3, :], ALU.mult).then_inc(s["hqa"], 1)
                    pool.tensor_tensor(hq[:, 2, :], hq[:, 0, :], nat[:, 1 - par, 4, :], ALU.mult).then_inc(s["hqb"], 1)
                if here(c, loop):
                    wait(pool, "ww", c)
                    wait(pool, "zq_mm", c - 2, loop)
                    pool.tensor_tensor(b4(dzw[:, par, :]), b4(dz[:, :]), ww[:, :].unsqueeze(2).to_broadcast([C, B, D]), ALU.mult).then_inc(s["dzw"], 1)
                    wait(pool, "rt_mm", c - 2, loop)
                    pool.tensor_tensor(b4(ew[:, par, :]), b4(ev[:, :]), ww[:, :].unsqueeze(2).to_broadcast([C, B, D]), ALU.mult).then_inc(s["ew"], 1)
                if here(n, loop):
                    wait(pool, "g2", n - 2, loop)
                    pool.tensor_copy(mt[:, 1 - par, :, :], MT[:, :, bass.ds(n * C, C)]).then_inc(s["mt"], 1)
                    wait(pool, "we", n - 2, loop)
                    pool.tensor_copy(ee[:, 1 - par, :].unsqueeze(2), E[:, :, bass.ds(n * C + (C - 1), 1)]).then_inc(s["ee"], 1)
            drive(pool, body)

        @block.tensor
        def _(pe):
            pe.wait_ge(s["init"], 1)
            pe.wait_ge(s["st_in"], 16 * 3 * B)
            ZK, ZA, ZB, ZQ, ZAQ, ZBQ, ZE = range(7)

            def nat_t(n, loop):
                wait(pe, "st_n", n)
                wait(pe, "nat_ev", n - 1, loop)
                wait(pe, "zq", n - 2, loop)
                wait(pe, "g1", n - 1, loop)
                wait(pe, "g2", n - 2, loop)
                pe.sem_inc(s["go"], 1)
                for i in range(5):
                    out = pN[0:C, i * P:(i + 1) * P] if i < 4 else pR[0:C, 384:512]
                    mm = pe.transpose(out, st_n[:, i, :], ident[:, :])
                mm.then_inc(s["nat_mm"], 1)

            def body(c, par, loop=False):
                R = c - 1
                rp = 1 - par
                if here(c, loop):
                    settled(pe)
                    wait(pe, "state", c - 1, loop)
                    wait(pe, "stateS", c - 1, loop)
                    pe.wait_ge(s["z_in%d" % par], (c // 2 + 1) * (16 * B))
                    wait(pe, "dz", c - 1, loop)
                    for b in range(B):
                        mm = pe.matmul(pZ[0:C, b * D:(b + 1) * D], zero[:, par, b, ZK, :], state[:, par, 0, b, 0, :],
                                       start=True, stop=True)
                    mm.then_inc(s["zk_mm"], 1)
                if here(R, loop):
                    settled(pe)
                    wait(pe, "g1", R)
                    wait(pe, "dzw", R)
                    if here(c, loop):
                        wait(pe, "nat_ev", c)
                    for b in range(B):
                        o = pR[0:C, 256 + b * D:256 + (b + 1) * D]
                        pe.matmul(o, zero[:, rp, b, ZAQ, :], state[:, rp, 0, b, 0, :], start=True, stop=False)
                        pe.matmul(o, zero[:, rp, b, ZBQ, :], state[:, rp, 0, b, 1, :], start=False, stop=False)
                        mm = pe.matmul(o, g1[:, b, :], dzw[:, rp, b * D:(b + 1) * D], start=False, stop=True)
                    mm.then_inc(s["zq_mm"], 1)
                if here(c, loop):
                    settled(pe)
                    wait(pe, "h", c)
                    wait(pe, "eT_ev", c - 1, loop)
                    for b in range(B):
                        mm = pe.transpose(pT[0:D, b * C:(b + 1) * C], hh[:, par, b * D:(b + 1) * D], ident[0:C, 0:C])
                    mm.then_inc(s["hT_mm"], 1)
                    settled(pe)
                    wait(pe, "hT_ev", c)
                    wait(pe, "z", c)
                    for b in range(B):
                        mm = pe.matmul(pZ[0:C, BD + b * D:BD + (b + 1) * D], hmT[:, par, b, :], state[:, par, 1, b, 0, :],
                                       start=True, stop=True)
                    mm.then_inc(s["pr_mm"], 1)
                if here(R, loop):
                    wait(pe, "hqa", R)
                    wait(pe, "hqb", R)
                    wait(pe, "hq", R)
                    wait(pe, "rt_ev", R - 1, loop)
                    pe.sem_inc(s["go"], 1)
                    for i in range(3):
                        for b in range(B):
                            bank = (pQ0, pQ1)[i // 2]
                            o = (i % 2) * B * C + b * C
                            mm = pe.transpose(bank[0:D, o:o + C], hq[:, i, b * D:(b + 1) * D], ident[0:C, 0:C])
                    mm.then_inc(s["hqT_mm"], 1)
                if here(c, loop):
                    settled(pe)
                    wait(pe, "ev", c)
                    wait(pe, "hT_ev", c)
                    for b in range(B):
                        mm = pe.transpose(pT[0:D, B * C + b * C:B * C + (b + 1) * C], ev[:, b * D:(b + 1) * D], ident[0:C, 0:C])
                    mm.then_inc(s["eT_mm"], 1)
                    settled(pe)
                    wait(pe, "eT_ev", c)
                    for b in range(B):
                        mm = pe.matmul(pZ[0:C, 2 * BD + b * D:2 * BD + (b + 1) * D], eT[:, b, :], state[:, par, 2, b, 0, :],
                                       start=True, stop=True)
                    mm.then_inc(s["dh_mm"], 1)
                if here(R, loop):
                    settled(pe)
                    wait(pe, "hqT_ev", 2 * R + 1)
                    wait(pe, "zq", R)
                    for b in range(B):
                        mm = pe.matmul(pR[0:C, b * C:(b + 1) * C], hmT[:, rp, b, :], hqT[:, 0, b, :], start=True, stop=True)
                    mm.then_inc(s["HQ_mm"], 1)
                    settled(pe)
                    wait(pe, "g2", R)
                    wait(pe, "ew", R)
                    for b in range(B):
                        o = pQ1[0:D, B * C + b * C:B * C + (b + 1) * C]
                        pe.matmul(o, state[:, rp, 1, b, 0, :], hqT[:, 1, b, :], start=True, stop=False)
                        pe.matmul(o, state[:, rp, 1, b, 1, :], hqT[:, 2, b, :], start=False, stop=False)
                        mm = pe.matmul(o, ew[:, rp, b * D:(b + 1) * D], g2[:, b, :], start=False, stop=True)
                    mm.then_inc(s["rt_mm"], 1)
                if here(c, loop):
                    for b in range(B):
                        mm = pe.matmul(pR[0:C, b * C:(b + 1) * C], zero[:, par, b, ZK, :], zero[:, par, b, ZQ, :],
                                       start=True, stop=True)
                    mm.then_inc(s["kq_mm"], 1)
                    settled(pe)
                    wait(pe, "r1", c)
                    wait(pe, "r2", c)
                    wait(pe, "state", c - 1, loop)
                    wait(pe, "stateS", c - 1, loop)
                    for b in range(B):
                        d = slice(b * D, (b + 1) * D)
                        o = b * 2 * D
                        pe.matmul(pU0[0:D, o:o + 2 * D], nat[:, par, 2, d], r1[:, b, :, :].rearrange("p a d -> p (a d)"),
                                  start=True, stop=True)
                        pe.matmul(pU0[0:D, 256 + o:256 + o + 2 * D], hh[:, par, d], r2[:, b, :, :].rearrange("p a d -> p (a d)"),
                                  start=True, stop=True)
                        pe.matmul(pU1[0:D, o:o + D], r2[:, b, 0, :], hh[:, par, d], start=True, stop=True)
                        mm = pe.matmul(pU1[0:D, o + D:o + 2 * D], r2[:, b, 1, :], hh[:, par, d], start=True, stop=True)
                    mm.then_inc(s["up_mm"], 1)
                if here(c + 1, loop):
                    nat_t(c + 1, loop)

            drive(pe, body)

        @block.scalar
        def _(act):
            act.preload_act_table_set(LN_EXP)

            def body(c, par, loop=False):
                R, n = c - 1, c + 1
                if here(c, loop):
                    wait(act, "z", c)
                    wait(act, "e1", c - 1, loop)
                    act.activation(ez[:, :], zz[:, :], ACT.Exp, scale=-1.0).then_inc(s["ez"], 1)
                if here(R, loop):
                    wait(act, "zq", R)
                    wait(act, "e1q", R - 1, loop)
                    act.activation(eq[:, :], zq[:, :], ACT.Exp, scale=-1.0).then_inc(s["eq"], 1)
                if here(c, loop):
                    wait(act, "hT_mm", c)
                    wait(act, "HQ_mm", c - 2, loop)
                    act.activation(hmT[:, par, :, :].rearrange("p b t -> p (b t)"), pT[0:D, 0:B * C], ACT.Copy).then_inc(s["hT_ev"], 1)
                    wait(act, "eT_mm", c)
                    wait(act, "dh_mm", c - 1, loop)
                    act.activation(eT[:, :, :].rearrange("p b t -> p (b t)"), pT[0:D, B * C:2 * B * C], ACT.Copy).then_inc(s["eT_ev"], 1)
                if here(R, loop):
                    wait(act, "hqT_mm", R)
                    wait(act, "rt_mm", R - 1, loop)
                    hf = hqT[:, :, :, :].rearrange("p i b t -> p (i b t)")
                    act.activation(hf[:, 0:512], pQ0[0:D, :], ACT.Copy).then_inc(s["hqT_ev"], 1)
                    act.activation(hf[:, 512:768], pQ1[0:D, 0:256], ACT.Copy).then_inc(s["hqT_ev"], 1)
                if here(c, loop):
                    wait(act, "gn", c)
                    act.activation(gl[:, :], gn[:, :], ACT.Ln).then_inc(s["gl"], 1)
                    wait(act, "gl", c)
                    wait(act, "ww", c - 1, loop)
                    act.activation(gf[:, :], gl[:, :], ACT.Exp, scale=-0.5).then_inc(s["gf"], 1)
                if here(R, loop):
                    wait(act, "rt_mm", R)
                    act.activation(RT[:, bass.ds(R * (C // WIN), C // WIN), :].rearrange("p w (b i) -> p w b i", b=B),
                                   pQ1[0:D, B * C:2 * B * C].rearrange("p (b w i) -> p w b i", b=B, i=WIN), ACT.Copy).then_inc(s["rt_ev"], 1)
                if here(n, loop):
                    wait(act, "nat_mm", n)
                    for q in ("sq_k", "v02", "ww", "up_mm"):
                        wait(act, q, n - 2, loop)
                    for q in ("hqa", "hqb"):
                        wait(act, q, n - 2, loop)
                    act.activation(nat[:, 1 - par, 0:4, :].rearrange("p i d -> p (i d)"), pN[0:C, :], ACT.Copy)
                    act.activation(nat[:, 1 - par, 4, :], pR[0:C, 384:512], ACT.Copy).then_inc(s["nat_ev"], 1)
            drive(act, body)

        @block.vector
        def _(dve):
            def body(c, par, loop=False):
                R = c - 1
                rp = 1 - par
                TT = dve.tensor_tensor
                if here(c, loop):
                    wait(dve, "zk_mm", c)
                    wait(dve, "h", c - 1, loop)
                    dve.tensor_scalar(zz[:, :], pZ[0:C, 0:BD], -80.0, None, ALU.max).then_inc(s["z"], 1)
                    wait(dve, "nat_ev", c)
                    wait(dve, "ev", c - 1, loop)
                    dve.tensor_scalar(v02[:, :], nat[:, par, 0, :], 0.2, None, ALU.mult).then_inc(s["v02"], 1)
                    wait(dve, "ez", c)
                    wait(dve, "sig", c - 1, loop)
                    dve.tensor_scalar(e1[:, :], ez[:, :], 1.0, None, ALU.add).then_inc(s["e1"], 1)
                    wait(dve, "e1", c)
                    wait(dve, "ds2", c - 1, loop)
                    wait(dve, "ds1", c - 1, loop)
                    dve.reciprocal(sig[:, :], e1[:, :]).then_inc(s["sig"], 1)
                    wait(dve, "sig", c)
                    wait(dve, "up_mm", c - 2, loop)
                    wait(dve, "sq_h", c - 2, loop)
                    TT(hh[:, par, :], zz[:, :], sig[:, :], ALU.mult).then_inc(s["h"], 1)
                if here(R, loop):
                    wait(dve, "zq_mm", R)
                    wait(dve, "hq", R - 1, loop)
                    dve.tensor_scalar(zq[:, :], pR[0:C, 256:256 + BD], -80.0, None, ALU.max).then_inc(s["zq"], 1)
                    wait(dve, "eq", R)
                    wait(dve, "sgq", R - 1, loop)
                    dve.tensor_scalar(e1q[:, :], eq[:, :], 1.0, None, ALU.add).then_inc(s["e1q"], 1)
                    wait(dve, "e1q", R)
                    dve.reciprocal(sgq[:, :], e1q[:, :]).then_inc(s["sgq"], 1)
                    wait(dve, "sgq", R)
                    wait(dve, "hqT_mm", R - 1, loop)
                    wait(dve, "hqa", R - 1, loop)
                    wait(dve, "hqb", R - 1, loop)
                    TT(hq[:, 0, :], zq[:, :], sgq[:, :], ALU.mult).then_inc(s["hq"], 1)
                if here(c, loop):
                    wait(dve, "pr_mm", c)
                    wait(dve, "v02", c)
                    wait(dve, "ew", c - 1, loop)
                    wait(dve, "eT_mm", c - 1, loop)
                    wait(dve, "r2", c - 1, loop)
                    dve.scalar_tensor_tensor(out=ev[:, :], in0=pZ[0:C, BD:2 * BD], scalar=0.2, in1=v02[:, :],
                                             op0=ALU.mult, op1=ALU.subtract).then_inc(s["ev"], 1)
                    W = lambda k: state[:, par, :, :, k, :]
                    last = lambda i: zero[:, par, :, i, C - 1].unsqueeze(1).unsqueeze(3).to_broadcast([D, 3, B, D])
                    wait(dve, "state", c - 1, loop)
                    wait(dve, "stateS", c - 1, loop)
                    TT(sa[:, :, :, :], W(0), last(1), ALU.mult).then_inc(s["sa"], 1)
                    TT(sbb[:, :, :, :], W(1), last(2), ALU.mult).then_inc(s["sbb"], 1)
                    TT(sc[:, :, :, :], W(1), last(6), ALU.mult).then_inc(s["sc"], 1)
                    wait(dve, "sa", c)
                    wait(dve, "sbb", c)
                    TT(sa[:, :, :, :], sa[:, :, :, :], sbb[:, :, :, :], ALU.add).then_inc(s["sab"], 1)
                    wait(dve, "sq_h", c)
                    wait(dve, "sq_k", c)
                    wait(dve, "sq_e", c)
                    wait(dve, "pd", c - 1, loop)
                    dve.tensor_reduce(nr[:, 2:4, :], sqs[:, 2:4, :].rearrange("p k (b d) -> p k b d", b=B), AX.X, ALU.add).then_inc(s["nr3"], 1)
                    dve.tensor_reduce(nr[:, 0, :], b4(sqs[:, 0, :]), AX.X, ALU.add).then_inc(s["nr3"], 1)
                    wait(dve, "dh_mm", c)
                    wait(dve, "ds", c)
                    wait(dve, "dzw", c - 1, loop)
                    TT(dz[:, :], pZ[0:C, 2 * BD:3 * BD], ds[:, :], ALU.mult).then_inc(s["dz"], 1)
                    wait(dve, "dz", c)
                    TT(sqs[:, 1, :], dz[:, :], dz[:, :], ALU.mult).then_inc(s["sq_z"], 1)
                    wait(dve, "sq_z", c)
                    dve.tensor_reduce(nr[:, 1, :], b4(sqs[:, 1, :]), AX.X, ALU.add).then_inc(s["nrz"], 1)
                    wait(dve, "nrz", c)
                    wait(dve, "nr3", 2 * c + 1)
                    TT(pd[:, :, :], nr[:, 0:2, :], nr[:, 2:4, :], ALU.mult).then_inc(s["pd"], 1)
                    wait(dve, "pd", c)
                    wait(dve, "gl", c - 1, loop)
                    TT(gn[:, :], pd[:, 0, :], pd[:, 1, :], ALU.add).then_inc(s["gn0"], 1)
                    wait(dve, "gn0", c)
                    dve.tensor_scalar(gn[:, :], gn[:, :], 1e-12, None, ALU.max).then_inc(s["gn"], 1)
                if here(R, loop):
                    wait(dve, "HQ_mm", R)
                    wait(dve, "rt_mm", R - 1, loop)
                    TT(g2[:, :, :], pR[0:C, 0:B * C].rearrange("p (b t) -> p b t", b=B), mt[:, rp, :, :], ALU.mult).then_inc(s["g2"], 1)
                if here(c, loop):
                    wait(dve, "gf", c)
                    wait(dve, "dzw", c - 1, loop)
                    wait(dve, "ew", c - 1, loop)
                    dve.scalar_tensor_tensor(out=ww[:, :], in0=gf[:, :], scalar=1.0, in1=b4(nat[:, par, 1, :])[:, :, 0],
                                             op0=ALU.min, op1=ALU.mult).then_inc(s["ww"], 1)
                    wait(dve, "ww", c)
                    wait(dve, "mt", c)
                    wait(dve, "ee", c)
                    wait(dve, "r1", c - 1, loop)
                    wait(dve, "r2", c - 1, loop)
                    TT(wme[:, :, 0], ww[:, :], mt[:, par, :, C - 1], ALU.mult).then_inc(s["wm"], 1)
                    TT(wme[:, :, 1], ww[:, :], ee[:, par, :], ALU.mult).then_inc(s["we"], 1)
                    wait(dve, "wm", c)
                    wait(dve, "we", c)
                    wait(dve, "up_mm", c - 1, loop)
                    ws = wme[:, :, :].unsqueeze(3).to_broadcast([C, B, 2, D])
                    TT(r1[:, :, :, :], b4(dz[:, :]).unsqueeze(2).to_broadcast([C, B, 2, D]), ws, ALU.mult).then_inc(s["r1"], 1)
                    TT(r2[:, :, :, :], b4(ev[:, :]).unsqueeze(2).to_broadcast([C, B, 2, D]), ws, ALU.mult).then_inc(s["r2"], 1)
                    wait(dve, "kq_mm", c)
                    wait(dve, "zq_mm", c - 1, loop)
                    TT(g1[:, :, :], pR[0:C, 0:B * C].rearrange("p (b t) -> p b t", b=B), mt[:, par, :, :], ALU.mult).then_inc(s["g1"], 1)
                    wait(dve, "up_mm", c)
                    wait(dve, "sab", c)
                    wait(dve, "sc", c)
                    wait(dve, "rt_mm", c - 1, loop)
                    for k, base, sg in ((0, sa, "state"), (1, sc, "stateS")):
                        TT(state[:, 1 - par, 0:2, :, k, :], base[:, 0:2, :, :],
                           pU0[0:D, :].rearrange("p (m b k d) -> p m b k d", m=2, b=B, k=2)[:, :, :, k, :], ALU.add)
                        TT(state[:, 1 - par, 2, :, k, :], base[:, 2, :, :],
                           pU1[0:D, 0:256].rearrange("p (b k d) -> p b k d", b=B, k=2)[:, :, k, :], ALU.add).then_inc(s[sg], 1)

            drive(dve, body)
    release(nc, s)
    return RT


def output(nc, e):
    Y, hT, banks, RT = e["Y"], e["hT"], e["banks"], e["RT"]
    B, WIN, DIM, D, NW, S = (e[k] for k in ("B", "WIN", "DIM", "D", "NW", "S"))
    G = 4
    GROUPS = NW // G
    N = G * DIM
    with ExitStack() as ctx:
        def sb(name, shape, dt=F32):
            return ctx.enter_context(nc.sbuf_tensor(name, shape, dt))

        def sem(name):
            return nc.alloc_semaphore(name)

        woT = sb("woT", [D, DIM])
        gwT = sb("gwT", [P, DIM])
        ng = sb("ng", [P, DIM])
        gbb = sb("gbb", [P, DIM])
        osq = sb("osq", [P, 2, N])
        ms = sb("ms", [P, GROUPS, G])
        lm = sb("lm", [P, GROUPS, G])
        rm = sb("rm", [P, GROUPS, G])
        on = sb("on", [P, 2, N])
        ga = sb("ga", [P, 2, N])
        ep = sb("ep6", [P, 1])
        s = {n: sem("o_" + n) for n in "w_in ep o_mm g_mm sq ms lm rm on on2 ga ga2 y".split()}
        block = ctx.enter_context(nc.Block())
        w3 = lambda t: t.rearrange("p (w n) -> p w n", n=DIM)
        bc = lambda t: t[:, :].unsqueeze(1).to_broadcast([P, G, DIM])

        @block.sync
        def _(sp):
            sp.dma_start(woT[:, :], e["WoT"]).then_inc(s["w_in"], 16)
            sp.dma_start(gwT[:, :], e["gWT"]).then_inc(s["w_in"], 16)
            sp.dma_start(ng[:, :], e["norm_g"].unsqueeze(0).to_broadcast([P, DIM])).then_inc(s["w_in"], 16)
            sp.dma_start(gbb[:, :], e["gb"].unsqueeze(0).to_broadcast([P, DIM])).then_inc(s["w_in"], 16)

        @block.tensor
        def _(pe):
            pe.wait_ge(s["w_in"], 64)
            for g in range(GROUPS):
                if g >= 2:
                    pe.wait_ge(s["on"], g - 1)
                for j in range(G):
                    w = G * g + j
                    mm = pe.matmul(banks[g % 2][:, j * DIM:(j + 1) * DIM], RT[:, w, :], woT[:, :], start=True, stop=True)
                mm.then_inc(s["o_mm"], 1)
                if g >= 2:
                    pe.wait_ge(s["ga"], g - 1)
                for j in range(G):
                    w = G * g + j
                    mm = pe.matmul(banks[2 + g % 2][:, j * DIM:(j + 1) * DIM], hT[:, w, :], gwT[:, :], start=True, stop=True)
                mm.then_inc(s["g_mm"], 1)

        @block.scalar
        def _(act):
            act.preload_act_table_set(LN_EXP)
            act.wait_ge(s["ep"], 1)
            for g in range(GROUPS):
                act.wait_ge(s["o_mm"], g + 1)
                if g >= 2:
                    act.wait_ge(s["ms"], g - 1)
                act.activation(osq[:, g % 2, :], banks[g % 2][:, :], ACT.Square).then_inc(s["sq"], 1)
                act.wait_ge(s["ms"], g + 1)
                act.activation(lm[:, g, :], ms[:, g, :], ACT.Ln, bias=ep[:, 0:1], scale=1.0 / DIM).then_inc(s["lm"], 1)
                act.wait_ge(s["lm"], g + 1)
                act.activation(rm[:, g, :], lm[:, g, :], ACT.Exp, scale=-0.5).then_inc(s["rm"], 1)

        @block.vector
        def _(dve):
            dve.memset(ep[:, :], 1e-6).then_inc(s["ep"], 1)
            dve.wait_ge(s["w_in"], 64)
            for g in range(GROUPS):
                r = g % 2
                dve.wait_ge(s["sq"], g + 1)
                dve.tensor_reduce(ms[:, g, :], w3(osq[:, r, :]), AX.X, ALU.add).then_inc(s["ms"], 1)
                if g >= 2:
                    dve.wait_ge(s["y"], g - 1)
                dve.wait_ge(s["g_mm"], g + 1)
                dve.tensor_tensor(w3(ga[:, r, :]), w3(banks[2 + r][:, :]), bc(gbb), ALU.add).then_inc(s["ga"], 1)
                dve.wait_ge(s["ga"], g + 1)
                dve.tensor_tensor(w3(ga[:, r, :]), w3(ga[:, r, :]), bc(ng), ALU.mult).then_inc(s["ga2"], 1)
                dve.wait_ge(s["rm"], g + 1)
                dve.tensor_tensor(w3(on[:, r, :]), w3(banks[r][:, :]), rm[:, g, :].unsqueeze(2).to_broadcast([P, G, DIM]),
                                  ALU.mult).then_inc(s["on"], 1)
                dve.wait_ge(s["ga2"], g + 1)
                dve.wait_ge(s["on"], g + 1)
                dve.tensor_tensor(Y[:, g * N:(g + 1) * N], ga[:, r, :], on[:, r, :], ALU.mult).then_inc(s["y"], 1)

def network(nc, hidden, proj, cols, mW1T, mW2T, mW2, WoT, gWT, norm_g, gb, Wqkv, q_scale, k_scale, Wo, ln_g, ln_b,
            W1, b1, W2, b2, rotary, masks, ident_in, center_in, mean_in, out):
    x_mid = nc.dram_tensor("x_mid", hidden.shape, F32, kind="Internal").ap()
    memory(nc, hidden, proj, cols, mW1T, mW2T, mW2, WoT, gWT, norm_g, gb, mean_in, ident_in, x_mid)
    transformer(nc, x_mid, Wqkv, q_scale, k_scale, Wo, ln_g, ln_b, W1, b1, W2, b2, rotary, masks, ident_in, center_in, out,
                DEPTH=Wqkv.shape[0])


def shape_constants(tokens, window, head_dim, batches):
    half = np.arange(0, head_dim, 2, dtype=np.float32)
    inv_freq = (1.0 / 10000.0 ** (half / head_dim)).astype(np.float32)
    t = np.arange(tokens, dtype=np.float32)
    freqs = t[:, None] * inv_freq[None, :]
    base = ((half + 0.4 * head_dim) / (1.4 * head_dim)).astype(np.float32)
    power = ((t - tokens // 2) / (window // 2)).astype(np.float32)
    scale = (base[None, :] ** power[:, None]).astype(np.float32)
    inv = np.float32(1.0) / scale
    tables = np.stack([np.cos(freqs) * scale, np.sin(freqs) * scale, np.cos(freqs) * inv, np.sin(freqs) * inv], 1)
    tables = tables.astype(np.float32).reshape(tokens // window, window, 2 * head_dim).transpose(1, 0, 2)
    tables = np.broadcast_to(tables[None], (batches,) + tables.shape).reshape(batches * window, -1)
    i, j = np.arange(window)[:, None], np.arange(window)[None, :]
    own = np.where(i < j, -1e30, 0.0)
    prev = np.where(i > j, -1e30, 0.0)
    none = np.full((window, window), -1e30)
    masks = np.stack([np.concatenate(pair, 1) for pair in ((own, none), (own, prev), (prev, own))], 1)
    masks = np.broadcast_to(masks[None], (batches,) + masks.shape).reshape(batches * window, 3, 2 * window)
    eye = np.eye(batches * window, dtype=np.float32)
    return dict(rotary=tables, masks=masks.astype(np.float32), ident_in=eye,
                center_in=eye - np.float32(1.0 / (batches * window)),
                mean_in=np.kron(np.eye(batches), np.full((window, window), 1.0 / window)).astype(np.float32))


def kernel(**inputs):
    import concourse.bacc as _bacc
    from concourse.bass_utils import run_bass_kernel_spmd as _run

    attn = lambda name: np.asarray(inputs["L0_attn_" + name])
    ffn = lambda name: np.asarray(inputs["L0_ffn_" + name])
    hidden = attn("hidden")
    batches, tokens, dim = hidden.shape
    window = P // batches
    windows = tokens // window
    arrays = dict(
        hidden=hidden.reshape(batches, windows, window, dim).transpose(0, 2, 1, 3).reshape(P, windows * dim),
        proj=np.stack([attn(n).T for n in ("Wk", "Wv", "Wq", "aW", "eW", "tW")], 1),
        cols=np.tile(np.concatenate([np.concatenate([attn(w), attn(b)[:, None]], 1)
                                     for w, b in (("ckw", "ckb"), ("cvw", "cvb"), ("cqw", "cqb"))]
                                    + [attn(n)[:, None] for n in ("ab", "eb", "tb")], 1), (batches, 1)),
        mW1T=attn("mW1").T, mW2T=attn("mW2").T, mW2=attn("mW2"), WoT=attn("Wo").T, gWT=attn("gW").T,
        norm_g=attn("norm_g"), gb=attn("gb"),
        Wqkv=ffn("Wqkv"), q_scale=ffn("q_scale"), k_scale=ffn("k_scale"), Wo=ffn("Wo"),
        ln_g=ffn("ln_g").T, ln_b=ffn("ln_b").T, W1=ffn("W1"), b1=ffn("b1"), W2=ffn("W2"), b2=ffn("b2"),
        **shape_constants(tokens, window, inputs["L0_ffn_q_scale"].shape[1], batches))
    nc = _bacc.Bacc("TRN2", target_bir_lowering=False, num_devices=1)
    feeds, aps = {}, {}
    for name, a in arrays.items():
        a = np.ascontiguousarray(a)
        feeds["in_" + name] = a
        aps[name] = nc.dram_tensor("in_" + name, a.shape, mybir.dt.from_np(a.dtype), kind="ExternalInput").ap()
    out = nc.dram_tensor("stream_out", (P, windows * dim), F32, kind="ExternalOutput").ap()
    network(nc, out=out, **aps)
    result = _run(nc, [feeds], core_ids=[0]).results[0]["stream_out"]
    return result.reshape(batches, window, windows, dim).transpose(0, 2, 1, 3).reshape(batches, tokens, dim)
```

```python
from contextlib import ExitStack

import numpy as np

import concourse.bass as bass
from concourse import mybir

ALU = mybir.AluOpType
ACT = mybir.ActivationFunctionType
AX = mybir.AxisListType
F32 = mybir.dt.float32
BF16 = mybir.dt.bfloat16

P = 128
LN_EXP = "natural_log_exp_and_others"
SIGMOID = "sigmoid_and_others"


def transformer(nc, x_mid, Wqkv, q_scale, k_scale, Wo, ln_g, ln_b, W1, b1, W2, b2,
                rotary, masks, ident_in, center_in, out, DEPTH=6):
    DIM = Wqkv.shape[1]
    INNER = Wo.shape[1]
    DH = q_scale.shape[1]
    HEADS = INNER // DH
    PAIRS = HEADS // 2
    HALF = DH // 2
    B = 4
    WIN = P // B
    NW = x_mid.shape[1] // DIM
    HID = W2.shape[1]
    HC = -(-HID // P)
    LAYERS = DEPTH
    TILES = LAYERS * NW
    QKS = 8.0
    LOG2_SHIFT = 20
    assert DIM == P and HEADS == 16 and DH == 64 and WIN == 32

    with ExitStack() as ctx:
        def sb(name, shape, dt=F32):
            return ctx.enter_context(nc.sbuf_tensor(name, shape, dt))

        def sem(name):
            return nc.alloc_semaphore(name)

        X = sb("X", [P, NW * DIM])
        tab = sb("tab", [P, NW * 4 * HALF])
        wqkv = sb("wqkv", [P, 2, 3 * INNER])
        wo = sb("wo", [P, 2, PAIRS * DIM])
        w1 = sb("w1", [P, LAYERS, 2 * HID])
        b1b = sb("b1b", [P, LAYERS, 2 * HID])
        w2 = sb("w2", [P, LAYERS, HC * DIM])
        b2b = sb("b2b", [P, LAYERS, DIM])
        qks = sb("qks", [P, LAYERS, 4 * DH])
        ident = sb("ident", [P, P])
        center = sb("center", [P, P])
        identb = sb("identb", [P, P], BF16)
        maskb = sb("maskb", [P, 3 * PAIRS * 2 * WIN], BF16)
        first = sb("first", [P, NW])

        R0 = ctx.enter_context(nc.psum_tensor("R0", [P, 1024], F32))
        R1 = ctx.enter_context(nc.psum_tensor("R1", [P, 1024], F32))
        R2 = ctx.enter_context(nc.psum_tensor("R2", [P, 1024], F32))
        b6 = ctx.enter_context(nc.psum_tensor("b6", [P, 512], F32))
        b7 = ctx.enter_context(nc.psum_tensor("b7", [P, 512], F32))

        wqkv_in = sem("wqkv_in")
        wo_in = sem("wo_in")
        x_ready = sem("x_ready")
        prep(nc, ctx, locals())
        stream(nc, ctx, locals())
        finish(nc, ctx, locals())


def prep(nc, ctx0, e):
    (X, tab, wqkv, wo, w1, b1b, w2, b2b, qks, ident, center, identb, maskb, first, R0, R1) = (e[k] for k in (
        "X", "tab", "wqkv", "wo", "w1", "b1b", "w2", "b2b", "qks", "ident", "center", "identb", "maskb", "first", "R0", "R1"))
    DIM, DH, HALF, NW, HID, HC, LAYERS, PAIRS, WIN = (e[k] for k in ("DIM", "DH", "HALF", "NW", "HID", "HC", "LAYERS", "PAIRS", "WIN"))
    G = 4
    GROUPS = NW // G
    with ExitStack() as ctx:
        def sb(name, shape, dt=F32):
            return ctx.enter_context(nc.sbuf_tensor(name, shape, dt))

        def sem(name):
            return nc.alloc_semaphore(name)

        w1r = sb("w1r", [P, LAYERS, 2 * HID])
        lng = sb("lng", [P, LAYERS])
        lnb = sb("lnb", [P, LAYERS])
        ones = sb("ones", [P, P])
        brep = sb("brep", [P, LAYERS, P])
        maskf = sb("maskf", [P, 3, 2 * WIN])
        m_in = sem("m_in"); s_in = sem("s_in"); x_in = sem("x_in"); w1_in = sem("w1_in")
        v = sem("v_step"); w1_mm = sem("w1_mm"); b1_mm = sem("b1_mm"); w1_ev = sem("w1_ev"); pad_done = sem("pad_done")
        w1g_ready = sem("w1g_ready"); brep_ready = sem("brep_ready")
        wi, wo_s = e["wqkv_in"], e["wo_in"]
        loads(nc, e, dict(w1r=w1r, lng=lng, lnb=lnb, maskf=maskf, x_in=x_in, s_in=s_in, w1_in=w1_in, m_in=m_in, pad_done=pad_done))
        layer_norm(nc, e, X, None, "mid")
        block = ctx.enter_context(nc.Block())

        @block.tensor
        def _(pe):
            pe.wait_ge(s_in, 16 * 7)
            for l in range(LAYERS):
                pe.wait_ge(brep_ready, l + 1)
                if l == 0:
                    pe.wait_ge(w1_in, 16 * LAYERS)
                if l >= 1:
                    pe.wait_ge(w1_ev, 2 * l)
                for h in range(2):
                    mm = pe.matmul(R0[:, 512 * h:512 * h + HID], brep[:, l, :], w1r[:, l, h * HID:(h + 1) * HID],
                                   start=True, stop=True)
                mm.then_inc(b1_mm, 1)
                pe.wait_ge(w1g_ready, l + 1)
                for h in range(2):
                    mm = pe.matmul(R1[:, 512 * h:512 * h + HID], center[:, :], w1[:, l, h * HID:(h + 1) * HID],
                                   start=True, stop=True)
                mm.then_inc(w1_mm, 1)

        @block.vector
        def _(dve):
            steps = [0]

            def link(ins):
                steps[0] += 1
                ins.then_inc(v, 1)
                dve.wait_ge(v, steps[0])

            dve.memset(ones[:, :], 1.0).then_inc(v, 1)
            dve.memset(first[:, :], 1.0).then_inc(v, 1)
            steps[0] = 2
            dve.wait_ge(v, 2)
            link(dve.memset(first[:, 0:1], 0.0))
            dve.wait_ge(s_in, 16 * 7)
            link(dve.tensor_copy(identb[:, :], ident[:, :]))
            link(dve.tensor_copy(maskb[:, :].rearrange("p (m c k) -> p m c k", m=3, c=PAIRS),
                                 maskf[:, :, :].unsqueeze(2).to_broadcast([P, 3, PAIRS, 2 * WIN])))
            for l in range(LAYERS):
                dve.tensor_scalar(brep[:, l, :], ones[:, :], lnb[:, l:l + 1], None, ALU.mult).then_inc(brep_ready, 1)
            for l in range(LAYERS):
                if l == 0:
                    dve.wait_ge(w1_in, 16 * LAYERS)
                dve.tensor_scalar(w1[:, l, :], w1r[:, l, :], lng[:, l:l + 1], None, ALU.mult).then_inc(w1g_ready, 1)
                dve.wait_ge(b1_mm, l + 1)
                bv = b1b[:, l, :].rearrange("p (h n) -> p h n", h=2)
                dve.tensor_tensor(bv, R0[:, :].rearrange("p (h n) -> p h n", h=2)[:, :, 0:HID], bv, ALU.add).then_inc(w1_ev, 1)
                dve.wait_ge(w1_mm, l + 1)
                dve.tensor_copy(w1[:, l, :].rearrange("p (h n) -> p h n", h=2),
                                R1[:, :].rearrange("p (h n) -> p h n", h=2)[:, :, 0:HID]).then_inc(w1_ev, 1)
            dve.wait_ge(m_in, 16 * (7 + HC))
            qv = qks[:, :, :].rearrange("p l (c d) -> p l c d", d=DH)
            for c in (1, 3):
                link(dve.tensor_scalar(qv[:, :, c, 0:HALF], qv[:, :, c, 0:HALF], -1.0, None, ALU.mult))


def loads(nc, e, d):
    X, tab, wqkv, wo, b1b, w2, b2b, qks, ident, center = (e[k] for k in (
        "X", "tab", "wqkv", "wo", "b1b", "w2", "b2b", "qks", "ident", "center"))
    DIM, DH, HALF, HID, HC, LAYERS = (e[k] for k in ("DIM", "DH", "HALF", "HID", "HC", "LAYERS"))
    w1r, lng, lnb, maskf, x_in, s_in, w1_in, m_in, pad_done = (d[k] for k in (
        "w1r", "lng", "lnb", "maskf", "x_in", "s_in", "w1_in", "m_in", "pad_done"))
    wi, wo_s = e["wqkv_in"], e["wo_in"]
    with ExitStack() as ctx:
        block = ctx.enter_context(nc.Block())

        @block.sync
        def _(sp):
            sp.dma_start(X[:, :], e["x_mid"]).then_inc(x_in, 16)
            sp.dma_start(ident[:, :], e["ident_in"]).then_inc(s_in, 16)
            sp.dma_start(center[:, :], e["center_in"]).then_inc(s_in, 16)
            sp.dma_start(maskf[:, :, :], e["masks"]).then_inc(s_in, 16)
            sp.dma_start(lng[:, :], e["ln_g"]).then_inc(s_in, 16)
            sp.dma_start(lnb[:, :], e["ln_b"]).then_inc(s_in, 16)
            sp.dma_start(b1b[:, :, :], e["b1"].unsqueeze(0).to_broadcast([P, LAYERS, 2 * HID])).then_inc(s_in, 16)
            sp.dma_start(b2b[:, :, :], e["b2"].unsqueeze(0).to_broadcast([P, LAYERS, DIM])).then_inc(s_in, 16)
            sp.dma_start(wqkv[:, 0, :], e["Wqkv"][0]).then_inc(wi, 16)
            sp.dma_start(wo[:, 0, :].rearrange("p (c n) -> p c n", n=DIM),
                         e["Wo"][0].rearrange("(c p) n -> p c n", p=P)).then_inc(wo_s, 16)
            sp.wait_ge(x_in, 16)

        @block.scalar
        def _(act):
            for l in range(LAYERS):
                act.dma_start(w1r[:, l, :], e["W1"][l]).then_inc(w1_in, 16)
            act.dma_start(tab[:, :], e["rotary"]).then_inc(m_in, 16)
            qv = qks[:, :, :].rearrange("p l (c d) -> p l c d", d=DH)
            for c, s in ((0, e["q_scale"]), (2, e["k_scale"])):
                s = s.unsqueeze(0).to_broadcast([P, LAYERS, DH])
                act.dma_start(qv[:, :, c, :], s).then_inc(m_in, 16)
                act.dma_start(qv[:, :, c + 1, 0:HALF], s[:, :, HALF:DH]).then_inc(m_in, 16)
                act.dma_start(qv[:, :, c + 1, HALF:DH], s[:, :, 0:HALF]).then_inc(m_in, 16)
            act.wait_ge(pad_done, 1)
            w2v = w2[:, :, :].rearrange("p l (c n) -> p l c n", n=DIM)
            for c in range(HC):
                n = min(P, HID - c * P)
                act.dma_start(w2v[0:n, :, c, :], e["W2"][0:LAYERS, c * P:c * P + n, :].rearrange("l p n -> p l n")).then_inc(m_in, 16)

        @block.vector
        def _(dve):
            dve.memset(w2[:, :, :], 0.0).then_inc(pad_done, 1)


def layer_norm(nc, e, X, resid, tag):
    DIM, NW = e["DIM"], e["NW"]
    G = 4
    GROUPS = NW // G
    N = G * DIM
    with ExitStack() as ctx:
        def sb(name, shape, dt=F32):
            return ctx.enter_context(nc.sbuf_tensor(name, shape, dt))

        def sem(name):
            return nc.alloc_semaphore(name)

        sq = sb(tag + "_sq", [P, 2, N])
        su = sb(tag + "_su", [P, GROUPS, G])
        va = sb(tag + "_va", [P, GROUPS, G])
        lg = sb(tag + "_lg", [P, GROUPS, G])
        rs = sb(tag + "_rs", [P, GROUPS, G])
        eps = sb(tag + "_eps", [P, 1])
        res = sb(tag + "_res", [P, 2, N])
        v = sem(tag + "_v"); cen = sem(tag + "_cen"); sqd = sem(tag + "_sq"); vard = sem(tag + "_var"); rsd = sem(tag + "_rs"); lgd = sem(tag + "_lg")
        r_in = [sem(tag + "_rin0"), sem(tag + "_rin1")]; done = sem(tag + "_done"); st = sem(tag + "_store")
        block = ctx.enter_context(nc.Block())

        def grp(t, g):
            return t[:, g * N:(g + 1) * N].rearrange("p (w n) -> p w n", n=DIM)

        @block.sync
        def _(sp):
            if resid is None:
                return
            for g in range(GROUPS):
                if g >= 2:
                    sp.wait_ge(done, g - 1)
                sp.dma_start(res[:, g % 2, :], resid[:, g * N:(g + 1) * N]).then_inc(r_in[g % 2], 16)
                if g >= 1:
                    sp.wait_ge(done, g)
                    sp.dma_start(e["out"][:, (g - 1) * N:g * N], X[:, (g - 1) * N:g * N]).then_inc(st, 16)
            sp.wait_ge(done, GROUPS)
            sp.dma_start(e["out"][:, (GROUPS - 1) * N:GROUPS * N], X[:, (GROUPS - 1) * N:GROUPS * N]).then_inc(st, 16)
            sp.wait_ge(st, 16 * GROUPS)

        def rstd(act, g):
            act.wait_ge(vard, g + 1)
            act.activation(lg[:, g, :], va[:, g, :], ACT.Ln, bias=eps[:, 0:1], scale=1.0 / DIM).then_inc(lgd, 1)
            act.wait_ge(lgd, g + 1)
            act.activation(rs[:, g, :], lg[:, g, :], ACT.Exp, scale=-0.5).then_inc(rsd, 1)

        @block.scalar
        def _(act):
            act.preload_act_table_set(LN_EXP)
            act.wait_ge(v, 1)
            for g in range(GROUPS):
                act.wait_ge(cen, g + 1)
                if g >= 2:
                    act.wait_ge(vard, g - 1)
                act.activation(sq[:, g % 2, :], X[:, g * N:(g + 1) * N], ACT.Square).then_inc(sqd, 1)
                if g >= 1:
                    rstd(act, g - 1)
            rstd(act, GROUPS - 1)

        @block.vector
        def _(dve):
            steps = [1]

            def link(ins):
                steps[0] += 1
                ins.then_inc(v, 1)
                dve.wait_ge(v, steps[0])

            dve.memset(eps[:, :], 1e-5).then_inc(v, 1)

            def centre(g):
                link(dve.tensor_reduce(su[:, g, :], grp(X, g), AX.X, ALU.add))
                link(dve.tensor_scalar(su[:, g, :], su[:, g, :], 1.0 / DIM, None, ALU.mult))
                dve.tensor_tensor(grp(X, g), grp(X, g), su[:, g, :].unsqueeze(2).to_broadcast([P, G, DIM]),
                                  ALU.subtract).then_inc(cen, 1)

            def variance(g):
                dve.wait_ge(sqd, g + 1)
                dve.tensor_reduce(va[:, g, :], sq[:, g % 2, :].rearrange("p (w n) -> p w n", n=DIM), AX.X,
                                  ALU.add).then_inc(vard, 1)

            def scale(g):
                dve.wait_ge(rsd, g + 1)
                ins = dve.tensor_tensor(grp(X, g), grp(X, g), rs[:, g, :].unsqueeze(2).to_broadcast([P, G, DIM]), ALU.mult)
                if resid is None:
                    ins.then_inc(done, 1)
                    return
                link(ins)
                dve.wait_ge(r_in[g % 2], 16 * (g // 2 + 1))
                dve.tensor_tensor(X[:, g * N:(g + 1) * N], X[:, g * N:(g + 1) * N], res[:, g % 2, :], ALU.add).then_inc(done, 1)

            for g in range(GROUPS + 2):
                if g < GROUPS:
                    centre(g)
                if 1 <= g <= GROUPS:
                    variance(g - 1)
                if g >= 2:
                    scale(g - 2)

        if resid is None and e["x_ready"] is not None:
            @block.gpsimd
            def _(pool):
                pool.wait_ge(done, GROUPS)
                pool.sem_inc(e["x_ready"], NW)


def finish(nc, ctx0, e):
    layer_norm(nc, e, e["X"], e["x_mid"], "last")


def stream(nc, ctx0, e):
    (X, tab, wqkv, wo, w1, b1b, w2, b2b, qks, ident, center, identb, maskb, first, R0, R1, R2, b6, b7) = (e[k] for k in (
        "X", "tab", "wqkv", "wo", "w1", "b1b", "w2", "b2b", "qks", "ident", "center", "identb", "maskb", "first",
        "R0", "R1", "R2", "b6", "b7"))
    DIM, DH, HALF, NW, HID, HC, LAYERS, PAIRS, WIN, HEADS, INNER, TILES, B = (e[k] for k in (
        "DIM", "DH", "HALF", "NW", "HID", "HC", "LAYERS", "PAIRS", "WIN", "HEADS", "INNER", "TILES", "B"))
    QKS, SHIFT = e["QKS"], e["LOG2_SHIFT"]
    wqkv_in, wo_in, x_ready = e["wqkv_in"], e["wo_in"], e["x_ready"]
    K2 = 2 * WIN
    HS = PAIRS * K2
    with ExitStack() as ctx:
        def sb(name, shape, dt=F32):
            return ctx.enter_context(nc.sbuf_tensor(name, shape, dt))

        def sem(name):
            return nc.alloc_semaphore(name)

        xs = sb("xs", [P, DIM])
        XS = sb("XS", [P, B, WIN])
        XS2 = sb("XS2", [P, B, WIN])
        cx = sb("cx", [P, B])
        cx2 = sb("cx2", [P, B])
        sq = sb("sq", [P, 2 * INNER])
        ss = sb("ss", [P, 2 * HEADS])
        lss = sb("lss", [P, 2 * HEADS])
        rn = sb("rn", [P, 2 * HEADS])
        nqk = sb("nqk", [P, 2 * INNER])
        t1 = sb("t1", [P, 2 * INNER])
        t2 = sb("t2", [P, 2 * INNER])
        tb = sb("tb", [P, 4 * DH])
        QT = sb("QT", [P, PAIRS, P])
        KT = sb("KT", [P, 2, PAIRS, P])
        mx = sb("mx", [P, HEADS])
        pr = sb("pr", [P, PAIRS, 2, K2])
        sm = sb("sm", [P, PAIRS, 2])
        rc = sb("rc", [P, HEADS])
        On = sb("On", [P, INNER])
        PT = sb("PT", [P, PAIRS, P])
        Vn = sb("Vn", [P, 2, PAIRS * DH])
        V2 = sb("V2", [P, B, PAIRS * DH])
        OT = sb("OT", [P, PAIRS, P])
        x1 = sb("x1", [P, DIM])
        x1b = sb("x1b", [P, 2, DIM])
        sqx = sb("sqx", [P, DIM])
        vx = sb("vx", [P, 1])
        lvx = sb("lvx", [P, 1])
        rx = sb("rx", [P, 1])
        ha = sb("ha", [P, HID])
        hg = sb("hg", [P, HID])
        hgl = sb("hgl", [P, HID])
        ac = sb("ac", [P, HC * P])
        AT = sb("AT", [P, HC, P])
        eps = sb("eps", [P, 1])
        lsh = sb("lsh", [P, 1])

        names = ("buffers_cleared x_tile_copied x_transposed x_shifted x_shift_step values_made queries_made "
                 "keys_made values_in_sbuf values_by_key q_squared k_squared q_square_sums k_square_sums "
                 "q_sums_clamped k_sums_clamped q_sums_logged k_sums_logged q_rnorm_ready k_rnorm_ready q_normed "
                 "k_normed tables_scaled q_cos_part k_cos_part q_sin_part k_sin_part q_transposed k_transposed "
                 "q_in_sbuf k_in_sbuf scores_made row_maxima maxima_subtracted exps_made exp_sums sums_inverted "
                 "attn_normed attn_transposed probs_transposed probs_in_sbuf attn_made attn_in_sbuf "
                 "attn_projected attn_residual_added output_bias_added mid_transposed mid_shifted mid_shift_step "
                 "variance_sum variance_logged rstd_ready hidden_made gate_made hidden_ready gate_ready "
                 "first_keys_cleared q_rotated attn_issued weights_ready gelu_made activations_made "
                 "activations_transposed activations_in_sbuf ffn_projected").split()
        s = {n: sem("s_" + n) for n in names}
        block = ctx.enter_context(nc.Block())

        Q4 = lambda t: t.rearrange("p (h s d) -> p h s d", s=2, d=HALF)
        swapped = lambda t: Q4(t)[:, :, ::-1, :]
        def table(i):
            return tb[:, i * DH:(i + 1) * DH].rearrange("p (s d) -> p s d", s=2).unsqueeze(1).to_broadcast([P, HEADS, 2, HALF])

        def win(t):
            return t % NW

        def lay(t):
            return t // NW

        def drive(eng, body):
            for n in range(-1, 4):
                body(n, n % 2)
            with eng.Fori(4, TILES - 2, 2) as n:
                body(n, 0, True)
                body(n + 1, 1, True)
            for n in range(TILES - 2, TILES + 3):
                body(n, n % 2)

        def has(t, loop):
            return loop or 0 <= t < TILES

        def above(n, loop, c):
            return loop or n - c > 0

        @block.tensor
        def _(pe):
            def body(n, par, loop=False):
                new, mid, ffn, done = n, n - 1, n - 2, n - 3
                wf = wqkv[:, :, :].rearrange("p l n -> p (l n)")

                def proj(t, region, part, sig):
                    for h in range(2):
                        o = (lay(t) % 2) * (3 * INNER) + (part * INNER + 512 * h)
                        mm = pe.matmul(region[:, 512 * h:512 * h + 512], XS[:, :, :].rearrange("p b i -> p (b i)"),
                                       wf[:, bass.ds(o, 512)], start=True, stop=True)
                    mm.then_inc(s[sig], 1)

                if has(new, loop):
                    if above(n, loop, 1):
                        pe.wait_ge(s["attn_in_sbuf"], n - 1)
                    proj(n, R2, 2, "values_made")
                    if above(n, loop, 0):
                        pe.wait_ge(s["maxima_subtracted"], 2 * n)
                    proj(n, R1, 1, "keys_made")
                if has(done, loop):
                    pe.wait_ge(s["activations_made"], done + 1)
                    pe.wait_ge(s["hidden_ready"], done + 1)
                    pe.wait_ge(s["variance_sum"], done + 1)
                    if has(ffn, loop):
                        pe.wait_ge(s["mid_shifted"], ffn + 1)
                    for c in range(HC):
                        mm = pe.transpose(b6[:, c * P:(c + 1) * P], ac[:, c * P:(c + 1) * P], ident[:, :])
                    mm.then_inc(s["activations_transposed"], 1)
                if has(mid, loop):
                    pe.wait_ge(s["exps_made"], 2 * mid + 2)
                    if has(new, loop):
                        pe.wait_ge(s["values_in_sbuf"], n + 1)
                    for p in range(PAIRS):
                        mm = pe.transpose(R2[:, p * P:(p + 1) * P], pr[:, p, :, :].rearrange("p a k -> p (a k)"), ident[:, :])
                    mm.then_inc(s["probs_transposed"], 1)
                if has(ffn, loop):
                    pe.wait_ge(s["attn_residual_added"], ffn + 1)
                    pe.wait_ge(s["mid_shifted"], ffn + 1)
                    lx = XS2[:, :, :].rearrange("p b i -> p (b i)")
                    w1f = w1[:, :, :].rearrange("p l n -> p (l n)")
                    o = lay(ffn) * (2 * HID)
                    pe.matmul(b7[:, 0:HID], lx, w1f[:, bass.ds(o + HID, HID)], start=True, stop=True).then_inc(s["gate_made"], 1)
                if has(done, loop):
                    pe.wait_ge(s["activations_in_sbuf"], done + 1)
                    w2f = w2[:, :, :].rearrange("p l n -> p (l n)")
                    for c in range(HC):
                        o = lay(done) * (HC * DIM) + c * DIM
                        mm = pe.matmul(b6[:, 0:DIM], AT[:, c, :], w2f[:, bass.ds(o, DIM)], start=(c == 0), stop=(c == HC - 1))
                    mm.then_inc(s["ffn_projected"], 1)
                if has(mid, loop):
                    pe.wait_ge(s["probs_in_sbuf"], mid + 1)
                    pe.wait_ge(s["values_by_key"], (mid + 1) * (16 * 2 * B))
                    pe.sem_inc(s["attn_issued"], 1)
                    for p in range(PAIRS):
                        for a in range(2):
                            q = slice(64 * a, 64 * a + 64)
                            o = a * (INNER // 2) + p * DH
                            for b in range(B):
                                mm = pe.matmul(R2[b * WIN:(b + 1) * WIN, o:o + DH], PT[q, p, b * WIN:(b + 1) * WIN],
                                               V2[q, b, p * DH:(p + 1) * DH], start=True, stop=True)
                    mm.then_inc(s["attn_made"], 1)

                if has(ffn, loop):
                    pe.wait_ge(s["mid_shifted"], ffn + 1)
                    if has(done, loop):
                        pe.wait_ge(x_ready, done + (NW + 1))
                    lx = XS2[:, :, :].rearrange("p b i -> p (b i)")
                    w1f = w1[:, :, :].rearrange("p l n -> p (l n)")
                    o = lay(ffn) * (2 * HID)
                    pe.matmul(b6[:, 512 - DIM:512], lx, center[:, :], start=True, stop=True)
                    pe.matmul(b6[:, 0:HID], lx, w1f[:, bass.ds(o, HID)], start=True, stop=True).then_inc(s["hidden_made"], 1)

                def rotated(reg, o, a, c, sig):
                    pe.wait_ge(s[a], n + 1)
                    pe.wait_ge(s[c], n + 1)
                    for p in range(PAIRS):
                        c0 = o + p * P
                        pe.matmul(reg[:, p * P:(p + 1) * P], t1[:, c0:c0 + P], ident[:, :], is_transpose=True,
                                  start=True, stop=False)
                        mm = pe.matmul(reg[:, p * P:(p + 1) * P], t2[:, c0:c0 + P], ident[:, :], is_transpose=True,
                                       start=False, stop=True)
                    mm.then_inc(s[sig], 1)

                if has(new, loop):
                    pe.wait_ge(s["q_rotated"], n + 1)
                    for p in range(PAIRS):
                        mm = pe.transpose(R0[:, p * P:(p + 1) * P], t2[:, p * P:(p + 1) * P], ident[:, :])
                    mm.then_inc(s["q_transposed"], 1)
                if has(mid, loop):
                    pe.wait_ge(s["attn_normed"], mid + 1)
                    for p in range(PAIRS):
                        mm = pe.transpose(R2[:, p * P:(p + 1) * P], On[:, p * P:(p + 1) * P], ident[:, :])
                    mm.then_inc(s["attn_transposed"], 1)
                if has(new, loop):
                    rotated(R1, INNER, "k_cos_part", "k_sin_part", "k_transposed")
                if loop or 0 <= n + 1 < TILES:
                    pe.wait_ge(s["x_tile_copied"], n + 2)
                    if has(ffn, loop):
                        pe.wait_ge(s["hidden_ready"], ffn + 1)
                        pe.wait_ge(s["variance_sum"], ffn + 1)
                    pe.transpose(b6[:, 0:P], xs[:, :], ident[:, :]).then_inc(s["x_transposed"], 1)
                if has(mid, loop):
                    pe.wait_ge(s["attn_in_sbuf"], mid + 1)
                    pe.wait_ge(s["weights_ready"], lay(mid) + 1)
                    if has(ffn, loop):
                        pe.wait_ge(s["gate_ready"], ffn + 1)
                    wof = wo[:, :, :].rearrange("p l n -> p (l n)")
                    for p in range(PAIRS):
                        o = (lay(mid) % 2) * (PAIRS * DIM) + p * DIM
                        mm = pe.matmul(b7[:, 0:DIM], OT[:, p, :], wof[:, bass.ds(o, DIM)], start=(p == 0), stop=(p == PAIRS - 1))
                    mm.then_inc(s["attn_projected"], 1)
                for a in range(2):
                    if has(new, loop):
                        if a == 0:
                            pe.wait_ge(s["q_in_sbuf"], n + 1)
                            pe.wait_ge(s["k_in_sbuf"], n + 1)
                            if par == 0:
                                pe.wait_ge(s["first_keys_cleared"], n // 2 + 1)
                        m = ((win(n) + (NW - 1)) // NW) if par == 0 else 2
                        pe.matmul(R1[:, a * HS:(a + 1) * HS], identb[:, :], maskb[:, bass.ds(m * HS, HS)],
                                  start=True, stop=False, skip_group_check=True)
                        q = slice(64 * a, 64 * a + 64)
                        for p in range(PAIRS):
                            for b in range(B):
                                mm = pe.matmul(R1[b * WIN:(b + 1) * WIN, a * HS + p * K2:a * HS + (p + 1) * K2],
                                               QT[q, p, b * WIN:(b + 1) * WIN], KT[q, :, p, b * WIN:(b + 1) * WIN],
                                               start=False, stop=True, skip_group_check=True)
                        mm.then_inc(s["scores_made"], 1)
                    if a == 0 and has(mid, loop):
                        pe.wait_ge(s["attn_residual_added"], mid + 1)
                        if has(ffn, loop):
                            pe.wait_ge(s["hidden_ready"], ffn + 1)
                            pe.wait_ge(s["variance_sum"], ffn + 1)
                        if loop or n + 1 < TILES:
                            pe.wait_ge(s["x_shifted"], n + 2)
                        pe.transpose(b6[:, 0:P], x1[:, :], ident[:, :]).then_inc(s["mid_transposed"], 1)
                    if a == 0 and (loop or 0 <= n + 1 < TILES):
                        pe.wait_ge(s["x_shifted"], n + 2)
                        pe.wait_ge(s["weights_ready"], lay(n + 1) + 1)
                        if above(n, loop, -1):
                            pe.wait_ge(s["q_in_sbuf"], n + 1)
                        proj(n + 1, R0, 0, "queries_made")


            pe.wait_ge(s["buffers_cleared"], 6)
            drive(pe, body)

        @block.scalar
        def _(act):
            def body(n, par, loop=False):
                new, mid, ffn, done = n, n - 1, n - 2, n - 3
                def softmax_exp(a):
                    act.wait_ge(s["maxima_subtracted"], 2 * mid + 1 + a)
                    act.activation(pr[:, :, a, :], pr[:, :, a, :], ACT.Exp, scale=QKS).then_inc(s["exps_made"], 1)
                def squares(reg, o, mm, prev, sig):
                    act.wait_ge(s[mm], n + 1)
                    if above(n, loop, 0):
                        act.wait_ge(s[prev], n)
                    act.activation(sq[:, o:o + INNER], reg[:, :], ACT.Square).then_inc(s[sig], 1)

                def norms(h, c, l, r):
                    hs = slice(h * HEADS, (h + 1) * HEADS)
                    act.wait_ge(s[c], n + 1)
                    act.activation(lss[:, hs], ss[:, hs], ACT.Ln, scale=float(2 ** SHIFT)).then_inc(s[l], 1)
                    act.wait_ge(s[l], n + 1)
                    if above(n, loop, 0):
                        act.wait_ge(s["k_normed"], n)
                        act.wait_ge(s["q_normed"], n)
                    act.activation(rn[:, hs], lss[:, hs], ACT.Exp, bias=lsh[:, 0:1], scale=-0.5).then_inc(s[r], 1)

                act.preload_act_table_set(LN_EXP)
                if has(mid, loop):
                    softmax_exp(0)
                if has(new, loop):
                    squares(R0, 0, "queries_made", "q_square_sums", "q_squared")
                if has(mid, loop):
                    softmax_exp(1)
                if has(new, loop):
                    act.wait_ge(s["values_made"], n + 1)
                    if above(n, loop, 0):
                        act.wait_ge(s["values_by_key"], n * (16 * 2 * B))
                    act.activation(Vn[:, :, :].rearrange("p a (c d) -> p c a d", d=DH),
                                   R2[:, :].rearrange("p (c a d) -> p c a d", a=2, d=DH), ACT.Copy).then_inc(s["values_in_sbuf"], 1)
                    norms(0, "q_sums_clamped", "q_sums_logged", "q_rnorm_ready")
                if has(new, loop):
                    squares(R1, INNER, "keys_made", "k_square_sums", "k_squared")
                if has(done, loop):
                    act.wait_ge(s["activations_transposed"], done + 1)
                    act.activation(AT[:, :, :].rearrange("p c k -> p (c k)"), b6[:, 0:HC * P], ACT.Copy).then_inc(s["activations_in_sbuf"], 1)
                if has(mid, loop):
                    act.wait_ge(s["probs_transposed"], mid + 1)
                    act.activation(PT[:, :, :].rearrange("p c k -> p (c k)"), R2[:, :], ACT.Copy).then_inc(s["probs_in_sbuf"], 1)
                if has(new, loop):
                    norms(1, "k_sums_clamped", "k_sums_logged", "k_rnorm_ready")
                if has(ffn, loop):
                    act.wait_ge(s["hidden_made"], ffn + 1)
                    act.activation(sqx[:, :], b6[:, 512 - DIM:512], ACT.Square, accum_out=vx[:, 0:1]).then_inc(s["variance_sum"], 1)
                    act.wait_ge(s["variance_sum"], ffn + 1)
                    act.activation(lvx[:, :], vx[:, :], ACT.Ln, bias=eps[:, 0:1], scale=1.0 / DIM).then_inc(s["variance_logged"], 1)
                    act.wait_ge(s["variance_logged"], ffn + 1)
                    act.activation(rx[:, :], lvx[:, :], ACT.Exp, scale=-0.5).then_inc(s["rstd_ready"], 1)
                if has(new, loop):
                    act.wait_ge(s["q_transposed"], n + 1)
                    act.activation(QT[:, :, :].rearrange("p c k -> p (c k)"), R0[:, :], ACT.Copy).then_inc(s["q_in_sbuf"], 1)
                if has(mid, loop):
                    act.wait_ge(s["attn_transposed"], mid + 1)
                    act.activation(OT[:, :, :].rearrange("p c k -> p (c k)"), R2[:, :], ACT.Copy).then_inc(s["attn_in_sbuf"], 1)
                if has(new, loop):
                    act.wait_ge(s["k_transposed"], n + 1)
                    act.activation(KT[:, par, :, :].rearrange("p c k -> p (c k)"), R1[:, :], ACT.Copy).then_inc(s["k_in_sbuf"], 1)
                if has(ffn, loop):
                    act.wait_ge(s["gate_ready"], ffn + 1)
                    act.activation(hgl[:, :], hg[:, :], ACT.Gelu).then_inc(s["gelu_made"], 1)

            act.wait_ge(s["buffers_cleared"], 6)
            drive(act, body)

        @block.vector
        def _(dve):
            dve.memset(KT[:, :, :, :], 0.0).then_inc(s["buffers_cleared"], 1)
            dve.memset(V2[:, :, :], 0.0).then_inc(s["buffers_cleared"], 1)
            dve.memset(cx[:, :], 0.0).then_inc(s["buffers_cleared"], 1)
            dve.memset(cx2[:, :], 0.0).then_inc(s["buffers_cleared"], 1)
            dve.memset(ac[:, :], 0.0).then_inc(s["buffers_cleared"], 1)
            dve.memset(eps[:, :], 1e-5).then_inc(s["buffers_cleared"], 1)
            dve.memset(lsh[:, :], 0.5 * SHIFT * float(np.log(2.0))).then_inc(s["buffers_cleared"], 1)

            def shifted(t, loop, src, dst, carry, step, done):
                up = slice(DIM // 2, DIM)
                lo = slice(0, DIM // 2)
                sv = src[:, 0:P].rearrange("p (b i) -> p b i", b=B)
                dve.tensor_copy(dst[lo, :, :], sv[lo, :, :]).then_inc(s[step], 1)
                dve.tensor_copy(dst[up, :, 1:WIN], sv[up, :, 0:WIN - 1]).then_inc(s[step], 1)
                dve.tensor_scalar(dst[up, :, 0], carry[up, :], first[up, bass.ds(win(t), 1)], None, ALU.mult).then_inc(s[step], 1)
                dve.wait_ge(s[step], t * 3 + 3)
                dve.tensor_copy(carry[up, :], sv[up, :, WIN - 1]).then_inc(s[done], 1)

            def body(n, par, loop=False):
                new, mid, ffn, done = n, n - 1, n - 2, n - 3
                def square_sums(h, a, b_, c):
                    hs = slice(h * HEADS, (h + 1) * HEADS)
                    dve.wait_ge(s[a], n + 1)
                    if above(n, loop, 0):
                        dve.wait_ge(s["k_sums_logged"], n)
                    dve.tensor_reduce(ss[:, hs], sq[:, h * INNER:(h + 1) * INNER].rearrange("p (h d) -> p h d", d=DH),
                                      AX.X, ALU.add).then_inc(s[b_], 1)
                    dve.wait_ge(s[b_], n + 1)
                    dve.tensor_scalar(ss[:, hs], ss[:, hs], 1e-24, None, ALU.max).then_inc(s[c], 1)

                if has(new, loop):
                    square_sums(0, "q_squared", "q_square_sums", "q_sums_clamped")
                def normed(h, reg, r, d, prev):
                    dve.wait_ge(s[r], n + 1)
                    if above(n, loop, 0):
                        dve.wait_ge(s[prev], n)
                    dve.tensor_tensor(nqk[:, h * INNER:(h + 1) * INNER].rearrange("p (h d) -> p h d", d=DH),
                                      reg[:, :].rearrange("p (h d) -> p h d", d=DH),
                                      rn[:, h * HEADS:(h + 1) * HEADS].unsqueeze(2).to_broadcast([P, HEADS, DH]),
                                      ALU.mult).then_inc(s[d], 1)

                def cosines(h, d, t, prev):
                    hs = slice(h * INNER, (h + 1) * INNER)
                    dve.wait_ge(s[d], n + 1)
                    dve.wait_ge(s["tables_scaled"], n + 1)
                    if above(n, loop, 0):
                        dve.wait_ge(s[prev], n)
                    dve.tensor_tensor(Q4(t1[:, hs]), Q4(nqk[:, hs]), table(2 * h), ALU.mult).then_inc(s[t], 1)

                def exp_sums(a):
                    dve.wait_ge(s["exps_made"], 2 * mid + 1 + a)
                    if above(mid, loop, 0):
                        dve.wait_ge(s["sums_inverted"], mid)
                    dve.tensor_reduce(sm[:, :, a], pr[:, :, a, :], AX.X, ALU.add).then_inc(s["exp_sums"], 1)

                if has(mid, loop):
                    exp_sums(0)
                if has(new, loop):
                    normed(0, R0, "q_rnorm_ready", "q_normed", "q_sin_part")
                    square_sums(1, "k_squared", "k_square_sums", "k_sums_clamped")
                    cosines(0, "q_normed", "q_cos_part", "q_transposed")
                if has(mid, loop):
                    exp_sums(1)
                    dve.wait_ge(s["exp_sums"], 2 * mid + 2)
                    if above(mid, loop, 0):
                        dve.wait_ge(s["attn_normed"], mid)
                    dve.reciprocal(rc[:, :], sm[:, :, :].rearrange("p c a -> p (c a)")).then_inc(s["sums_inverted"], 1)
                if has(done, loop):
                    dve.wait_ge(s["ffn_projected"], done + 1)
                    dve.wait_ge(s["output_bias_added"], done + 1)
                    dve.tensor_tensor(X[:, bass.ds(win(done) * DIM, DIM)], b6[:, 0:DIM], x1b[:, 1 - par, :], ALU.add).then_inc(x_ready, 1)
                if has(new, loop):
                    normed(1, R1, "k_rnorm_ready", "k_normed", "k_sin_part")
                if has(mid, loop):
                    dve.wait_ge(s["attn_made"], mid + 1)
                    dve.wait_ge(s["sums_inverted"], mid + 1)
                    if above(mid, loop, 0):
                        dve.wait_ge(s["attn_transposed"], mid)
                    dve.tensor_tensor(On[:, :].rearrange("p (c a d) -> p c a d", a=2, d=DH),
                                      R2[:, :].rearrange("p (a c d) -> p c a d", a=2, d=DH),
                                      rc[:, :].rearrange("p (c a) -> p c a", a=2).unsqueeze(3).to_broadcast([P, PAIRS, 2, DH]),
                                      ALU.mult).then_inc(s["attn_normed"], 1)
                if has(new, loop):
                    cosines(1, "k_normed", "k_cos_part", "k_transposed")
                if has(ffn, loop):
                    b1f = b1b[:, :, :].rearrange("p l n -> p (l n)")
                    o = lay(ffn) * (2 * HID)
                    dve.wait_ge(s["rstd_ready"], ffn + 1)
                    dve.wait_ge(s["hidden_made"], ffn + 1)
                    dve.scalar_tensor_tensor(out=ha[:, :], in0=b6[:, 0:HID], scalar=rx[:, 0:1], in1=b1f[:, bass.ds(o, HID)],
                                             op0=ALU.mult, op1=ALU.add).then_inc(s["hidden_ready"], 1)
                    dve.wait_ge(s["gate_made"], ffn + 1)
                    dve.scalar_tensor_tensor(out=hg[:, :], in0=b7[:, 0:HID], scalar=rx[:, 0:1], in1=b1f[:, bass.ds(o + HID, HID)],
                                             op0=ALU.mult, op1=ALU.add).then_inc(s["gate_ready"], 1)
                if has(new, loop) and par == 0:
                    if above(n, loop, 0):
                        dve.wait_ge(s["scores_made"], 2 * n)
                        dve.wait_ge(s["k_in_sbuf"], n)
                    kz = KT[:, 1, :, :].rearrange("p c k -> p (c k)")
                    dve.tensor_scalar(kz, kz, first[:, bass.ds(win(n), 1)], None, ALU.mult).then_inc(s["first_keys_cleared"], 1)
                if loop or 0 <= n + 1 < TILES:
                    t = n + 1
                    dve.wait_ge(s["x_transposed"], t + 1)
                    if above(t, loop, 0):
                        dve.wait_ge(s["keys_made"], t)
                        dve.wait_ge(s["x_shifted"], t)
                    shifted(t, loop, b6, XS, cx, "x_shift_step", "x_shifted")
                if has(mid, loop):
                    dve.wait_ge(s["attn_projected"], mid + 1)
                    if above(mid, loop, 0):
                        dve.wait_ge(s["output_bias_added"], mid)
                        dve.wait_ge(s["mid_transposed"], mid)
                    dve.tensor_tensor(x1[:, :], b7[:, 0:DIM], X[:, bass.ds(win(mid) * DIM, DIM)], ALU.add).then_inc(s["attn_residual_added"], 1)
                    dve.wait_ge(s["mid_transposed"], mid + 1)
                    if above(mid, loop, 0):
                        dve.wait_ge(s["gate_made"], mid)
                        dve.wait_ge(s["mid_shifted"], mid)
                    shifted(mid, loop, b6, XS2, cx2, "mid_shift_step", "mid_shifted")
                if has(ffn, loop):
                    dve.wait_ge(s["gelu_made"], ffn + 1)
                    if above(ffn, loop, 0):
                        dve.wait_ge(s["activations_transposed"], ffn)
                    dve.tensor_tensor(ac[:, 0:HID], ha[:, :], hgl[:, :], ALU.mult).then_inc(s["activations_made"], 1)
                if has(new, loop):
                    for a in range(2):
                        hs = slice(a * PAIRS, (a + 1) * PAIRS)
                        sv = R1[:, a * HS:(a + 1) * HS].rearrange("p (c k) -> p c k", k=K2)
                        dve.wait_ge(s["scores_made"], 2 * n + 1 + a)
                        dve.tensor_reduce(mx[:, hs], sv, AX.X, ALU.max).then_inc(s["row_maxima"], 1)
                        dve.wait_ge(s["row_maxima"], 2 * n + 1 + a)
                        if above(n, loop, 0):
                            dve.wait_ge(s["probs_transposed"], n)
                            dve.wait_ge(s["exp_sums"], 2 * n)
                        dve.tensor_tensor(pr[:, :, a, :], sv,
                                          mx[:, hs].unsqueeze(2).to_broadcast([P, PAIRS, K2]), ALU.subtract).then_inc(s["maxima_subtracted"], 1)

            dve.wait_ge(s["buffers_cleared"], 7)
            drive(dve, body)

        @block.gpsimd
        def _(pool):
            def body(n, par, loop=False):
                new, mid, ffn, done = n, n - 1, n - 2, n - 3
                if has(new, loop):
                    if above(n, loop, 0):
                        pool.wait_ge(s["k_cos_part"], n)
                        pool.wait_ge(s["k_sin_part"], n)
                    qf = qks[:, :, :].rearrange("p l n -> p (l n)")
                    pool.tensor_tensor(tb[:, :].rearrange("p (c s d) -> p c s d", s=2, d=HALF),
                                       qf[:, bass.ds(lay(n) * (4 * DH), 4 * DH)].rearrange("p (c s d) -> p c s d", s=2, d=HALF),
                                       tab[:, bass.ds(win(n) * (4 * HALF), 4 * HALF)].rearrange("p (c d) -> p c d", d=HALF)
                                       .unsqueeze(2).to_broadcast([P, 4, 2, HALF]), ALU.mult).then_inc(s["tables_scaled"], 1)
                if loop or 0 <= n + 1 < TILES:
                    t = n + 1
                    pool.wait_ge(x_ready, t + 1)
                    if above(t, loop, 0):
                        pool.wait_ge(s["x_transposed"], t)
                    pool.tensor_copy(xs[:, :], X[:, bass.ds(win(t) * DIM, DIM)]).then_inc(s["x_tile_copied"], 1)
                if has(new, loop):
                    pool.wait_ge(s["tables_scaled"], n + 1)
                    for h, d, t, prev in ((0, "q_normed", "q_sin_part", "q_transposed"), (1, "k_normed", "k_sin_part", "k_transposed")):
                        hs = slice(h * INNER, (h + 1) * INNER)
                        if h == 1:
                            pool.wait_ge(s["q_cos_part"], n + 1)
                            pool.wait_ge(s["q_sin_part"], n + 1)
                            qs = slice(0, INNER)
                            pool.tensor_tensor(t2[:, qs], t2[:, qs], t1[:, qs], ALU.add).then_inc(s["q_rotated"], 1)
                        pool.wait_ge(s[d], n + 1)
                        if above(n, loop, 0):
                            pool.wait_ge(s[prev], n)
                        pool.tensor_tensor(Q4(t2[:, hs]), swapped(nqk[:, hs]), table(2 * h + 1), ALU.mult).then_inc(s[t], 1)
                if has(mid, loop):
                    pool.wait_ge(s["attn_residual_added"], mid + 1)
                    if above(mid, loop, 1):
                        pool.wait_ge(x_ready, mid + (NW - 1))
                    b2f = b2b[:, :, :].rearrange("p l n -> p (l n)")
                    pool.tensor_tensor(x1b[:, 1 - par, :], x1[:, :], b2f[:, bass.ds(lay(mid) * DIM, DIM)], ALU.add).then_inc(s["output_bias_added"], 1)

            pool.wait_ge(s["buffers_cleared"], 7)
            drive(pool, body)

        @block.sync
        def _(sp):
            def values(t, par, loop=False):
                sp.wait_ge(s["values_in_sbuf"], t + 1)
                if above(t, loop, 0):
                    sp.wait_ge(s["attn_made"], t)
                for a in range(2):
                    for b in range(B):
                        q = 64 * a + WIN * par
                        sp.dma_start(V2[q:q + WIN, b, :], Vn[b * WIN:(b + 1) * WIN, a, :]).then_inc(s["values_by_key"], 16)

            sp.wait_ge(s["buffers_cleared"], 7)
            sp.wait_ge(wqkv_in, 16)
            sp.wait_ge(wo_in, 16)
            sp.sem_inc(s["weights_ready"], 1)
            for l in range(LAYERS):
                t0 = l * NW
                values(t0, 0)
                values(t0 + 1, 1)
                if l + 1 < LAYERS:
                    sl = (l + 1) % 2
                    if l >= 1:
                        sp.wait_ge(s["keys_made"], t0)
                    sp.dma_start(wqkv[:, sl, :], e["Wqkv"][l + 1]).then_inc(wqkv_in, 16)
                    if l >= 1:
                        sp.wait_ge(s["attn_projected"], t0)
                    sp.dma_start(wo[:, sl, :].rearrange("p (c n) -> p c n", n=DIM),
                                 e["Wo"][l + 1].rearrange("(c p) n -> p c n", p=P)).then_inc(wo_in, 16)
                with sp.Fori(t0 + 2, t0 + NW - 2, 2) as t:
                    values(t, 0, True)
                    values(t + 1, 1, True)
                if l + 1 < LAYERS:
                    sp.wait_ge(wqkv_in, 16 * (l + 2))
                    sp.wait_ge(wo_in, 16 * (l + 2))
                    sp.sem_inc(s["weights_ready"], 1)
                values(t0 + NW - 2, 0)
                values(t0 + NW - 1, 1)
            sp.wait_ge(s["values_by_key"], TILES * 16 * 2 * B)


def memory(nc, hidden, proj, cols, mW1T, mW2T, mW2, WoT, gWT, norm_g, gb, mean_in, ident_in, x_mid):
    B, WIN = 4, P // 4
    DIM = gWT.shape[0]
    D = mW1T.shape[0]
    NW = hidden.shape[1] // DIM
    S = NW * WIN
    C = 64
    NC = S // C
    with ExitStack() as ctx:
        def sb(name, shape, dt=F32):
            return ctx.enter_context(nc.sbuf_tensor(name, shape, dt))

        Y = sb("Y", [P, NW * DIM])
        hT = sb("hT", [P, NW, P])
        big = sb("big", [P, 9, S])
        ident = sb("m_ident", [P, P])
        MT = sb("MT", [C, B, S])
        E = sb("E", [C, B, S])
        banks = [ctx.enter_context(nc.psum_tensor(f"bank{i}", [P, 512], F32)) for i in range(8)]
        e = dict(locals())
        e.update(x_ready=None, out=x_mid)
        load_and_norm(nc, e)
        gates(nc, e)
        read = chunks(nc, ctx, e)
        e["RT"] = read
        output(nc, e)
        layer_norm(nc, dict(DIM=DIM, NW=NW, out=x_mid), Y, hidden, "memory")


def load_and_norm(nc, e):
    with ExitStack() as ctx:
        x_in = nc.alloc_semaphore("y_in")
        block = ctx.enter_context(nc.Block())

        @block.sync
        def _(sp):
            sp.dma_start(e["Y"][:, :], e["hidden"]).then_inc(x_in, 16)
            sp.dma_start(e["ident"][:, :], e["ident_in"]).then_inc(x_in, 16)
            sp.wait_ge(x_in, 32)
    layer_norm(nc, dict(DIM=e["DIM"], NW=e["NW"], x_ready=None), e["Y"], None, "start")


V_, TH, K_, A_, B_, Q_, AQ, BQ, EB = range(9)


def gates(nc, e):
    Y, hT, big, ident, MT, E, banks = (e[k] for k in ("Y", "hT", "big", "ident", "MT", "E", "banks"))
    B, WIN, DIM, D, NW, S, C, NC = (e[k] for k in ("B", "WIN", "DIM", "D", "NW", "S", "C", "NC"))
    H2 = S // 512
    with ExitStack() as ctx:
        def sb(name, shape, dt=F32):
            return ctx.enter_context(nc.sbuf_tensor(name, shape, dt))

        def sem(name):
            return nc.alloc_semaphore(name)

        pw = sb("pw", [P, 6, D])
        cl = sb("cl", [P, 18])
        mean = sb("mean", [P, P])
        sel = sb("sel", [P, B, C])
        PAD = 3
        cin = sb("cin", [P, 3, PAD + S])
        cacc = sb("cacc", [P, 2, S])
        sg = sb("sg", [P, 3, S])
        gm = sb("gm", [P, 3, S])
        inj = sb("inj", [P, 2, S])
        aM = sb("aM", [C, B, S])
        eM = sb("eM", [C, B, S])
        ab = sb("ab", [P, 512])
        ex = sb("ex", [P, 512])
        offset = sb("offset", [P, 3])
        s = {n: sem("g_" + n) for n in (
            "w_in pad t_mm t_ev p_mm p_ev m_mm m_ev v abs ex sp conv".split())}
        block = ctx.enter_context(nc.Block())
        ORDER = (3, 4, 5, 0, 1, 2)
        factor, added = (-0.1, 0.9, -0.1), (1.0, 0.05, 0.0)
        cw = lambda i, j: cl[:, 5 * i + j:5 * i + j + 1]

        @block.sync
        def _(sp):
            sp.dma_start(pw[:, :, :], e["proj"]).then_inc(s["w_in"], 16)
            sp.dma_start(cl[:, :], e["cols"]).then_inc(s["w_in"], 16)
            sp.dma_start(mean[:, :], e["mean_in"]).then_inc(s["w_in"], 16)

        @block.gpsimd
        def _(pool):
            pool.wait_ge(s["w_in"], 48)
            for b in range(B):
                pool.tensor_copy(sel[:, b, :].rearrange("p (r c) -> p r c", r=2),
                                 mean[:, b * WIN:(b + 1) * WIN].unsqueeze(1).to_broadcast([P, 2, WIN])).then_inc(s["pad"], 1)
            pool.memset(cin[:, :, 0:PAD], 0.0).then_inc(s["pad"], 1)
            pool.memset(inj[:, :, :], 0.0).then_inc(s["pad"], 1)
            pool.tensor_copy(MT[:, :, :].rearrange("p b (c t) -> p (b c) t", t=C),
                             ident[0:C, 0:C].unsqueeze(1).to_broadcast([C, B * NC, C])).then_inc(s["pad"], 1)
            for i in range(3):
                pool.memset(offset[:, i:i + 1], added[i]).then_inc(s["pad"], 1)

        @block.tensor
        def _(pe):
            for g in range(NW // 4):
                if g >= 2:
                    pe.wait_ge(s["t_ev"], g - 1)
                for j in range(4):
                    w = 4 * g + j
                    mm = pe.transpose(banks[g % 2][:, j * P:(j + 1) * P], Y[:, w * DIM:(w + 1) * DIM], ident[:, :])
                mm.then_inc(s["t_mm"], 1)
            pe.wait_ge(s["w_in"], 48)
            pe.wait_ge(s["t_ev"], NW // 4)
            n = 0
            for i in ORDER:
                for h in range(H2):
                    if n >= 3:
                        pe.wait_ge(s["p_ev"], n - 2)
                    for b in range(B):
                        mm = pe.matmul(banks[2 + n % 3][b * D:(b + 1) * D, :], pw[:, i, :],
                                       hT[:, h * (512 // WIN):(h + 1) * (512 // WIN), b * WIN:(b + 1) * WIN], start=True, stop=True)
                    mm.then_inc(s["p_mm"], 1)
                    n += 1
            pe.wait_ge(s["pad"], B)
            n = 0
            for i in range(3):
                pe.wait_ge(s["p_ev"], 2 * H2) if i < 2 else pe.wait_ge(s["sp"], H2)
                for h in range(H2):
                    if n >= 3:
                        pe.wait_ge(s["m_ev"], n - 2)
                    pe.matmul(banks[5 + n % 3][:, :], mean[:, :], sg[:, i, 512 * h:512 * h + 512],
                              start=True, stop=True).then_inc(s["m_mm"], 1)
                    n += 1
            for i in range(2):
                for b in range(B):
                    for h in range(H2):
                        pe.wait_ge(s["m_ev"], n - 2)
                        pe.matmul(banks[5 + n % 3][0:C, :], sel[:, b, :], sg[:, i, 512 * h:512 * h + 512],
                                  start=True, stop=True).then_inc(s["m_mm"], 1)
                        n += 1

        @block.scalar
        def _(act):
            act.preload_act_table_set(SIGMOID)
            act.wait_ge(s["w_in"], 48)
            n = 0
            for i in ORDER:
                if i == 5:
                    act.preload_act_table_set(LN_EXP)
                for h in range(H2):
                    src = banks[2 + n % 3][:, :]
                    hs = slice(512 * h, 512 * h + 512)
                    act.wait_ge(s["p_mm"], n + 1)
                    if i in (3, 4):
                        act.activation(sg[:, i - 3, hs], src, ACT.Sigmoid, bias=cl[:, 12 + i:13 + i]).then_inc(s["p_ev"], 1)
                    elif i == 5:
                        act.activation(sg[:, 2, hs], src, ACT.Identity, bias=cl[:, 17:18]).then_inc(s["p_ev"], 1)
                        act.wait_ge(s["p_ev"], n + 1)
                        if h:
                            act.wait_ge(s["ex"], 2 * h)
                        act.activation(ab[:, :], sg[:, 2, hs], ACT.Abs).then_inc(s["abs"], 1)
                        act.wait_ge(s["abs"], h + 1)
                        if h:
                            act.wait_ge(s["sp"], h)
                        act.activation(ex[:, :], ab[:, :], ACT.Exp, scale=-1.0).then_inc(s["ex"], 1)
                        act.wait_ge(s["ex"], 2 * h + 1)
                        act.activation(ex[:, :], ex[:, :], ACT.Ln, bias=1.0).then_inc(s["ex"], 1)
                    else:
                        act.activation(cin[:, i, PAD + 512 * h:PAD + 512 * h + 512], src, ACT.Copy).then_inc(s["p_ev"], 1)
                    n += 1
            n = 0
            act.wait_ge(s["pad"], B + 6)
            for i in range(3):
                for h in range(H2):
                    act.wait_ge(s["m_mm"], n + 1)
                    act.activation(gm[:, i, 512 * h:512 * h + 512], banks[5 + n % 3][:, :], ACT.Identity,
                                   bias=offset[:, i:i + 1], scale=factor[i]).then_inc(s["m_ev"], 1)
                    n += 1
            for i, dst in ((0, aM), (1, eM)):
                for b in range(B):
                    for h in range(H2):
                        act.wait_ge(s["m_mm"], n + 1)
                        act.activation(dst[:, b, 512 * h:512 * h + 512], banks[5 + n % 3][0:C, :], ACT.Identity,
                                       bias=offset[0:C, i:i + 1], scale=factor[i]).then_inc(s["m_ev"], 1)
                        n += 1

        @block.vector
        def _(dve):
            steps = [0]

            def link(ins):
                steps[0] += 1
                ins.then_inc(s["v"], 1)
                dve.wait_ge(s["v"], steps[0])

            for g in range(NW // 4):
                dve.wait_ge(s["t_mm"], g + 1)
                dve.tensor_copy(hT[:, 4 * g:4 * (g + 1), :].rearrange("p w n -> p (w n)"), banks[g % 2][:, :]).then_inc(s["t_ev"], 1)
            for h in range(H2):
                hs = slice(512 * h, 512 * h + 512)
                dve.wait_ge(s["ex"], 2 * h + 2)
                dve.scalar_tensor_tensor(out=sg[:, 2, hs], in0=sg[:, 2, hs], scalar=0.0, in1=ex[:, :],
                                         op0=ALU.max, op1=ALU.add).then_inc(s["sp"], 1)
            dve.wait_ge(s["p_ev"], 6 * H2)
            dve.wait_ge(s["pad"], B + 1)
            for i, item in ((0, K_), (1, V_), (2, Q_)):
                link(dve.tensor_scalar(cacc[:, 0, :], cin[:, i, 0:S], cw(i, 0), cw(i, 4), ALU.mult, ALU.add))
                for j in (1, 2, 3):
                    dst = big[:, item, :] if j == 3 else cacc[:, j % 2, :]
                    link(dve.scalar_tensor_tensor(out=dst, in0=cin[:, i, j:j + S], scalar=cw(i, j),
                                                  in1=cacc[:, (j + 1) % 2, :], op0=ALU.mult, op1=ALU.add))
            dve.wait_ge(s["m_ev"], H2 * (3 + 2 * B))
            dve.wait_ge(s["pad"], B + 3)
            starts = lambda t: t.rearrange("p (c t) -> p c t", t=C)[:, :, 0:1]
            for i in range(2):
                link(dve.tensor_copy(starts(inj[:, i, :]), starts(gm[:, i, :])))
                link(dve.memset(starts(gm[:, i, :]), 0.0))
            link(dve.memset(starts(aM[:, :, :].rearrange("p b t -> p (b t)")), 0.0))
            link(dve.memset(starts(eM[:, :, :].rearrange("p b t -> p (b t)")), 0.0))
            link(dve.tensor_tensor_scan(big[:, A_, :], gm[:, 0, :], inj[:, 0, :], 0.0, ALU.mult, ALU.add))
            link(dve.tensor_tensor_scan(big[:, EB, :], gm[:, 1, :], inj[:, 1, :], 0.0, ALU.mult, ALU.add))
            link(dve.tensor_tensor_scan(big[:, B_, :], gm[:, 0, :], big[:, EB, :], 0.0, ALU.mult, ALU.add))
            link(dve.tensor_copy(big[:, TH, :], gm[:, 2, :]))
            fl = lambda t: t.rearrange("p b t -> p (b t)")
            link(dve.tensor_tensor_scan(fl(E[:, :, :]), fl(eM[:, :, :]), fl(MT[:, :, :]), 0.0, ALU.mult, ALU.add))
            link(dve.tensor_tensor_scan(fl(MT[:, :, :]), fl(aM[:, :, :]), fl(E[:, :, :]), 0.0, ALU.mult, ALU.add))
            link(dve.tensor_tensor(big[:, AQ, :], big[:, Q_, :], big[:, A_, :], ALU.mult))
            link(dve.tensor_tensor(big[:, BQ, :], big[:, Q_, :], big[:, B_, :], ALU.mult))

    release(nc, s)


def release(nc, semaphores):
    nc.clear_and_free_semaphores(list(semaphores.values()))
    nc.all_engine_barrier()


def chunks(nc, ctx0, e):
    big, ident, MT, E, banks = (e[k] for k in ("big", "ident", "MT", "E", "banks"))
    B, WIN, DIM, D, NW, S, C, NC = (e[k] for k in ("B", "WIN", "DIM", "D", "NW", "S", "C", "NC"))
    RT = ctx0.enter_context(nc.sbuf_tensor("RT", [D, NW, P], F32))
    BD = B * D
    with ExitStack() as ctx:
        def sb(name, shape, dt=F32):
            return ctx.enter_context(nc.sbuf_tensor(name, shape, dt))

        def sem(name):
            return nc.alloc_semaphore(name)

        st_n = sb("st_n", [P, 5, C])
        zero = sb("zero", [D, 2, B, 7, C])
        mt = sb("mt", [C, 2, B, C])
        ee = sb("ee", [C, 2, B])
        nat = sb("nat", [C, 2, 5, BD])
        v02 = sb("v02", [C, BD])
        state = sb("state", [D, 2, 3, B, 2, D])
        sa = sb("sa", [D, 3, B, D])
        sbb = sb("sbb", [D, 3, B, D])
        sc = sb("sc", [D, 3, B, D])
        zz, ez, e1, sig, ds, dt1, dt2, dz = (sb(n, [C, BD]) for n in ("zz", "ez", "e1", "sig", "ds", "dt1", "dt2", "dz"))
        hh = sb("hh", [C, 2, BD])
        ev = sb("ev", [C, BD])
        hmT = sb("hmT", [D, 2, B, C])
        eT = sb("eT", [D, B, C])
        sqs = sb("sqs", [C, 4, BD])
        nr = sb("nr", [C, 4, B])
        pd = sb("pd", [C, 2, B])
        gn, gl, gf, ww = (sb(n, [C, B]) for n in ("gn", "gl", "gf", "ww"))
        wme = sb("wme", [C, B, 2])
        r1 = sb("r1", [C, B, 2, D])
        r2 = sb("r2", [C, B, 2, D])
        dzw = sb("dzw", [C, 2, BD])
        ew = sb("ew", [C, 2, BD])
        g1 = sb("g1", [C, B, C])
        g2 = sb("g2", [C, B, C])
        zq, eq, e1q, sgq = (sb(n, [C, BD]) for n in ("zq", "eq", "e1q", "sgq"))
        hq = sb("hq", [C, 3, BD])
        hqT = sb("hqT", [D, 3, B, C])
        names = ("momentum_cleared small_products_issued state_loaded features_loaded0 features_loaded1 "
                 "rows_staged mt_staged ee_staged tokens_transposed tokens_in_sbuf target_scaled z_made z_clamped "
                 "z_exp z_exp_plus_one sigmoid_ready hidden_ready slope_product slope_sum slope_ready "
                 "hidden_transposed hidden_t_in_sbuf prediction_made error_ready error_transposed error_t_in_sbuf "
                 "dhidden_made dz_ready hidden_squared keys_squared error_squared dz_squared norms_but_dz dz_norm "
                 "norm_products grad_norm_summed grad_norm_clamped grad_norm_logged grad_rnorm token_weights "
                 "weights_for_w weights_for_momentum dz_weighted error_weighted dz_for_queries error_for_queries "
                 "update_made decayed_w decayed_momentum_part state_base momentum_base w_updated momentum_updated "
                 "keys_by_queries keys_by_queries_weighted query_z_made query_z_clamped query_z_exp "
                 "query_z_exp_plus_one query_sigmoid query_hidden query_hidden_a query_hidden_b "
                 "query_hidden_transposed query_hidden_t_in_sbuf hidden_by_queries hidden_by_queries_weighted "
                 "read_made read_in_sbuf").split()
        s = {n: sem("c_" + n) for n in names}
        block = ctx.enter_context(nc.Block())
        b4 = lambda t: t.rearrange("p (b d) -> p b d", b=B)
        pN, pZ, pR, pT, pQ0, pQ1, pU0, pU1 = banks
        TAIL = NC - 2

        def drive(eng, body):
            body(-1, 1)
            body(0, 0)
            body(1, 1)
            with eng.Fori(2, TAIL, 2) as c:
                body(c, 0, True)
                body(c + 1, 1, True)
            for c in range(TAIL, NC + 1):
                body(c, c % 2)

        def wait(eng, name, c, loop=True):
            if loop or c >= 0:
                eng.wait_ge(s[name], c + 1)

        def settled(eng):
            eng.wait_ge(s["momentum_cleared"], 1)

        def here(c, loop):
            return loop or 0 <= c < NC

        @block.sync
        def _(sp):
            def body(c, par, loop=False):
                n = c + 1
                if not here(n, loop):
                    return
                wait(sp, "update_made", n - 2, loop)
                wait(sp, "query_z_made", n - 2, loop)
                wait(sp, "keys_by_queries", n - 2, loop)
                wait(sp, "momentum_base", n - 2, loop)
                for b in range(B):
                    sp.dma_start(zero[:, 1 - par, b, :, :], big[b * D:(b + 1) * D, K_:EB + 1, bass.ds(n * C, C)]
                                 ).then_inc(s["features_loaded%d" % (1 - par)], 16)
            drive(sp, body)

        @block.gpsimd
        def _(pool):
            pool.memset(state[:, 0, :, :, 1, :], 0.0).then_inc(s["momentum_cleared"], 1)

            def body(c, par, loop=False):
                n, R = c + 1, c - 1
                if here(n, loop):
                    wait(pool, "tokens_transposed", n - 1, loop)
                    pool.tensor_copy(st_n[:, :, :], big[:, 0:5, bass.ds(n * C, C)]).then_inc(s["rows_staged"], 1)
                if here(c, loop):
                    wait(pool, "tokens_in_sbuf", c)
                    wait(pool, "norms_but_dz", 2 * c - 1, loop)
                    pool.tensor_tensor(sqs[:, 3, :], nat[:, par, 2, :], nat[:, par, 2, :], ALU.mult).then_inc(s["keys_squared"], 1)
                    wait(pool, "hidden_ready", c)
                    wait(pool, "dz_ready", c - 1, loop)
                    pool.tensor_tensor(dt1[:, :], hh[:, par, :], sig[:, :], ALU.mult).then_inc(s["slope_product"], 1)
                    pool.tensor_tensor(dt2[:, :], hh[:, par, :], sig[:, :], ALU.add).then_inc(s["slope_sum"], 1)
                    wait(pool, "slope_product", c)
                    wait(pool, "slope_sum", c)
                    pool.tensor_tensor(ds[:, :], dt2[:, :], dt1[:, :], ALU.subtract).then_inc(s["slope_ready"], 1)
                    wait(pool, "norms_but_dz", 2 * c - 1, loop)
                    pool.tensor_tensor(sqs[:, 2, :], hh[:, par, :], hh[:, par, :], ALU.mult).then_inc(s["hidden_squared"], 1)
                    wait(pool, "error_ready", c)
                    pool.tensor_tensor(sqs[:, 0, :], ev[:, :], ev[:, :], ALU.mult).then_inc(s["error_squared"], 1)
                if here(R, loop):
                    wait(pool, "query_hidden", R)
                    wait(pool, "query_hidden_transposed", R - 1, loop)
                    pool.tensor_tensor(hq[:, 1, :], hq[:, 0, :], nat[:, 1 - par, 3, :], ALU.mult).then_inc(s["query_hidden_a"], 1)
                    pool.tensor_tensor(hq[:, 2, :], hq[:, 0, :], nat[:, 1 - par, 4, :], ALU.mult).then_inc(s["query_hidden_b"], 1)
                if here(c, loop):
                    wait(pool, "token_weights", c)
                    wait(pool, "query_z_made", c - 2, loop)
                    pool.tensor_tensor(b4(dzw[:, par, :]), b4(dz[:, :]), ww[:, :].unsqueeze(2).to_broadcast([C, B, D]), ALU.mult).then_inc(s["dz_for_queries"], 1)
                    wait(pool, "read_made", c - 2, loop)
                    pool.tensor_tensor(b4(ew[:, par, :]), b4(ev[:, :]), ww[:, :].unsqueeze(2).to_broadcast([C, B, D]), ALU.mult).then_inc(s["error_for_queries"], 1)
                if here(n, loop):
                    wait(pool, "hidden_by_queries_weighted", n - 2, loop)
                    pool.tensor_copy(mt[:, 1 - par, :, :], MT[:, :, bass.ds(n * C, C)]).then_inc(s["mt_staged"], 1)
                    wait(pool, "weights_for_momentum", n - 2, loop)
                    pool.tensor_copy(ee[:, 1 - par, :].unsqueeze(2), E[:, :, bass.ds(n * C + (C - 1), 1)]).then_inc(s["ee_staged"], 1)
            drive(pool, body)

        @block.tensor
        def _(pe):
            pe.wait_ge(s["momentum_cleared"], 1)
            pe.wait_ge(s["state_loaded"], 16 * 3 * B)
            ZK, ZA, ZB, ZQ, ZAQ, ZBQ, ZE = range(7)

            def nat_t(n, loop):
                wait(pe, "rows_staged", n)
                wait(pe, "tokens_in_sbuf", n - 1, loop)
                wait(pe, "dz_ready", n - 1, loop)
                pe.sem_inc(s["small_products_issued"], 1)
                for i in range(5):
                    out = pN[0:C, i * P:(i + 1) * P] if i < 4 else pZ[0:C, 384:512]
                    mm = pe.transpose(out, st_n[:, i, :], ident[:, :])
                mm.then_inc(s["tokens_transposed"], 1)

            def body(c, par, loop=False):
                R = c - 1
                rp = 1 - par
                if here(c, loop):
                    settled(pe)
                    wait(pe, "w_updated", c - 1, loop)
                    wait(pe, "tokens_in_sbuf", c)
                    pe.wait_ge(s["features_loaded%d" % par], (c // 2 + 1) * (16 * B))
                    wait(pe, "dz_ready", c - 1, loop)
                    for b in range(B):
                        mm = pe.matmul(pZ[0:C, b * D:(b + 1) * D], zero[:, par, b, ZK, :], state[:, par, 0, b, 0, :],
                                       start=True, stop=True)
                    mm.then_inc(s["z_made"], 1)
                if here(R, loop):
                    settled(pe)
                    wait(pe, "keys_by_queries_weighted", R)
                    wait(pe, "dz_for_queries", R)
                    wait(pe, "hidden_by_queries_weighted", R - 1, loop)
                    for b in range(B):
                        o = pR[0:C, 256 + b * D:256 + (b + 1) * D]
                        pe.matmul(o, zero[:, rp, b, ZAQ, :], state[:, rp, 0, b, 0, :], start=True, stop=False)
                        pe.matmul(o, zero[:, rp, b, ZBQ, :], state[:, rp, 0, b, 1, :], start=False, stop=False)
                        mm = pe.matmul(o, g1[:, b, :], dzw[:, rp, b * D:(b + 1) * D], start=False, stop=True)
                    mm.then_inc(s["query_z_made"], 1)
                if here(c, loop):
                    settled(pe)
                    wait(pe, "hidden_ready", c)
                    wait(pe, "error_t_in_sbuf", c - 1, loop)
                    for b in range(B):
                        mm = pe.transpose(pT[0:D, b * C:(b + 1) * C], hh[:, par, b * D:(b + 1) * D], ident[0:C, 0:C])
                    mm.then_inc(s["hidden_transposed"], 1)
                    settled(pe)
                    wait(pe, "hidden_t_in_sbuf", c)
                    wait(pe, "z_clamped", c)
                    for b in range(B):
                        mm = pe.matmul(pZ[0:C, BD + b * D:BD + (b + 1) * D], hmT[:, par, b, :], state[:, par, 1, b, 0, :],
                                       start=True, stop=True)
                    mm.then_inc(s["prediction_made"], 1)
                if here(c, loop):
                    settled(pe)
                    wait(pe, "error_ready", c)
                    wait(pe, "hidden_t_in_sbuf", c)
                    for b in range(B):
                        mm = pe.transpose(pT[0:D, B * C + b * C:B * C + (b + 1) * C], ev[:, b * D:(b + 1) * D], ident[0:C, 0:C])
                    mm.then_inc(s["error_transposed"], 1)
                    settled(pe)
                    wait(pe, "error_t_in_sbuf", c)
                    for b in range(B):
                        mm = pe.matmul(pZ[0:C, 2 * BD + b * D:2 * BD + (b + 1) * D], eT[:, b, :], state[:, par, 2, b, 0, :],
                                       start=True, stop=True)
                    mm.then_inc(s["dhidden_made"], 1)
                    settled(pe)
                    wait(pe, "momentum_updated", c - 1, loop)
                    for b in range(B):
                        mm = pe.matmul(pU1[0:C, 256 + b * C:256 + (b + 1) * C], zero[:, par, b, ZK, :], zero[:, par, b, ZQ, :],
                                       start=True, stop=True)
                    mm.then_inc(s["keys_by_queries"], 1)
                if here(R, loop):
                    wait(pe, "query_hidden_a", R)
                    wait(pe, "query_hidden_b", R)
                    wait(pe, "query_hidden", R)
                    wait(pe, "read_in_sbuf", R - 1, loop)
                    pe.sem_inc(s["small_products_issued"], 1)
                    for i in range(3):
                        for b in range(B):
                            bank = (pQ0, pQ1)[i // 2]
                            o = (i % 2) * B * C + b * C
                            mm = pe.transpose(bank[0:D, o:o + C], hq[:, i, b * D:(b + 1) * D], ident[0:C, 0:C])
                    mm.then_inc(s["query_hidden_transposed"], 1)
                if here(c + 1, loop):
                    nat_t(c + 1, loop)
                if here(R, loop):
                    settled(pe)
                    wait(pe, "query_hidden_t_in_sbuf", 2 * R + 1)
                    wait(pe, "query_z_clamped", R)
                    for b in range(B):
                        mm = pe.matmul(pR[0:C, b * C:(b + 1) * C], hmT[:, rp, b, :], hqT[:, 0, b, :], start=True, stop=True)
                    mm.then_inc(s["hidden_by_queries"], 1)
                if here(c, loop):
                    settled(pe)
                    wait(pe, "dz_weighted", c)
                    wait(pe, "error_weighted", c)
                    wait(pe, "keys_by_queries_weighted", c)
                    for b in range(B):
                        d = slice(b * D, (b + 1) * D)
                        o = b * 2 * D
                        pe.matmul(pU0[0:D, o:o + 2 * D], nat[:, par, 2, d], r1[:, b, :, :].rearrange("p a d -> p (a d)"),
                                  start=True, stop=True)
                        pe.matmul(pU0[0:D, 256 + o:256 + o + 2 * D], hh[:, par, d], r2[:, b, :, :].rearrange("p a d -> p (a d)"),
                                  start=True, stop=True)
                        pe.matmul(pU1[0:D, o:o + D], r2[:, b, 0, :], hh[:, par, d], start=True, stop=True)
                        mm = pe.matmul(pU1[0:D, o + D:o + 2 * D], r2[:, b, 1, :], hh[:, par, d], start=True, stop=True)
                    mm.then_inc(s["update_made"], 1)
                if here(R, loop):
                    settled(pe)
                    wait(pe, "hidden_by_queries_weighted", R)
                    wait(pe, "error_for_queries", R)
                    for b in range(B):
                        o = pQ1[0:D, B * C + b * C:B * C + (b + 1) * C]
                        pe.matmul(o, state[:, rp, 1, b, 0, :], hqT[:, 1, b, :], start=True, stop=False)
                        pe.matmul(o, state[:, rp, 1, b, 1, :], hqT[:, 2, b, :], start=False, stop=False)
                        mm = pe.matmul(o, ew[:, rp, b * D:(b + 1) * D], g2[:, b, :], start=False, stop=True)
                    mm.then_inc(s["read_made"], 1)

            drive(pe, body)

        @block.scalar
        def _(act):
            for m, src in ((0, e["mW1T"]), (1, e["mW2T"]), (2, e["mW2"])):
                for b in range(B):
                    act.dma_start(state[:, 0, m, b, 0, :], src).then_inc(s["state_loaded"], 16)
            act.preload_act_table_set(LN_EXP)

            def body(c, par, loop=False):
                R, n = c - 1, c + 1
                if here(c, loop):
                    wait(act, "z_clamped", c)
                    wait(act, "z_exp_plus_one", c - 1, loop)
                    act.activation(ez[:, :], zz[:, :], ACT.Exp, scale=-1.0).then_inc(s["z_exp"], 1)
                if here(R, loop):
                    wait(act, "query_z_clamped", R)
                    wait(act, "query_z_exp_plus_one", R - 1, loop)
                    act.activation(eq[:, :], zq[:, :], ACT.Exp, scale=-1.0).then_inc(s["query_z_exp"], 1)
                if here(c, loop):
                    wait(act, "hidden_transposed", c)
                    wait(act, "hidden_by_queries", c - 2, loop)
                    act.activation(hmT[:, par, :, :].rearrange("p b t -> p (b t)"), pT[0:D, 0:B * C], ACT.Copy).then_inc(s["hidden_t_in_sbuf"], 1)
                    wait(act, "error_transposed", c)
                    wait(act, "dhidden_made", c - 1, loop)
                    act.activation(eT[:, :, :].rearrange("p b t -> p (b t)"), pT[0:D, B * C:2 * B * C], ACT.Copy).then_inc(s["error_t_in_sbuf"], 1)
                if here(c, loop):
                    wait(act, "grad_norm_clamped", c)
                    act.activation(gl[:, :], gn[:, :], ACT.Ln).then_inc(s["grad_norm_logged"], 1)
                    wait(act, "grad_norm_logged", c)
                    wait(act, "token_weights", c - 1, loop)
                    act.activation(gf[:, :], gl[:, :], ACT.Exp, scale=-0.5).then_inc(s["grad_rnorm"], 1)
                if here(R, loop):
                    wait(act, "query_hidden_transposed", R)
                    wait(act, "read_made", R - 1, loop)
                    hf = hqT[:, :, :, :].rearrange("p i b t -> p (i b t)")
                    act.activation(hf[:, 0:512], pQ0[0:D, :], ACT.Copy).then_inc(s["query_hidden_t_in_sbuf"], 1)
                    act.activation(hf[:, 512:768], pQ1[0:D, 0:256], ACT.Copy).then_inc(s["query_hidden_t_in_sbuf"], 1)
                if here(n, loop):
                    wait(act, "tokens_transposed", n)
                    for q in ("keys_squared", "target_scaled", "token_weights", "update_made"):
                        wait(act, q, n - 2, loop)
                    for q in ("query_hidden_a", "query_hidden_b"):
                        wait(act, q, n - 2, loop)
                    act.activation(nat[:, 1 - par, 0:4, :].rearrange("p i d -> p (i d)"), pN[0:C, :], ACT.Copy)
                    act.activation(nat[:, 1 - par, 4, :], pZ[0:C, 384:512], ACT.Copy).then_inc(s["tokens_in_sbuf"], 1)
                if here(R, loop):
                    wait(act, "read_made", R)
                    act.activation(RT[:, bass.ds(R * (C // WIN), C // WIN), :].rearrange("p w (b i) -> p w b i", b=B),
                                   pQ1[0:D, B * C:2 * B * C].rearrange("p (b w i) -> p w b i", b=B, i=WIN), ACT.Copy).then_inc(s["read_in_sbuf"], 1)

            drive(act, body)

        @block.vector
        def _(dve):
            def body(c, par, loop=False):
                R = c - 1
                rp = 1 - par
                TT = dve.tensor_tensor
                if here(c, loop):
                    wait(dve, "z_made", c)
                    wait(dve, "hidden_ready", c - 1, loop)
                    dve.tensor_scalar(zz[:, :], pZ[0:C, 0:BD], -80.0, None, ALU.max).then_inc(s["z_clamped"], 1)
                    wait(dve, "tokens_in_sbuf", c)
                    wait(dve, "error_ready", c - 1, loop)
                    dve.tensor_scalar(v02[:, :], nat[:, par, 0, :], 0.2, None, ALU.mult).then_inc(s["target_scaled"], 1)
                    wait(dve, "z_exp", c)
                    wait(dve, "sigmoid_ready", c - 1, loop)
                    dve.tensor_scalar(e1[:, :], ez[:, :], 1.0, None, ALU.add).then_inc(s["z_exp_plus_one"], 1)
                    wait(dve, "z_exp_plus_one", c)
                    wait(dve, "slope_sum", c - 1, loop)
                    wait(dve, "slope_product", c - 1, loop)
                    dve.reciprocal(sig[:, :], e1[:, :]).then_inc(s["sigmoid_ready"], 1)
                    wait(dve, "sigmoid_ready", c)
                    wait(dve, "update_made", c - 2, loop)
                    wait(dve, "hidden_squared", c - 2, loop)
                    TT(hh[:, par, :], zz[:, :], sig[:, :], ALU.mult).then_inc(s["hidden_ready"], 1)
                if here(R, loop):
                    wait(dve, "query_z_made", R)
                    wait(dve, "query_hidden", R - 1, loop)
                    dve.tensor_scalar(zq[:, :], pR[0:C, 256:256 + BD], -80.0, None, ALU.max).then_inc(s["query_z_clamped"], 1)
                if here(c, loop):
                    W = lambda k: state[:, par, :, :, k, :]
                    last = lambda i: zero[:, par, :, i, C - 1].unsqueeze(1).unsqueeze(3).to_broadcast([D, 3, B, D])
                    wait(dve, "w_updated", c - 1, loop)
                    wait(dve, "momentum_updated", c - 1, loop)
                    TT(sa[:, :, :, :], W(0), last(1), ALU.mult).then_inc(s["decayed_w"], 1)
                if here(R, loop):
                    wait(dve, "query_z_exp", R)
                    wait(dve, "query_sigmoid", R - 1, loop)
                    dve.tensor_scalar(e1q[:, :], eq[:, :], 1.0, None, ALU.add).then_inc(s["query_z_exp_plus_one"], 1)
                    wait(dve, "query_z_exp_plus_one", R)
                    dve.reciprocal(sgq[:, :], e1q[:, :]).then_inc(s["query_sigmoid"], 1)
                if here(c, loop):
                    wait(dve, "prediction_made", c)
                    wait(dve, "target_scaled", c)
                    wait(dve, "error_for_queries", c - 1, loop)
                    wait(dve, "error_transposed", c - 1, loop)
                    wait(dve, "error_weighted", c - 1, loop)
                    dve.scalar_tensor_tensor(out=ev[:, :], in0=pZ[0:C, BD:2 * BD], scalar=0.2, in1=v02[:, :],
                                             op0=ALU.mult, op1=ALU.subtract).then_inc(s["error_ready"], 1)
                if here(R, loop):
                    wait(dve, "query_sigmoid", R)
                    wait(dve, "query_hidden_transposed", R - 1, loop)
                    wait(dve, "query_hidden_a", R - 1, loop)
                    wait(dve, "query_hidden_b", R - 1, loop)
                    TT(hq[:, 0, :], zq[:, :], sgq[:, :], ALU.mult).then_inc(s["query_hidden"], 1)
                if here(c, loop):
                    TT(sbb[:, :, :, :], W(1), last(2), ALU.mult).then_inc(s["decayed_momentum_part"], 1)
                    TT(sc[:, :, :, :], W(1), last(6), ALU.mult).then_inc(s["momentum_base"], 1)
                    wait(dve, "decayed_w", c)
                    wait(dve, "decayed_momentum_part", c)
                    TT(sa[:, :, :, :], sa[:, :, :, :], sbb[:, :, :, :], ALU.add).then_inc(s["state_base"], 1)
                    wait(dve, "hidden_squared", c)
                    wait(dve, "keys_squared", c)
                    wait(dve, "error_squared", c)
                    wait(dve, "norm_products", c - 1, loop)
                    dve.tensor_reduce(nr[:, 2:4, :], sqs[:, 2:4, :].rearrange("p k (b d) -> p k b d", b=B), AX.X, ALU.add).then_inc(s["norms_but_dz"], 1)
                    dve.tensor_reduce(nr[:, 0, :], b4(sqs[:, 0, :]), AX.X, ALU.add).then_inc(s["norms_but_dz"], 1)
                    wait(dve, "dhidden_made", c)
                    wait(dve, "slope_ready", c)
                    wait(dve, "dz_for_queries", c - 1, loop)
                    TT(dz[:, :], pZ[0:C, 2 * BD:3 * BD], ds[:, :], ALU.mult).then_inc(s["dz_ready"], 1)
                    wait(dve, "dz_ready", c)
                    TT(sqs[:, 1, :], dz[:, :], dz[:, :], ALU.mult).then_inc(s["dz_squared"], 1)
                    wait(dve, "dz_squared", c)
                    dve.tensor_reduce(nr[:, 1, :], b4(sqs[:, 1, :]), AX.X, ALU.add).then_inc(s["dz_norm"], 1)
                    wait(dve, "dz_norm", c)
                    wait(dve, "norms_but_dz", 2 * c + 1)
                    TT(pd[:, :, :], nr[:, 0:2, :], nr[:, 2:4, :], ALU.mult).then_inc(s["norm_products"], 1)
                    wait(dve, "norm_products", c)
                    wait(dve, "grad_norm_logged", c - 1, loop)
                    TT(gn[:, :], pd[:, 0, :], pd[:, 1, :], ALU.add).then_inc(s["grad_norm_summed"], 1)
                    wait(dve, "grad_norm_summed", c)
                    dve.tensor_scalar(gn[:, :], gn[:, :], 1e-12, None, ALU.max).then_inc(s["grad_norm_clamped"], 1)
                if here(c, loop):
                    wait(dve, "grad_rnorm", c)
                    wait(dve, "dz_for_queries", c - 1, loop)
                    wait(dve, "error_for_queries", c - 1, loop)
                    dve.scalar_tensor_tensor(out=ww[:, :], in0=gf[:, :], scalar=1.0, in1=b4(nat[:, par, 1, :])[:, :, 0],
                                             op0=ALU.min, op1=ALU.mult).then_inc(s["token_weights"], 1)
                    wait(dve, "token_weights", c)
                    wait(dve, "mt_staged", c)
                    wait(dve, "ee_staged", c)
                    wait(dve, "dz_weighted", c - 1, loop)
                    wait(dve, "error_weighted", c - 1, loop)
                    TT(wme[:, :, 0], ww[:, :], mt[:, par, :, C - 1], ALU.mult).then_inc(s["weights_for_w"], 1)
                    TT(wme[:, :, 1], ww[:, :], ee[:, par, :], ALU.mult).then_inc(s["weights_for_momentum"], 1)
                    wait(dve, "weights_for_w", c)
                    wait(dve, "weights_for_momentum", c)
                    wait(dve, "update_made", c - 1, loop)
                    ws = wme[:, :, :].unsqueeze(3).to_broadcast([C, B, 2, D])
                    TT(r1[:, :, :, :], b4(dz[:, :]).unsqueeze(2).to_broadcast([C, B, 2, D]), ws, ALU.mult).then_inc(s["dz_weighted"], 1)
                    TT(r2[:, :, :, :], b4(ev[:, :]).unsqueeze(2).to_broadcast([C, B, 2, D]), ws, ALU.mult).then_inc(s["error_weighted"], 1)
                if here(c, loop):
                    wait(dve, "keys_by_queries", c)
                    wait(dve, "mt_staged", c)
                    wait(dve, "query_z_made", c - 1, loop)
                    TT(g1[:, :, :], pU1[0:C, 256:512].rearrange("p (b t) -> p b t", b=B), mt[:, par, :, :], ALU.mult).then_inc(s["keys_by_queries_weighted"], 1)
                if here(R, loop):
                    wait(dve, "hidden_by_queries", R)
                    wait(dve, "read_made", R - 1, loop)
                    TT(g2[:, :, :], pR[0:C, 0:B * C].rearrange("p (b t) -> p b t", b=B), mt[:, rp, :, :], ALU.mult).then_inc(s["hidden_by_queries_weighted"], 1)
                if here(c, loop):
                    wait(dve, "update_made", c)
                    wait(dve, "state_base", c)
                    wait(dve, "momentum_base", c)
                    for k, base in ((0, sa), (1, sc)):
                        mm = TT(state[:, 1 - par, 0, :, k, :], base[:, 0, :, :],
                                pU0[0:D, 0:256].rearrange("p (b k d) -> p b k d", b=B, k=2)[:, :, k, :], ALU.add)
                    mm.then_inc(s["w_updated"], 1)
                    wait(dve, "read_made", c - 1, loop)
                    for k, base in ((0, sa), (1, sc)):
                        TT(state[:, 1 - par, 1, :, k, :], base[:, 1, :, :],
                           pU0[0:D, 256:512].rearrange("p (b k d) -> p b k d", b=B, k=2)[:, :, k, :], ALU.add)
                        mm = TT(state[:, 1 - par, 2, :, k, :], base[:, 2, :, :],
                                pU1[0:D, 0:256].rearrange("p (b k d) -> p b k d", b=B, k=2)[:, :, k, :], ALU.add)
                    mm.then_inc(s["momentum_updated"], 1)

            drive(dve, body)
    release(nc, s)
    return RT


def output(nc, e):
    Y, hT, banks, RT = e["Y"], e["hT"], e["banks"], e["RT"]
    B, WIN, DIM, D, NW, S = (e[k] for k in ("B", "WIN", "DIM", "D", "NW", "S"))
    G = 4
    GROUPS = NW // G
    N = G * DIM
    with ExitStack() as ctx:
        def sb(name, shape, dt=F32):
            return ctx.enter_context(nc.sbuf_tensor(name, shape, dt))

        def sem(name):
            return nc.alloc_semaphore(name)

        woT = sb("woT", [D, DIM])
        gwT = sb("gwT", [P, DIM])
        ng = sb("ng", [P, DIM])
        gbb = sb("gbb", [P, DIM])
        osq = sb("osq", [P, 2, N])
        ms = sb("ms", [P, GROUPS, G])
        lm = sb("lm", [P, GROUPS, G])
        rm = sb("rm", [P, GROUPS, G])
        on = sb("on", [P, 2, N])
        ga = sb("ga", [P, 2, N])
        ep = sb("ep6", [P, 1])
        s = {n: sem("o_" + n) for n in "w_in ep o_mm g_mm sq ms lm rm on on2 ga ga2 y".split()}
        block = ctx.enter_context(nc.Block())
        w3 = lambda t: t.rearrange("p (w n) -> p w n", n=DIM)
        bc = lambda t: t[:, :].unsqueeze(1).to_broadcast([P, G, DIM])

        @block.sync
        def _(sp):
            sp.dma_start(woT[:, :], e["WoT"]).then_inc(s["w_in"], 16)
            sp.dma_start(gwT[:, :], e["gWT"]).then_inc(s["w_in"], 16)
            sp.dma_start(ng[:, :], e["norm_g"].unsqueeze(0).to_broadcast([P, DIM])).then_inc(s["w_in"], 16)
            sp.dma_start(gbb[:, :], e["gb"].unsqueeze(0).to_broadcast([P, DIM])).then_inc(s["w_in"], 16)

        @block.tensor
        def _(pe):
            pe.wait_ge(s["w_in"], 64)
            for g in range(GROUPS):
                if g >= 2:
                    pe.wait_ge(s["on"], g - 1)
                for j in range(G):
                    w = G * g + j
                    mm = pe.matmul(banks[g % 2][:, j * DIM:(j + 1) * DIM], RT[:, w, :], woT[:, :], start=True, stop=True)
                mm.then_inc(s["o_mm"], 1)
                if g >= 2:
                    pe.wait_ge(s["ga"], g - 1)
                for j in range(G):
                    w = G * g + j
                    mm = pe.matmul(banks[2 + g % 2][:, j * DIM:(j + 1) * DIM], hT[:, w, :], gwT[:, :], start=True, stop=True)
                mm.then_inc(s["g_mm"], 1)

        @block.scalar
        def _(act):
            act.preload_act_table_set(LN_EXP)
            act.wait_ge(s["ep"], 1)
            for g in range(GROUPS):
                act.wait_ge(s["o_mm"], g + 1)
                if g >= 2:
                    act.wait_ge(s["ms"], g - 1)
                act.activation(osq[:, g % 2, :], banks[g % 2][:, :], ACT.Square).then_inc(s["sq"], 1)
                act.wait_ge(s["ms"], g + 1)
                act.activation(lm[:, g, :], ms[:, g, :], ACT.Ln, bias=ep[:, 0:1], scale=1.0 / DIM).then_inc(s["lm"], 1)
                act.wait_ge(s["lm"], g + 1)
                act.activation(rm[:, g, :], lm[:, g, :], ACT.Exp, scale=-0.5).then_inc(s["rm"], 1)

        @block.vector
        def _(dve):
            dve.memset(ep[:, :], 1e-6).then_inc(s["ep"], 1)
            dve.wait_ge(s["w_in"], 64)
            for g in range(GROUPS):
                r = g % 2
                dve.wait_ge(s["sq"], g + 1)
                dve.tensor_reduce(ms[:, g, :], w3(osq[:, r, :]), AX.X, ALU.add).then_inc(s["ms"], 1)
                if g >= 2:
                    dve.wait_ge(s["y"], g - 1)
                dve.wait_ge(s["g_mm"], g + 1)
                dve.tensor_tensor(w3(ga[:, r, :]), w3(banks[2 + r][:, :]), bc(gbb), ALU.add).then_inc(s["ga"], 1)
                dve.wait_ge(s["ga"], g + 1)
                dve.tensor_tensor(w3(ga[:, r, :]), w3(ga[:, r, :]), bc(ng), ALU.mult).then_inc(s["ga2"], 1)
                dve.wait_ge(s["rm"], g + 1)
                dve.tensor_tensor(w3(on[:, r, :]), w3(banks[r][:, :]), rm[:, g, :].unsqueeze(2).to_broadcast([P, G, DIM]),
                                  ALU.mult).then_inc(s["on"], 1)
                dve.wait_ge(s["ga2"], g + 1)
                dve.wait_ge(s["on"], g + 1)
                dve.tensor_tensor(Y[:, g * N:(g + 1) * N], ga[:, r, :], on[:, r, :], ALU.mult).then_inc(s["y"], 1)

def network(nc, hidden, proj, cols, mW1T, mW2T, mW2, WoT, gWT, norm_g, gb, Wqkv, q_scale, k_scale, Wo, ln_g, ln_b,
            W1, b1, W2, b2, rotary, masks, ident_in, center_in, mean_in, out):
    x_mid = nc.dram_tensor("x_mid", hidden.shape, F32, kind="Internal").ap()
    memory(nc, hidden, proj, cols, mW1T, mW2T, mW2, WoT, gWT, norm_g, gb, mean_in, ident_in, x_mid)
    transformer(nc, x_mid, Wqkv, q_scale, k_scale, Wo, ln_g, ln_b, W1, b1, W2, b2, rotary, masks, ident_in, center_in, out,
                DEPTH=Wqkv.shape[0])


def shape_constants(tokens, window, head_dim, batches):
    half = np.arange(0, head_dim, 2, dtype=np.float32)
    inv_freq = (1.0 / 10000.0 ** (half / head_dim)).astype(np.float32)
    t = np.arange(tokens, dtype=np.float32)
    freqs = t[:, None] * inv_freq[None, :]
    base = ((half + 0.4 * head_dim) / (1.4 * head_dim)).astype(np.float32)
    power = ((t - tokens // 2) / (window // 2)).astype(np.float32)
    scale = (base[None, :] ** power[:, None]).astype(np.float32)
    inv = np.float32(1.0) / scale
    tables = np.stack([np.cos(freqs) * scale, np.sin(freqs) * scale, np.cos(freqs) * inv, np.sin(freqs) * inv], 1)
    tables = tables.astype(np.float32).reshape(tokens // window, window, 2 * head_dim).transpose(1, 0, 2)
    tables = np.broadcast_to(tables[None], (batches,) + tables.shape).reshape(batches * window, -1)
    i, j = np.arange(window)[:, None], np.arange(window)[None, :]
    own = np.where(i < j, -1e30, 0.0)
    prev = np.where(i > j, -1e30, 0.0)
    none = np.full((window, window), -1e30)
    masks = np.stack([np.concatenate(pair, 1) for pair in ((own, none), (own, prev), (prev, own))], 1)
    masks = np.broadcast_to(masks[None], (batches,) + masks.shape).reshape(batches * window, 3, 2 * window)
    eye = np.eye(batches * window, dtype=np.float32)
    return dict(rotary=tables, masks=masks.astype(np.float32), ident_in=eye,
                center_in=eye - np.float32(1.0 / (batches * window)),
                mean_in=np.kron(np.eye(batches), np.full((window, window), 1.0 / window)).astype(np.float32))


def kernel(**inputs):
    import concourse.bacc as _bacc
    from concourse.bass_utils import run_bass_kernel_spmd as _run

    attn = lambda name: np.asarray(inputs["L0_attn_" + name])
    ffn = lambda name: np.asarray(inputs["L0_ffn_" + name])
    hidden = attn("hidden")
    batches, tokens, dim = hidden.shape
    window = P // batches
    windows = tokens // window
    arrays = dict(
        hidden=hidden.reshape(batches, windows, window, dim).transpose(0, 2, 1, 3).reshape(P, windows * dim),
        proj=np.stack([attn(n).T for n in ("Wk", "Wv", "Wq", "aW", "eW", "tW")], 1),
        cols=np.tile(np.concatenate([np.concatenate([attn(w), attn(b)[:, None]], 1)
                                     for w, b in (("ckw", "ckb"), ("cvw", "cvb"), ("cqw", "cqb"))]
                                    + [attn(n)[:, None] for n in ("ab", "eb", "tb")], 1), (batches, 1)),
        mW1T=attn("mW1").T, mW2T=attn("mW2").T, mW2=attn("mW2"), WoT=attn("Wo").T, gWT=attn("gW").T,
        norm_g=attn("norm_g"), gb=attn("gb"),
        Wqkv=ffn("Wqkv"), q_scale=ffn("q_scale"), k_scale=ffn("k_scale"), Wo=ffn("Wo"),
        ln_g=ffn("ln_g").T, ln_b=ffn("ln_b").T, W1=ffn("W1"), b1=ffn("b1"), W2=ffn("W2"), b2=ffn("b2"),
        **shape_constants(tokens, window, inputs["L0_ffn_q_scale"].shape[1], batches))
    nc = _bacc.Bacc("TRN2", target_bir_lowering=False, num_devices=1)
    feeds, aps = {}, {}
    for name, a in arrays.items():
        a = np.ascontiguousarray(a)
        feeds["in_" + name] = a
        aps[name] = nc.dram_tensor("in_" + name, a.shape, mybir.dt.from_np(a.dtype), kind="ExternalInput").ap()
    out = nc.dram_tensor("stream_out", (P, windows * dim), F32, kind="ExternalOutput").ap()
    network(nc, out=out, **aps)
    result = _run(nc, [feeds], core_ids=[0]).results[0]["stream_out"]
    return result.reshape(batches, window, windows, dim).transpose(0, 2, 1, 3).reshape(batches, tokens, dim)
```

```python
from contextlib import ExitStack

import numpy as np

import concourse.bass as bass
from concourse import mybir

ALU = mybir.AluOpType
ACT = mybir.ActivationFunctionType
AX = mybir.AxisListType
F32 = mybir.dt.float32
BF16 = mybir.dt.bfloat16

P = 128
LN_EXP = "natural_log_exp_and_others"
SIGMOID = "sigmoid_and_others"


def transformer(nc, x_mid, Wqkv, q_scale, k_scale, Wo, ln_g, ln_b, W1, b1, W2, b2,
                rotary, masks, ident_in, center_in, out, DEPTH=6):
    DIM = Wqkv.shape[1]
    INNER = Wo.shape[1]
    DH = q_scale.shape[1]
    HEADS = INNER // DH
    PAIRS = HEADS // 2
    HALF = DH // 2
    B = 4
    WIN = P // B
    NW = x_mid.shape[1] // DIM
    HID = W2.shape[1]
    HC = -(-HID // P)
    LAYERS = DEPTH
    TILES = LAYERS * NW
    QKS = 8.0
    LOG2_SHIFT = 20
    assert DIM == P and HEADS == 16 and DH == 64 and WIN == 32

    with ExitStack() as ctx:
        def sb(name, shape, dt=F32):
            return ctx.enter_context(nc.sbuf_tensor(name, shape, dt))

        def sem(name):
            return nc.alloc_semaphore(name)

        X = sb("X", [P, NW * DIM])
        tab = sb("tab", [P, NW * 4 * HALF])
        wqkv = sb("wqkv", [P, 2, 3 * INNER])
        wo = sb("wo", [P, 2, PAIRS * DIM])
        w1 = sb("w1", [P, LAYERS, 2 * HID])
        b1b = sb("b1b", [P, LAYERS, 2 * HID])
        w2 = sb("w2", [P, LAYERS, HC * DIM])
        b2b = sb("b2b", [P, LAYERS, DIM])
        qks = sb("qks", [P, LAYERS, 4 * DH])
        ident = sb("ident", [P, P])
        center = sb("center", [P, P])
        identb = sb("identb", [P, P], BF16)
        maskb = sb("maskb", [P, 3 * PAIRS * 2 * WIN], BF16)
        first = sb("first", [P, NW])

        R0 = ctx.enter_context(nc.psum_tensor("R0", [P, 1024], F32))
        R1 = ctx.enter_context(nc.psum_tensor("R1", [P, 1024], F32))
        R2 = ctx.enter_context(nc.psum_tensor("R2", [P, 1024], F32))
        b6 = ctx.enter_context(nc.psum_tensor("b6", [P, 512], F32))
        b7 = ctx.enter_context(nc.psum_tensor("b7", [P, 512], F32))

        wqkv_in = sem("wqkv_in")
        wo_in = sem("wo_in")
        x_ready = sem("x_ready")
        prep(nc, ctx, locals())
        stream(nc, ctx, locals())
        finish(nc, ctx, locals())


def prep(nc, ctx0, e):
    (X, tab, wqkv, wo, w1, b1b, w2, b2b, qks, ident, center, identb, maskb, first, R0, R1) = (e[k] for k in (
        "X", "tab", "wqkv", "wo", "w1", "b1b", "w2", "b2b", "qks", "ident", "center", "identb", "maskb", "first", "R0", "R1"))
    DIM, DH, HALF, NW, HID, HC, LAYERS, PAIRS, WIN = (e[k] for k in ("DIM", "DH", "HALF", "NW", "HID", "HC", "LAYERS", "PAIRS", "WIN"))
    G = 4
    GROUPS = NW // G
    with ExitStack() as ctx:
        def sb(name, shape, dt=F32):
            return ctx.enter_context(nc.sbuf_tensor(name, shape, dt))

        def sem(name):
            return nc.alloc_semaphore(name)

        w1r = sb("w1r", [P, LAYERS, 2 * HID])
        lng = sb("lng", [P, LAYERS])
        lnb = sb("lnb", [P, LAYERS])
        ones = sb("ones", [P, P])
        brep = sb("brep", [P, LAYERS, P])
        maskf = sb("maskf", [P, 3, 2 * WIN])
        m_in = sem("m_in"); s_in = sem("s_in"); x_in = sem("x_in"); w1_in = sem("w1_in")
        v = sem("v_step"); w1_mm = sem("w1_mm"); b1_mm = sem("b1_mm"); w1_ev = sem("w1_ev"); pad_done = sem("pad_done")
        w1g_ready = sem("w1g_ready"); brep_ready = sem("brep_ready")
        wi, wo_s = e["wqkv_in"], e["wo_in"]
        loads(nc, e, dict(w1r=w1r, lng=lng, lnb=lnb, maskf=maskf, x_in=x_in, s_in=s_in, w1_in=w1_in, m_in=m_in, pad_done=pad_done))
        layer_norm(nc, e, X, None, "mid")
        block = ctx.enter_context(nc.Block())

        @block.tensor
        def _(pe):
            pe.wait_ge(s_in, 16 * 7)
            for l in range(LAYERS):
                pe.wait_ge(brep_ready, l + 1)
                if l == 0:
                    pe.wait_ge(w1_in, 16 * LAYERS)
                if l >= 1:
                    pe.wait_ge(w1_ev, 2 * l - 1)
                for h in range(2):
                    mm = pe.matmul(R0[:, 512 * h:512 * h + HID], brep[:, l, :], w1r[:, l, h * HID:(h + 1) * HID],
                                   start=True, stop=True)
                mm.then_inc(b1_mm, 1)
                pe.wait_ge(w1g_ready, l + 1)
                if l >= 1:
                    pe.wait_ge(w1_ev, 2 * l)
                for h in range(2):
                    mm = pe.matmul(R1[:, 512 * h:512 * h + HID], center[:, :], w1[:, l, h * HID:(h + 1) * HID],
                                   start=True, stop=True)
                mm.then_inc(w1_mm, 1)

        @block.vector
        def _(dve):
            steps = [0]

            def link(ins):
                steps[0] += 1
                ins.then_inc(v, 1)
                dve.wait_ge(v, steps[0])

            dve.memset(ones[:, :], 1.0).then_inc(v, 1)
            dve.memset(first[:, :], 1.0).then_inc(v, 1)
            steps[0] = 2
            dve.wait_ge(v, 2)
            link(dve.memset(first[:, 0:1], 0.0))
            dve.wait_ge(s_in, 16 * 7)
            link(dve.tensor_copy(identb[:, :], ident[:, :]))
            link(dve.tensor_copy(maskb[:, :].rearrange("p (m c k) -> p m c k", m=3, c=PAIRS),
                                 maskf[:, :, :].unsqueeze(2).to_broadcast([P, 3, PAIRS, 2 * WIN])))
            for l in range(LAYERS):
                dve.tensor_scalar(brep[:, l, :], ones[:, :], lnb[:, l:l + 1], None, ALU.mult).then_inc(brep_ready, 1)
            for l in range(LAYERS):
                if l == 0:
                    dve.wait_ge(w1_in, 16 * LAYERS)
                dve.tensor_scalar(w1[:, l, :], w1r[:, l, :], lng[:, l:l + 1], None, ALU.mult).then_inc(w1g_ready, 1)
            for l in range(LAYERS):
                dve.wait_ge(b1_mm, l + 1)
                bv = b1b[:, l, :].rearrange("p (h n) -> p h n", h=2)
                dve.tensor_tensor(bv, R0[:, :].rearrange("p (h n) -> p h n", h=2)[:, :, 0:HID], bv, ALU.add).then_inc(w1_ev, 1)
                dve.wait_ge(w1_mm, l + 1)
                dve.tensor_copy(w1[:, l, :].rearrange("p (h n) -> p h n", h=2),
                                R1[:, :].rearrange("p (h n) -> p h n", h=2)[:, :, 0:HID]).then_inc(w1_ev, 1)
            dve.wait_ge(m_in, 16 * (7 + HC))
            qv = qks[:, :, :].rearrange("p l (c d) -> p l c d", d=DH)
            for c in (1, 3):
                link(dve.tensor_scalar(qv[:, :, c, 0:HALF], qv[:, :, c, 0:HALF], -1.0, None, ALU.mult))


def loads(nc, e, d):
    X, tab, wqkv, wo, b1b, w2, b2b, qks, ident, center = (e[k] for k in (
        "X", "tab", "wqkv", "wo", "b1b", "w2", "b2b", "qks", "ident", "center"))
    DIM, DH, HALF, HID, HC, LAYERS = (e[k] for k in ("DIM", "DH", "HALF", "HID", "HC", "LAYERS"))
    w1r, lng, lnb, maskf, x_in, s_in, w1_in, m_in, pad_done = (d[k] for k in (
        "w1r", "lng", "lnb", "maskf", "x_in", "s_in", "w1_in", "m_in", "pad_done"))
    wi, wo_s = e["wqkv_in"], e["wo_in"]
    with ExitStack() as ctx:
        block = ctx.enter_context(nc.Block())

        @block.sync
        def _(sp):
            sp.dma_start(X[:, :], e["x_mid"]).then_inc(x_in, 16)
            sp.dma_start(ident[:, :], e["ident_in"]).then_inc(s_in, 16)
            sp.dma_start(center[:, :], e["center_in"]).then_inc(s_in, 16)
            sp.dma_start(maskf[:, :, :], e["masks"]).then_inc(s_in, 16)
            sp.dma_start(lng[:, :], e["ln_g"]).then_inc(s_in, 16)
            sp.dma_start(lnb[:, :], e["ln_b"]).then_inc(s_in, 16)
            sp.dma_start(b1b[:, :, :], e["b1"].unsqueeze(0).to_broadcast([P, LAYERS, 2 * HID])).then_inc(s_in, 16)
            sp.dma_start(b2b[:, :, :], e["b2"].unsqueeze(0).to_broadcast([P, LAYERS, DIM])).then_inc(s_in, 16)
            sp.dma_start(wqkv[:, 0, :], e["Wqkv"][0]).then_inc(wi, 16)
            sp.dma_start(wo[:, 0, :].rearrange("p (c n) -> p c n", n=DIM),
                         e["Wo"][0].rearrange("(c p) n -> p c n", p=P)).then_inc(wo_s, 16)
            sp.wait_ge(x_in, 16)

        @block.scalar
        def _(act):
            for l in range(LAYERS):
                act.dma_start(w1r[:, l, :], e["W1"][l]).then_inc(w1_in, 16)
            act.dma_start(tab[:, :], e["rotary"]).then_inc(m_in, 16)
            qv = qks[:, :, :].rearrange("p l (c d) -> p l c d", d=DH)
            for c, s in ((0, e["q_scale"]), (2, e["k_scale"])):
                s = s.unsqueeze(0).to_broadcast([P, LAYERS, DH])
                act.dma_start(qv[:, :, c, :], s).then_inc(m_in, 16)
                act.dma_start(qv[:, :, c + 1, 0:HALF], s[:, :, HALF:DH]).then_inc(m_in, 16)
                act.dma_start(qv[:, :, c + 1, HALF:DH], s[:, :, 0:HALF]).then_inc(m_in, 16)
            act.wait_ge(pad_done, 1)
            w2v = w2[:, :, :].rearrange("p l (c n) -> p l c n", n=DIM)
            for c in range(HC):
                n = min(P, HID - c * P)
                act.dma_start(w2v[0:n, :, c, :], e["W2"][0:LAYERS, c * P:c * P + n, :].rearrange("l p n -> p l n")).then_inc(m_in, 16)

        @block.vector
        def _(dve):
            dve.memset(w2[:, :, :], 0.0).then_inc(pad_done, 1)


def layer_norm(nc, e, X, resid, tag):
    DIM, NW = e["DIM"], e["NW"]
    G = 4
    GROUPS = NW // G
    N = G * DIM
    with ExitStack() as ctx:
        def sb(name, shape, dt=F32):
            return ctx.enter_context(nc.sbuf_tensor(name, shape, dt))

        def sem(name):
            return nc.alloc_semaphore(name)

        sq = sb(tag + "_sq", [P, 2, N])
        su = sb(tag + "_su", [P, GROUPS, G])
        va = sb(tag + "_va", [P, GROUPS, G])
        lg = sb(tag + "_lg", [P, GROUPS, G])
        rs = sb(tag + "_rs", [P, GROUPS, G])
        eps = sb(tag + "_eps", [P, 1])
        res = sb(tag + "_res", [P, 2, N])
        v = sem(tag + "_v"); cen = sem(tag + "_cen"); sqd = sem(tag + "_sq"); vard = sem(tag + "_var"); rsd = sem(tag + "_rs"); lgd = sem(tag + "_lg")
        r_in = [sem(tag + "_rin0"), sem(tag + "_rin1")]; done = sem(tag + "_done"); scaled = sem(tag + "_scaled"); st = sem(tag + "_store")
        block = ctx.enter_context(nc.Block())

        def grp(t, g):
            return t[:, g * N:(g + 1) * N].rearrange("p (w n) -> p w n", n=DIM)

        @block.sync
        def _(sp):
            if resid is None:
                return
            for g in range(GROUPS):
                if g >= 2:
                    sp.wait_ge(done, g - 1)
                sp.dma_start(res[:, g % 2, :], resid[:, g * N:(g + 1) * N]).then_inc(r_in[g % 2], 16)
                if g >= 1:
                    sp.wait_ge(done, g)
                    sp.dma_start(e["out"][:, (g - 1) * N:g * N], X[:, (g - 1) * N:g * N]).then_inc(st, 16)
            sp.wait_ge(done, GROUPS)
            sp.dma_start(e["out"][:, (GROUPS - 1) * N:GROUPS * N], X[:, (GROUPS - 1) * N:GROUPS * N]).then_inc(st, 16)
            sp.wait_ge(st, 16 * GROUPS)

        def rstd(act, g):
            act.wait_ge(vard, g + 1)
            act.activation(lg[:, g, :], va[:, g, :], ACT.Ln, bias=eps[:, 0:1], scale=1.0 / DIM).then_inc(lgd, 1)
            act.wait_ge(lgd, g + 1)
            act.activation(rs[:, g, :], lg[:, g, :], ACT.Exp, scale=-0.5).then_inc(rsd, 1)

        @block.scalar
        def _(act):
            act.preload_act_table_set(LN_EXP)
            act.wait_ge(v, 1)
            for g in range(GROUPS):
                act.wait_ge(cen, g + 1)
                if g >= 2:
                    act.wait_ge(vard, g - 1)
                act.activation(sq[:, g % 2, :], X[:, g * N:(g + 1) * N], ACT.Square).then_inc(sqd, 1)
                if g >= 1:
                    rstd(act, g - 1)
            rstd(act, GROUPS - 1)

        @block.vector
        def _(dve):
            steps = [1]

            def link(ins):
                steps[0] += 1
                ins.then_inc(v, 1)
                dve.wait_ge(v, steps[0])

            dve.memset(eps[:, :], 1e-5).then_inc(v, 1)

            def centre(g):
                link(dve.tensor_reduce(su[:, g, :], grp(X, g), AX.X, ALU.add))
                link(dve.tensor_scalar(su[:, g, :], su[:, g, :], 1.0 / DIM, None, ALU.mult))
                dve.tensor_tensor(grp(X, g), grp(X, g), su[:, g, :].unsqueeze(2).to_broadcast([P, G, DIM]),
                                  ALU.subtract).then_inc(cen, 1)

            def variance(g):
                dve.wait_ge(sqd, g + 1)
                dve.tensor_reduce(va[:, g, :], sq[:, g % 2, :].rearrange("p (w n) -> p w n", n=DIM), AX.X,
                                  ALU.add).then_inc(vard, 1)

            def scale(g):
                dve.wait_ge(rsd, g + 1)
                ins = dve.tensor_tensor(grp(X, g), grp(X, g), rs[:, g, :].unsqueeze(2).to_broadcast([P, G, DIM]), ALU.mult)
                if resid is None:
                    ins.then_inc(done, 1)
                    return
                ins.then_inc(scaled, 1)

            for g in range(GROUPS + 2):
                if g < GROUPS:
                    centre(g)
                if 1 <= g <= GROUPS:
                    variance(g - 1)
                if g >= 2:
                    scale(g - 2)

        if resid is not None:
            @block.gpsimd
            def _(pool):
                for g in range(GROUPS):
                    pool.wait_ge(scaled, g + 1)
                    pool.wait_ge(r_in[g % 2], 16 * (g // 2 + 1))
                    pool.tensor_tensor(X[:, g * N:(g + 1) * N], X[:, g * N:(g + 1) * N], res[:, g % 2, :], ALU.add).then_inc(done, 1)

        if resid is None and e["x_ready"] is not None:
            @block.gpsimd
            def _(pool):
                pool.wait_ge(done, GROUPS)
                pool.sem_inc(e["x_ready"], NW)


def finish(nc, ctx0, e):
    layer_norm(nc, e, e["X"], e["x_mid"], "last")


def stream(nc, ctx0, e):
    (X, tab, wqkv, wo, w1, b1b, w2, b2b, qks, ident, center, identb, maskb, first, R0, R1, R2, b6, b7) = (e[k] for k in (
        "X", "tab", "wqkv", "wo", "w1", "b1b", "w2", "b2b", "qks", "ident", "center", "identb", "maskb", "first",
        "R0", "R1", "R2", "b6", "b7"))
    DIM, DH, HALF, NW, HID, HC, LAYERS, PAIRS, WIN, HEADS, INNER, TILES, B = (e[k] for k in (
        "DIM", "DH", "HALF", "NW", "HID", "HC", "LAYERS", "PAIRS", "WIN", "HEADS", "INNER", "TILES", "B"))
    QKS, SHIFT = e["QKS"], e["LOG2_SHIFT"]
    wqkv_in, wo_in, x_ready = e["wqkv_in"], e["wo_in"], e["x_ready"]
    K2 = 2 * WIN
    HS = PAIRS * K2
    with ExitStack() as ctx:
        def sb(name, shape, dt=F32):
            return ctx.enter_context(nc.sbuf_tensor(name, shape, dt))

        def sem(name):
            return nc.alloc_semaphore(name)

        x_tile = sb("x_tile", [P, DIM])
        shifted_t = sb("shifted_t", [P, B, WIN])
        mid_shifted_t = sb("mid_shifted_t", [P, B, WIN])
        carry_in = sb("carry_in", [P, B])
        mid_carry_in = sb("mid_carry_in", [P, B])
        qk_squares = sb("qk_squares", [P, 2 * INNER])
        square_sum = sb("square_sum", [P, 2 * HEADS])
        log_square_sum = sb("log_square_sum", [P, 2 * HEADS])
        rnorm = sb("rnorm", [P, 2 * HEADS])
        normed_qk = sb("normed_qk", [P, 2 * INNER])
        cos_part = sb("cos_part", [P, 2 * INNER])
        sin_part = sb("sin_part", [P, 2 * INNER])
        scaled_tables = sb("scaled_tables", [P, 4 * DH])
        queries_t = sb("queries_t", [P, PAIRS, P])
        keys_t = sb("keys_t", [P, 2, PAIRS, P])
        row_max = sb("row_max", [P, HEADS])
        probs = sb("probs", [P, PAIRS, 2, K2])
        prob_sum = sb("prob_sum", [P, PAIRS, 2])
        inv_prob_sum = sb("inv_prob_sum", [P, HEADS])
        attn_out = sb("attn_out", [P, INNER])
        probs_t = sb("probs_t", [P, PAIRS, P])
        values_raw = sb("values_raw", [P, 2, PAIRS * DH])
        values_ring = sb("values_ring", [P, B, PAIRS * DH])
        attn_out_t = sb("attn_out_t", [P, PAIRS, P])
        mid_x = sb("mid_x", [P, DIM])
        mid_x_biased = sb("mid_x_biased", [P, 2, DIM])
        centred_squares = sb("centred_squares", [P, DIM])
        var_sum = sb("var_sum", [P, 1])
        log_var = sb("log_var", [P, 1])
        rstd_x = sb("rstd_x", [P, 1])
        hidden_a = sb("hidden_a", [P, HID])
        hidden_gate = sb("hidden_gate", [P, HID])
        gate_gelu = sb("gate_gelu", [P, HID])
        activated = sb("activated", [P, HC * P])
        activated_t = sb("activated_t", [P, HC, P])
        eps = sb("eps", [P, 1])
        norm_shift = sb("norm_shift", [P, 1])

        names = ("buffers_cleared x_tile_copied x_transposed x_shifted x_shift_step values_made queries_made "
                 "keys_made values_in_sbuf values_by_key q_squared k_squared q_square_sums k_square_sums "
                 "q_sums_clamped k_sums_clamped q_sums_logged k_sums_logged q_rnorm_ready k_rnorm_ready q_normed "
                 "k_normed tables_scaled q_cos_part k_cos_part q_sin_part k_sin_part q_transposed k_transposed "
                 "q_in_sbuf k_in_sbuf scores_made row_maxima maxima_subtracted exps_made exp_sums sums_inverted "
                 "attn_normed attn_transposed probs_transposed probs_in_sbuf attn_made attn_in_sbuf "
                 "attn_projected attn_residual_added output_bias_added mid_transposed mid_shifted mid_shift_step "
                 "variance_sum variance_logged rstd_ready hidden_made gate_made hidden_ready gate_ready "
                 "first_keys_cleared q_rotated attn_issued weights_ready gelu_made activations_made "
                 "activations_transposed activations_in_sbuf ffn_projected").split()
        s = {n: sem("s_" + n) for n in names}
        block = ctx.enter_context(nc.Block())

        Q4 = lambda t: t.rearrange("p (h s d) -> p h s d", s=2, d=HALF)
        swapped = lambda t: Q4(t)[:, :, ::-1, :]
        def table(i):
            return scaled_tables[:, i * DH:(i + 1) * DH].rearrange("p (s d) -> p s d", s=2).unsqueeze(1).to_broadcast([P, HEADS, 2, HALF])

        def win(t):
            return t % NW

        def lay(t):
            return t // NW

        def drive(eng, body):
            for n in range(-1, 4):
                body(n, n % 2)
            with eng.Fori(4, TILES - 2, 2) as n:
                body(n, 0, True)
                body(n + 1, 1, True)
            for n in range(TILES - 2, TILES + 3):
                body(n, n % 2)

        def has(t, loop):
            return loop or 0 <= t < TILES

        def above(n, loop, c):
            return loop or n - c > 0

        @block.tensor
        def _(pe):
            def body(n, par, loop=False):
                new, mid, ffn, done = n, n - 1, n - 2, n - 3
                wf = wqkv[:, :, :].rearrange("p l n -> p (l n)")

                def proj(t, region, part, sig):
                    for h in range(2):
                        o = (lay(t) % 2) * (3 * INNER) + (part * INNER + 512 * h)
                        mm = pe.matmul(region[:, 512 * h:512 * h + 512], shifted_t[:, :, :].rearrange("p b i -> p (b i)"),
                                       wf[:, bass.ds(o, 512)], start=True, stop=True)
                    mm.then_inc(s[sig], 1)

                if has(new, loop):
                    if above(n, loop, 1):
                        pe.wait_ge(s["attn_in_sbuf"], n - 1)
                    proj(n, R2, 2, "values_made")
                    if above(n, loop, 0):
                        pe.wait_ge(s["maxima_subtracted"], 2 * n)
                    proj(n, R1, 1, "keys_made")
                if has(done, loop):
                    pe.wait_ge(s["activations_made"], done + 1)
                    pe.wait_ge(s["hidden_ready"], done + 1)
                    pe.wait_ge(s["variance_sum"], done + 1)
                    if has(ffn, loop):
                        pe.wait_ge(s["mid_shifted"], ffn + 1)
                    for c in range(HC):
                        mm = pe.transpose(b6[:, c * P:(c + 1) * P], activated[:, c * P:(c + 1) * P], ident[:, :])
                    mm.then_inc(s["activations_transposed"], 1)
                if has(mid, loop):
                    pe.wait_ge(s["exps_made"], 2 * mid + 2)
                    if has(new, loop):
                        pe.wait_ge(s["values_in_sbuf"], n + 1)
                    for p in range(PAIRS):
                        mm = pe.transpose(R2[:, p * P:(p + 1) * P], probs[:, p, :, :].rearrange("p a k -> p (a k)"), ident[:, :])
                    mm.then_inc(s["probs_transposed"], 1)
                if has(ffn, loop):
                    pe.wait_ge(s["attn_residual_added"], ffn + 1)
                    pe.wait_ge(s["mid_shifted"], ffn + 1)
                    lx = mid_shifted_t[:, :, :].rearrange("p b i -> p (b i)")
                    w1f = w1[:, :, :].rearrange("p l n -> p (l n)")
                    o = lay(ffn) * (2 * HID)
                    pe.matmul(b7[:, 0:HID], lx, w1f[:, bass.ds(o + HID, HID)], start=True, stop=True).then_inc(s["gate_made"], 1)
                if has(done, loop):
                    pe.wait_ge(s["activations_in_sbuf"], done + 1)
                    w2f = w2[:, :, :].rearrange("p l n -> p (l n)")
                    for c in range(HC):
                        o = lay(done) * (HC * DIM) + c * DIM
                        mm = pe.matmul(b6[:, 0:DIM], activated_t[:, c, :], w2f[:, bass.ds(o, DIM)], start=(c == 0), stop=(c == HC - 1))
                    mm.then_inc(s["ffn_projected"], 1)
                if has(mid, loop):
                    pe.wait_ge(s["probs_in_sbuf"], mid + 1)
                    pe.wait_ge(s["values_by_key"], (mid + 1) * (16 * 2 * B))
                    pe.sem_inc(s["attn_issued"], 1)
                    for p in range(PAIRS):
                        for a in range(2):
                            q = slice(64 * a, 64 * a + 64)
                            o = a * (INNER // 2) + p * DH
                            for b in range(B):
                                mm = pe.matmul(R2[b * WIN:(b + 1) * WIN, o:o + DH], probs_t[q, p, b * WIN:(b + 1) * WIN],
                                               values_ring[q, b, p * DH:(p + 1) * DH], start=True, stop=True)
                    mm.then_inc(s["attn_made"], 1)

                if has(ffn, loop):
                    pe.wait_ge(s["mid_shifted"], ffn + 1)
                    if has(done, loop):
                        pe.wait_ge(x_ready, done + (NW + 1))
                    lx = mid_shifted_t[:, :, :].rearrange("p b i -> p (b i)")
                    w1f = w1[:, :, :].rearrange("p l n -> p (l n)")
                    o = lay(ffn) * (2 * HID)
                    pe.matmul(b6[:, 512 - DIM:512], lx, center[:, :], start=True, stop=True)
                    pe.matmul(b6[:, 0:HID], lx, w1f[:, bass.ds(o, HID)], start=True, stop=True).then_inc(s["hidden_made"], 1)

                def rotated(reg, o, a, c, sig):
                    pe.wait_ge(s[a], n + 1)
                    pe.wait_ge(s[c], n + 1)
                    for p in range(PAIRS):
                        c0 = o + p * P
                        pe.matmul(reg[:, p * P:(p + 1) * P], cos_part[:, c0:c0 + P], ident[:, :], is_transpose=True,
                                  start=True, stop=False)
                        mm = pe.matmul(reg[:, p * P:(p + 1) * P], sin_part[:, c0:c0 + P], ident[:, :], is_transpose=True,
                                       start=False, stop=True)
                    mm.then_inc(s[sig], 1)

                if has(new, loop):
                    pe.wait_ge(s["q_rotated"], n + 1)
                    for p in range(PAIRS):
                        mm = pe.transpose(R0[:, p * P:(p + 1) * P], sin_part[:, p * P:(p + 1) * P], ident[:, :])
                    mm.then_inc(s["q_transposed"], 1)
                if has(mid, loop):
                    pe.wait_ge(s["attn_normed"], mid + 1)
                    for p in range(PAIRS):
                        mm = pe.transpose(R2[:, p * P:(p + 1) * P], attn_out[:, p * P:(p + 1) * P], ident[:, :])
                    mm.then_inc(s["attn_transposed"], 1)
                if has(new, loop):
                    rotated(R1, INNER, "k_cos_part", "k_sin_part", "k_transposed")
                if loop or 0 <= n + 1 < TILES:
                    pe.wait_ge(s["x_tile_copied"], n + 2)
                    if has(ffn, loop):
                        pe.wait_ge(s["hidden_ready"], ffn + 1)
                        pe.wait_ge(s["variance_sum"], ffn + 1)
                    pe.transpose(b6[:, 0:P], x_tile[:, :], ident[:, :]).then_inc(s["x_transposed"], 1)
                if has(mid, loop):
                    pe.wait_ge(s["attn_in_sbuf"], mid + 1)
                    pe.wait_ge(s["weights_ready"], lay(mid) + 1)
                    if has(ffn, loop):
                        pe.wait_ge(s["gate_ready"], ffn + 1)
                    wof = wo[:, :, :].rearrange("p l n -> p (l n)")
                    for p in range(PAIRS):
                        o = (lay(mid) % 2) * (PAIRS * DIM) + p * DIM
                        mm = pe.matmul(b7[:, 0:DIM], attn_out_t[:, p, :], wof[:, bass.ds(o, DIM)], start=(p == 0), stop=(p == PAIRS - 1))
                    mm.then_inc(s["attn_projected"], 1)
                for a in range(2):
                    if has(new, loop):
                        if a == 0:
                            pe.wait_ge(s["q_in_sbuf"], n + 1)
                            pe.wait_ge(s["k_in_sbuf"], n + 1)
                            if par == 0:
                                pe.wait_ge(s["first_keys_cleared"], n // 2 + 1)
                        m = ((win(n) + (NW - 1)) // NW) if par == 0 else 2
                        pe.matmul(R1[:, a * HS:(a + 1) * HS], identb[:, :], maskb[:, bass.ds(m * HS, HS)],
                                  start=True, stop=False, skip_group_check=True)
                        q = slice(64 * a, 64 * a + 64)
                        for p in range(PAIRS):
                            for b in range(B):
                                mm = pe.matmul(R1[b * WIN:(b + 1) * WIN, a * HS + p * K2:a * HS + (p + 1) * K2],
                                               queries_t[q, p, b * WIN:(b + 1) * WIN], keys_t[q, :, p, b * WIN:(b + 1) * WIN],
                                               start=False, stop=True, skip_group_check=True)
                        mm.then_inc(s["scores_made"], 1)
                    if a == 0 and has(mid, loop):
                        pe.wait_ge(s["attn_residual_added"], mid + 1)
                        if has(ffn, loop):
                            pe.wait_ge(s["hidden_ready"], ffn + 1)
                            pe.wait_ge(s["variance_sum"], ffn + 1)
                        if loop or n + 1 < TILES:
                            pe.wait_ge(s["x_shifted"], n + 2)
                        pe.transpose(b6[:, 0:P], mid_x[:, :], ident[:, :]).then_inc(s["mid_transposed"], 1)
                    if a == 0 and (loop or 0 <= n + 1 < TILES):
                        pe.wait_ge(s["x_shifted"], n + 2)
                        pe.wait_ge(s["weights_ready"], lay(n + 1) + 1)
                        if above(n, loop, -1):
                            pe.wait_ge(s["q_in_sbuf"], n + 1)
                        proj(n + 1, R0, 0, "queries_made")


            pe.wait_ge(s["buffers_cleared"], 6)
            drive(pe, body)

        @block.scalar
        def _(act):
            def body(n, par, loop=False):
                new, mid, ffn, done = n, n - 1, n - 2, n - 3
                def softmax_exp(a):
                    act.wait_ge(s["maxima_subtracted"], 2 * mid + 1 + a)
                    act.activation(probs[:, :, a, :], probs[:, :, a, :], ACT.Exp, scale=QKS).then_inc(s["exps_made"], 1)
                def squares(reg, o, mm, prev, sig):
                    act.wait_ge(s[mm], n + 1)
                    if above(n, loop, 0):
                        act.wait_ge(s[prev], n)
                    act.activation(qk_squares[:, o:o + INNER], reg[:, :], ACT.Square).then_inc(s[sig], 1)

                def norms(h, c, l, r):
                    hs = slice(h * HEADS, (h + 1) * HEADS)
                    act.wait_ge(s[c], n + 1)
                    act.activation(log_square_sum[:, hs], square_sum[:, hs], ACT.Ln, scale=float(2 ** SHIFT)).then_inc(s[l], 1)
                    act.wait_ge(s[l], n + 1)
                    if above(n, loop, 0):
                        act.wait_ge(s["k_normed"], n)
                        act.wait_ge(s["q_normed"], n)
                    act.activation(rnorm[:, hs], log_square_sum[:, hs], ACT.Exp, bias=norm_shift[:, 0:1], scale=-0.5).then_inc(s[r], 1)

                act.preload_act_table_set(LN_EXP)
                if has(mid, loop):
                    softmax_exp(0)
                if has(new, loop):
                    squares(R0, 0, "queries_made", "q_square_sums", "q_squared")
                if has(mid, loop):
                    softmax_exp(1)
                if has(new, loop):
                    act.wait_ge(s["values_made"], n + 1)
                    if above(n, loop, 0):
                        act.wait_ge(s["values_by_key"], n * (16 * 2 * B))
                    act.activation(values_raw[:, :, :].rearrange("p a (c d) -> p c a d", d=DH),
                                   R2[:, :].rearrange("p (c a d) -> p c a d", a=2, d=DH), ACT.Copy).then_inc(s["values_in_sbuf"], 1)
                    norms(0, "q_sums_clamped", "q_sums_logged", "q_rnorm_ready")
                if has(new, loop):
                    squares(R1, INNER, "keys_made", "k_square_sums", "k_squared")
                if has(done, loop):
                    act.wait_ge(s["activations_transposed"], done + 1)
                    act.activation(activated_t[:, :, :].rearrange("p c k -> p (c k)"), b6[:, 0:HC * P], ACT.Copy).then_inc(s["activations_in_sbuf"], 1)
                if has(mid, loop):
                    act.wait_ge(s["probs_transposed"], mid + 1)
                    act.activation(probs_t[:, :, :].rearrange("p c k -> p (c k)"), R2[:, :], ACT.Copy).then_inc(s["probs_in_sbuf"], 1)
                if has(new, loop):
                    norms(1, "k_sums_clamped", "k_sums_logged", "k_rnorm_ready")
                if has(ffn, loop):
                    act.wait_ge(s["hidden_made"], ffn + 1)
                    act.activation(centred_squares[:, :], b6[:, 512 - DIM:512], ACT.Square, accum_out=var_sum[:, 0:1]).then_inc(s["variance_sum"], 1)
                    act.wait_ge(s["variance_sum"], ffn + 1)
                    act.activation(log_var[:, :], var_sum[:, :], ACT.Ln, bias=eps[:, 0:1], scale=1.0 / DIM).then_inc(s["variance_logged"], 1)
                    act.wait_ge(s["variance_logged"], ffn + 1)
                    act.activation(rstd_x[:, :], log_var[:, :], ACT.Exp, scale=-0.5).then_inc(s["rstd_ready"], 1)
                if has(new, loop):
                    act.wait_ge(s["q_transposed"], n + 1)
                    act.activation(queries_t[:, :, :].rearrange("p c k -> p (c k)"), R0[:, :], ACT.Copy).then_inc(s["q_in_sbuf"], 1)
                if has(mid, loop):
                    act.wait_ge(s["attn_transposed"], mid + 1)
                    act.activation(attn_out_t[:, :, :].rearrange("p c k -> p (c k)"), R2[:, :], ACT.Copy).then_inc(s["attn_in_sbuf"], 1)
                if has(new, loop):
                    act.wait_ge(s["k_transposed"], n + 1)
                    act.activation(keys_t[:, par, :, :].rearrange("p c k -> p (c k)"), R1[:, :], ACT.Copy).then_inc(s["k_in_sbuf"], 1)
                if has(ffn, loop):
                    act.wait_ge(s["gate_ready"], ffn + 1)
                    act.activation(gate_gelu[:, :], hidden_gate[:, :], ACT.Gelu).then_inc(s["gelu_made"], 1)

            act.wait_ge(s["buffers_cleared"], 6)
            drive(act, body)

        @block.vector
        def _(dve):
            dve.memset(keys_t[:, :, :, :], 0.0).then_inc(s["buffers_cleared"], 1)
            dve.memset(values_ring[:, :, :], 0.0).then_inc(s["buffers_cleared"], 1)
            dve.memset(carry_in[:, :], 0.0).then_inc(s["buffers_cleared"], 1)
            dve.memset(mid_carry_in[:, :], 0.0).then_inc(s["buffers_cleared"], 1)
            dve.memset(activated[:, :], 0.0).then_inc(s["buffers_cleared"], 1)
            dve.memset(eps[:, :], 1e-5).then_inc(s["buffers_cleared"], 1)
            dve.memset(norm_shift[:, :], 0.5 * SHIFT * float(np.log(2.0))).then_inc(s["buffers_cleared"], 1)

            def shifted(t, loop, src, dst, carry, step, done):
                up = slice(DIM // 2, DIM)
                lo = slice(0, DIM // 2)
                sv = src[:, 0:P].rearrange("p (b i) -> p b i", b=B)
                dve.tensor_copy(dst[lo, :, :], sv[lo, :, :]).then_inc(s[step], 1)
                dve.tensor_copy(dst[up, :, 1:WIN], sv[up, :, 0:WIN - 1]).then_inc(s[step], 1)
                dve.tensor_scalar(dst[up, :, 0], carry[up, :], first[up, bass.ds(win(t), 1)], None, ALU.mult).then_inc(s[step], 1)
                dve.wait_ge(s[step], t * 3 + 3)
                dve.tensor_copy(carry[up, :], sv[up, :, WIN - 1]).then_inc(s[done], 1)

            def body(n, par, loop=False):
                new, mid, ffn, done = n, n - 1, n - 2, n - 3
                def square_sums(h, a, b_, c):
                    hs = slice(h * HEADS, (h + 1) * HEADS)
                    dve.wait_ge(s[a], n + 1)
                    if above(n, loop, 0):
                        dve.wait_ge(s["k_sums_logged"], n)
                    dve.tensor_reduce(square_sum[:, hs], qk_squares[:, h * INNER:(h + 1) * INNER].rearrange("p (h d) -> p h d", d=DH),
                                      AX.X, ALU.add).then_inc(s[b_], 1)
                    dve.wait_ge(s[b_], n + 1)
                    dve.tensor_scalar(square_sum[:, hs], square_sum[:, hs], 1e-24, None, ALU.max).then_inc(s[c], 1)

                if has(new, loop):
                    square_sums(0, "q_squared", "q_square_sums", "q_sums_clamped")
                def normed(h, reg, r, d, prev):
                    dve.wait_ge(s[r], n + 1)
                    if above(n, loop, 0):
                        dve.wait_ge(s[prev], n)
                    dve.tensor_tensor(normed_qk[:, h * INNER:(h + 1) * INNER].rearrange("p (h d) -> p h d", d=DH),
                                      reg[:, :].rearrange("p (h d) -> p h d", d=DH),
                                      rnorm[:, h * HEADS:(h + 1) * HEADS].unsqueeze(2).to_broadcast([P, HEADS, DH]),
                                      ALU.mult).then_inc(s[d], 1)

                def cosines(h, d, t, prev):
                    hs = slice(h * INNER, (h + 1) * INNER)
                    dve.wait_ge(s[d], n + 1)
                    dve.wait_ge(s["tables_scaled"], n + 1)
                    if above(n, loop, 0):
                        dve.wait_ge(s[prev], n)
                    dve.tensor_tensor(Q4(cos_part[:, hs]), Q4(normed_qk[:, hs]), table(2 * h), ALU.mult).then_inc(s[t], 1)

                def exp_sums(a):
                    dve.wait_ge(s["exps_made"], 2 * mid + 1 + a)
                    if above(mid, loop, 0):
                        dve.wait_ge(s["sums_inverted"], mid)
                    dve.tensor_reduce(prob_sum[:, :, a], probs[:, :, a, :], AX.X, ALU.add).then_inc(s["exp_sums"], 1)

                if has(mid, loop):
                    exp_sums(0)
                if has(new, loop):
                    normed(0, R0, "q_rnorm_ready", "q_normed", "q_sin_part")
                    square_sums(1, "k_squared", "k_square_sums", "k_sums_clamped")
                    cosines(0, "q_normed", "q_cos_part", "q_transposed")
                if has(mid, loop):
                    exp_sums(1)
                    dve.wait_ge(s["exp_sums"], 2 * mid + 2)
                    if above(mid, loop, 0):
                        dve.wait_ge(s["attn_normed"], mid)
                    dve.reciprocal(inv_prob_sum[:, :], prob_sum[:, :, :].rearrange("p c a -> p (c a)")).then_inc(s["sums_inverted"], 1)
                if has(done, loop):
                    dve.wait_ge(s["ffn_projected"], done + 1)
                    dve.wait_ge(s["output_bias_added"], done + 1)
                    dve.tensor_tensor(X[:, bass.ds(win(done) * DIM, DIM)], b6[:, 0:DIM], mid_x_biased[:, 1 - par, :], ALU.add).then_inc(x_ready, 1)
                if has(new, loop):
                    normed(1, R1, "k_rnorm_ready", "k_normed", "k_sin_part")
                if has(mid, loop):
                    dve.wait_ge(s["attn_made"], mid + 1)
                    dve.wait_ge(s["sums_inverted"], mid + 1)
                    if above(mid, loop, 0):
                        dve.wait_ge(s["attn_transposed"], mid)
                    dve.tensor_tensor(attn_out[:, :].rearrange("p (c a d) -> p c a d", a=2, d=DH),
                                      R2[:, :].rearrange("p (a c d) -> p c a d", a=2, d=DH),
                                      inv_prob_sum[:, :].rearrange("p (c a) -> p c a", a=2).unsqueeze(3).to_broadcast([P, PAIRS, 2, DH]),
                                      ALU.mult).then_inc(s["attn_normed"], 1)
                if has(new, loop):
                    cosines(1, "k_normed", "k_cos_part", "k_transposed")
                if has(ffn, loop):
                    b1f = b1b[:, :, :].rearrange("p l n -> p (l n)")
                    o = lay(ffn) * (2 * HID)
                    dve.wait_ge(s["rstd_ready"], ffn + 1)
                    dve.wait_ge(s["hidden_made"], ffn + 1)
                    dve.scalar_tensor_tensor(out=hidden_a[:, :], in0=b6[:, 0:HID], scalar=rstd_x[:, 0:1], in1=b1f[:, bass.ds(o, HID)],
                                             op0=ALU.mult, op1=ALU.add).then_inc(s["hidden_ready"], 1)
                    dve.wait_ge(s["gate_made"], ffn + 1)
                    dve.scalar_tensor_tensor(out=hidden_gate[:, :], in0=b7[:, 0:HID], scalar=rstd_x[:, 0:1], in1=b1f[:, bass.ds(o + HID, HID)],
                                             op0=ALU.mult, op1=ALU.add).then_inc(s["gate_ready"], 1)
                if has(new, loop) and par == 0:
                    if above(n, loop, 0):
                        dve.wait_ge(s["scores_made"], 2 * n)
                        dve.wait_ge(s["k_in_sbuf"], n)
                    old_keys = keys_t[:, 1, :, :].rearrange("p c k -> p (c k)")
                    dve.tensor_scalar(old_keys, old_keys, first[:, bass.ds(win(n), 1)], None, ALU.mult).then_inc(s["first_keys_cleared"], 1)
                if loop or 0 <= n + 1 < TILES:
                    t = n + 1
                    dve.wait_ge(s["x_transposed"], t + 1)
                    if above(t, loop, 0):
                        dve.wait_ge(s["keys_made"], t)
                        dve.wait_ge(s["x_shifted"], t)
                    shifted(t, loop, b6, shifted_t, carry_in, "x_shift_step", "x_shifted")
                if has(mid, loop):
                    dve.wait_ge(s["attn_projected"], mid + 1)
                    if above(mid, loop, 0):
                        dve.wait_ge(s["output_bias_added"], mid)
                        dve.wait_ge(s["mid_transposed"], mid)
                    dve.tensor_tensor(mid_x[:, :], b7[:, 0:DIM], X[:, bass.ds(win(mid) * DIM, DIM)], ALU.add).then_inc(s["attn_residual_added"], 1)
                    dve.wait_ge(s["mid_transposed"], mid + 1)
                    if above(mid, loop, 0):
                        dve.wait_ge(s["gate_made"], mid)
                        dve.wait_ge(s["mid_shifted"], mid)
                    shifted(mid, loop, b6, mid_shifted_t, mid_carry_in, "mid_shift_step", "mid_shifted")
                if has(ffn, loop):
                    dve.wait_ge(s["gelu_made"], ffn + 1)
                    if above(ffn, loop, 0):
                        dve.wait_ge(s["activations_transposed"], ffn)
                    dve.tensor_tensor(activated[:, 0:HID], hidden_a[:, :], gate_gelu[:, :], ALU.mult).then_inc(s["activations_made"], 1)
                if has(new, loop):
                    for a in range(2):
                        hs = slice(a * PAIRS, (a + 1) * PAIRS)
                        sv = R1[:, a * HS:(a + 1) * HS].rearrange("p (c k) -> p c k", k=K2)
                        dve.wait_ge(s["scores_made"], 2 * n + 1 + a)
                        dve.tensor_reduce(row_max[:, hs], sv, AX.X, ALU.max).then_inc(s["row_maxima"], 1)
                        dve.wait_ge(s["row_maxima"], 2 * n + 1 + a)
                        if above(n, loop, 0):
                            dve.wait_ge(s["probs_transposed"], n)
                            dve.wait_ge(s["exp_sums"], 2 * n)
                        dve.tensor_tensor(probs[:, :, a, :], sv,
                                          row_max[:, hs].unsqueeze(2).to_broadcast([P, PAIRS, K2]), ALU.subtract).then_inc(s["maxima_subtracted"], 1)

            dve.wait_ge(s["buffers_cleared"], 7)
            drive(dve, body)

        @block.gpsimd
        def _(pool):
            def body(n, par, loop=False):
                new, mid, ffn, done = n, n - 1, n - 2, n - 3
                if has(new, loop):
                    if above(n, loop, 0):
                        pool.wait_ge(s["k_cos_part"], n)
                        pool.wait_ge(s["k_sin_part"], n)
                    qf = qks[:, :, :].rearrange("p l n -> p (l n)")
                    pool.tensor_tensor(scaled_tables[:, :].rearrange("p (c s d) -> p c s d", s=2, d=HALF),
                                       qf[:, bass.ds(lay(n) * (4 * DH), 4 * DH)].rearrange("p (c s d) -> p c s d", s=2, d=HALF),
                                       tab[:, bass.ds(win(n) * (4 * HALF), 4 * HALF)].rearrange("p (c d) -> p c d", d=HALF)
                                       .unsqueeze(2).to_broadcast([P, 4, 2, HALF]), ALU.mult).then_inc(s["tables_scaled"], 1)
                if loop or 0 <= n + 1 < TILES:
                    t = n + 1
                    pool.wait_ge(x_ready, t + 1)
                    if above(t, loop, 0):
                        pool.wait_ge(s["x_transposed"], t)
                    pool.tensor_copy(x_tile[:, :], X[:, bass.ds(win(t) * DIM, DIM)]).then_inc(s["x_tile_copied"], 1)
                if has(new, loop):
                    pool.wait_ge(s["tables_scaled"], n + 1)
                    for h, d, t, prev in ((0, "q_normed", "q_sin_part", "q_transposed"), (1, "k_normed", "k_sin_part", "k_transposed")):
                        hs = slice(h * INNER, (h + 1) * INNER)
                        if h == 1:
                            pool.wait_ge(s["q_cos_part"], n + 1)
                            pool.wait_ge(s["q_sin_part"], n + 1)
                            qs = slice(0, INNER)
                            pool.tensor_tensor(sin_part[:, qs], sin_part[:, qs], cos_part[:, qs], ALU.add).then_inc(s["q_rotated"], 1)
                        pool.wait_ge(s[d], n + 1)
                        if above(n, loop, 0):
                            pool.wait_ge(s[prev], n)
                        pool.tensor_tensor(Q4(sin_part[:, hs]), swapped(normed_qk[:, hs]), table(2 * h + 1), ALU.mult).then_inc(s[t], 1)
                if has(mid, loop):
                    pool.wait_ge(s["attn_residual_added"], mid + 1)
                    if above(mid, loop, 1):
                        pool.wait_ge(x_ready, mid + (NW - 1))
                    b2f = b2b[:, :, :].rearrange("p l n -> p (l n)")
                    pool.tensor_tensor(mid_x_biased[:, 1 - par, :], mid_x[:, :], b2f[:, bass.ds(lay(mid) * DIM, DIM)], ALU.add).then_inc(s["output_bias_added"], 1)

            pool.wait_ge(s["buffers_cleared"], 7)
            drive(pool, body)

        @block.sync
        def _(sp):
            def values(t, par, loop=False):
                sp.wait_ge(s["values_in_sbuf"], t + 1)
                if above(t, loop, 0):
                    sp.wait_ge(s["attn_made"], t)
                for a in range(2):
                    for b in range(B):
                        q = 64 * a + WIN * par
                        sp.dma_start(values_ring[q:q + WIN, b, :], values_raw[b * WIN:(b + 1) * WIN, a, :]).then_inc(s["values_by_key"], 16)

            sp.wait_ge(s["buffers_cleared"], 7)
            sp.wait_ge(wqkv_in, 16)
            sp.wait_ge(wo_in, 16)
            sp.sem_inc(s["weights_ready"], 1)
            for l in range(LAYERS):
                t0 = l * NW
                values(t0, 0)
                values(t0 + 1, 1)
                if l + 1 < LAYERS:
                    sl = (l + 1) % 2
                    if l >= 1:
                        sp.wait_ge(s["keys_made"], t0)
                    sp.dma_start(wqkv[:, sl, :], e["Wqkv"][l + 1]).then_inc(wqkv_in, 16)
                    if l >= 1:
                        sp.wait_ge(s["attn_projected"], t0)
                    sp.dma_start(wo[:, sl, :].rearrange("p (c n) -> p c n", n=DIM),
                                 e["Wo"][l + 1].rearrange("(c p) n -> p c n", p=P)).then_inc(wo_in, 16)
                with sp.Fori(t0 + 2, t0 + NW - 2, 2) as t:
                    values(t, 0, True)
                    values(t + 1, 1, True)
                if l + 1 < LAYERS:
                    sp.wait_ge(wqkv_in, 16 * (l + 2))
                    sp.wait_ge(wo_in, 16 * (l + 2))
                    sp.sem_inc(s["weights_ready"], 1)
                values(t0 + NW - 2, 0)
                values(t0 + NW - 1, 1)
            sp.wait_ge(s["values_by_key"], TILES * 16 * 2 * B)


def memory(nc, hidden, proj, cols, mW1T, mW2T, mW2, WoT, gWT, norm_g, gb, mean_in, ident_in, x_mid):
    B, WIN = 4, P // 4
    DIM = gWT.shape[0]
    D = mW1T.shape[0]
    NW = hidden.shape[1] // DIM
    S = NW * WIN
    C = 64
    NC = S // C
    with ExitStack() as ctx:
        def sb(name, shape, dt=F32):
            return ctx.enter_context(nc.sbuf_tensor(name, shape, dt))

        Y = sb("Y", [P, NW * DIM])
        hT = sb("hT", [P, NW, P])
        big = sb("big", [P, 9, S])
        ident = sb("m_ident", [P, P])
        MT = sb("MT", [C, B, S])
        E = sb("E", [C, B, S])
        banks = [ctx.enter_context(nc.psum_tensor(f"bank{i}", [P, 512], F32)) for i in range(8)]
        e = dict(locals())
        e.update(x_ready=None, out=x_mid)
        load_and_norm(nc, e)
        gates(nc, e)
        read = chunks(nc, ctx, e)
        e["RT"] = read
        output(nc, e)
        layer_norm(nc, dict(DIM=DIM, NW=NW, out=x_mid), Y, hidden, "memory")


def load_and_norm(nc, e):
    with ExitStack() as ctx:
        x_in = nc.alloc_semaphore("y_in")
        block = ctx.enter_context(nc.Block())

        @block.sync
        def _(sp):
            sp.dma_start(e["Y"][:, :], e["hidden"]).then_inc(x_in, 16)
            sp.dma_start(e["ident"][:, :], e["ident_in"]).then_inc(x_in, 16)
            sp.wait_ge(x_in, 32)
    layer_norm(nc, dict(DIM=e["DIM"], NW=e["NW"], x_ready=None), e["Y"], None, "start")


V_, TH, K_, A_, B_, Q_, AQ, BQ, EB = range(9)


def gates(nc, e):
    Y, hT, big, ident, MT, E, banks = (e[k] for k in ("Y", "hT", "big", "ident", "MT", "E", "banks"))
    B, WIN, DIM, D, NW, S, C, NC = (e[k] for k in ("B", "WIN", "DIM", "D", "NW", "S", "C", "NC"))
    H2 = S // 512
    with ExitStack() as ctx:
        def sb(name, shape, dt=F32):
            return ctx.enter_context(nc.sbuf_tensor(name, shape, dt))

        def sem(name):
            return nc.alloc_semaphore(name)

        pw = sb("pw", [P, 6, D])
        cl = sb("cl", [P, 18])
        mean = sb("mean", [P, P])
        sel = sb("sel", [P, B, C])
        PAD = 3
        cin = sb("cin", [P, 3, PAD + S])
        cacc = sb("cacc", [P, 2, S])
        sg = sb("sg", [P, 3, S])
        gm = sb("gm", [P, 3, S])
        inj = sb("inj", [P, 2, S])
        aM = sb("aM", [C, B, S])
        eM = sb("eM", [C, B, S])
        ab = sb("ab", [P, 512])
        ex = sb("ex", [P, 512])
        offset = sb("offset", [P, 3])
        s = {n: sem("g_" + n) for n in (
            "w_in pad t_mm t_ev p_mm p_ev m_mm m_ev v abs ex sp conv".split())}
        block = ctx.enter_context(nc.Block())
        ORDER = (3, 4, 5, 0, 1, 2)
        factor, added = (-0.1, 0.9, -0.1), (1.0, 0.05, 0.0)
        cw = lambda i, j: cl[:, 5 * i + j:5 * i + j + 1]

        @block.sync
        def _(sp):
            sp.dma_start(pw[:, :, :], e["proj"]).then_inc(s["w_in"], 16)
            sp.dma_start(cl[:, :], e["cols"]).then_inc(s["w_in"], 16)
            sp.dma_start(mean[:, :], e["mean_in"]).then_inc(s["w_in"], 16)

        @block.gpsimd
        def _(pool):
            pool.wait_ge(s["w_in"], 48)
            for b in range(B):
                pool.tensor_copy(sel[:, b, :].rearrange("p (r c) -> p r c", r=2),
                                 mean[:, b * WIN:(b + 1) * WIN].unsqueeze(1).to_broadcast([P, 2, WIN])).then_inc(s["pad"], 1)
            pool.memset(cin[:, :, 0:PAD], 0.0).then_inc(s["pad"], 1)
            pool.memset(inj[:, :, :], 0.0).then_inc(s["pad"], 1)
            pool.tensor_copy(MT[:, :, :].rearrange("p b (c t) -> p (b c) t", t=C),
                             ident[0:C, 0:C].unsqueeze(1).to_broadcast([C, B * NC, C])).then_inc(s["pad"], 1)
            for i in range(3):
                pool.memset(offset[:, i:i + 1], added[i]).then_inc(s["pad"], 1)

        @block.tensor
        def _(pe):
            for g in range(NW // 4):
                if g >= 2:
                    pe.wait_ge(s["t_ev"], g - 1)
                for j in range(4):
                    w = 4 * g + j
                    mm = pe.transpose(banks[g % 2][:, j * P:(j + 1) * P], Y[:, w * DIM:(w + 1) * DIM], ident[:, :])
                mm.then_inc(s["t_mm"], 1)
            pe.wait_ge(s["w_in"], 48)
            pe.wait_ge(s["t_ev"], NW // 4)
            n = 0
            for i in ORDER:
                for h in range(H2):
                    if n >= 3:
                        pe.wait_ge(s["p_ev"], n - 2)
                    for b in range(B):
                        mm = pe.matmul(banks[2 + n % 3][b * D:(b + 1) * D, :], pw[:, i, :],
                                       hT[:, h * (512 // WIN):(h + 1) * (512 // WIN), b * WIN:(b + 1) * WIN], start=True, stop=True)
                    mm.then_inc(s["p_mm"], 1)
                    n += 1
            pe.wait_ge(s["pad"], B)
            n = 0
            for i in range(3):
                pe.wait_ge(s["p_ev"], 2 * H2) if i < 2 else pe.wait_ge(s["sp"], H2)
                for h in range(H2):
                    if n >= 3:
                        pe.wait_ge(s["m_ev"], n - 2)
                    pe.matmul(banks[5 + n % 3][:, :], mean[:, :], sg[:, i, 512 * h:512 * h + 512],
                              start=True, stop=True).then_inc(s["m_mm"], 1)
                    n += 1
            for i in range(2):
                for b in range(B):
                    for h in range(H2):
                        pe.wait_ge(s["m_ev"], n - 2)
                        pe.matmul(banks[5 + n % 3][0:C, :], sel[:, b, :], sg[:, i, 512 * h:512 * h + 512],
                                  start=True, stop=True).then_inc(s["m_mm"], 1)
                        n += 1

        @block.scalar
        def _(act):
            act.preload_act_table_set(SIGMOID)
            act.wait_ge(s["w_in"], 48)
            n = 0
            for i in ORDER:
                if i == 5:
                    act.preload_act_table_set(LN_EXP)
                for h in range(H2):
                    src = banks[2 + n % 3][:, :]
                    hs = slice(512 * h, 512 * h + 512)
                    act.wait_ge(s["p_mm"], n + 1)
                    if i in (3, 4):
                        act.activation(sg[:, i - 3, hs], src, ACT.Sigmoid, bias=cl[:, 12 + i:13 + i]).then_inc(s["p_ev"], 1)
                    elif i == 5:
                        act.activation(sg[:, 2, hs], src, ACT.Identity, bias=cl[:, 17:18]).then_inc(s["p_ev"], 1)
                        act.wait_ge(s["p_ev"], n + 1)
                        if h:
                            act.wait_ge(s["ex"], 2 * h)
                        act.activation(ab[:, :], sg[:, 2, hs], ACT.Abs).then_inc(s["abs"], 1)
                        act.wait_ge(s["abs"], h + 1)
                        if h:
                            act.wait_ge(s["sp"], h)
                        act.activation(ex[:, :], ab[:, :], ACT.Exp, scale=-1.0).then_inc(s["ex"], 1)
                        act.wait_ge(s["ex"], 2 * h + 1)
                        act.activation(ex[:, :], ex[:, :], ACT.Ln, bias=1.0).then_inc(s["ex"], 1)
                    else:
                        act.activation(cin[:, i, PAD + 512 * h:PAD + 512 * h + 512], src, ACT.Copy).then_inc(s["p_ev"], 1)
                    n += 1
            n = 0
            act.wait_ge(s["pad"], B + 6)
            for i in range(3):
                for h in range(H2):
                    act.wait_ge(s["m_mm"], n + 1)
                    act.activation(gm[:, i, 512 * h:512 * h + 512], banks[5 + n % 3][:, :], ACT.Identity,
                                   bias=offset[:, i:i + 1], scale=factor[i]).then_inc(s["m_ev"], 1)
                    n += 1
            for i, dst in ((0, aM), (1, eM)):
                for b in range(B):
                    for h in range(H2):
                        act.wait_ge(s["m_mm"], n + 1)
                        act.activation(dst[:, b, 512 * h:512 * h + 512], banks[5 + n % 3][0:C, :], ACT.Identity,
                                       bias=offset[0:C, i:i + 1], scale=factor[i]).then_inc(s["m_ev"], 1)
                        n += 1

        @block.vector
        def _(dve):
            steps = [0]

            def link(ins):
                steps[0] += 1
                ins.then_inc(s["v"], 1)
                dve.wait_ge(s["v"], steps[0])

            for g in range(NW // 4):
                dve.wait_ge(s["t_mm"], g + 1)
                dve.tensor_copy(hT[:, 4 * g:4 * (g + 1), :].rearrange("p w n -> p (w n)"), banks[g % 2][:, :]).then_inc(s["t_ev"], 1)
            for h in range(H2):
                hs = slice(512 * h, 512 * h + 512)
                dve.wait_ge(s["ex"], 2 * h + 2)
                dve.scalar_tensor_tensor(out=sg[:, 2, hs], in0=sg[:, 2, hs], scalar=0.0, in1=ex[:, :],
                                         op0=ALU.max, op1=ALU.add).then_inc(s["sp"], 1)
            dve.wait_ge(s["p_ev"], 6 * H2)
            dve.wait_ge(s["pad"], B + 1)
            for i, item in ((0, K_), (1, V_), (2, Q_)):
                link(dve.tensor_scalar(cacc[:, 0, :], cin[:, i, 0:S], cw(i, 0), cw(i, 4), ALU.mult, ALU.add))
                for j in (1, 2, 3):
                    dst = big[:, item, :] if j == 3 else cacc[:, j % 2, :]
                    link(dve.scalar_tensor_tensor(out=dst, in0=cin[:, i, j:j + S], scalar=cw(i, j),
                                                  in1=cacc[:, (j + 1) % 2, :], op0=ALU.mult, op1=ALU.add))
            dve.wait_ge(s["m_ev"], H2 * (3 + 2 * B))
            dve.wait_ge(s["pad"], B + 3)
            starts = lambda t: t.rearrange("p (c t) -> p c t", t=C)[:, :, 0:1]
            for i in range(2):
                link(dve.tensor_copy(starts(inj[:, i, :]), starts(gm[:, i, :])))
                link(dve.memset(starts(gm[:, i, :]), 0.0))
            link(dve.memset(starts(aM[:, :, :].rearrange("p b t -> p (b t)")), 0.0))
            link(dve.memset(starts(eM[:, :, :].rearrange("p b t -> p (b t)")), 0.0))
            link(dve.tensor_tensor_scan(big[:, A_, :], gm[:, 0, :], inj[:, 0, :], 0.0, ALU.mult, ALU.add))
            link(dve.tensor_tensor_scan(big[:, EB, :], gm[:, 1, :], inj[:, 1, :], 0.0, ALU.mult, ALU.add))
            link(dve.tensor_tensor_scan(big[:, B_, :], gm[:, 0, :], big[:, EB, :], 0.0, ALU.mult, ALU.add))
            link(dve.tensor_copy(big[:, TH, :], gm[:, 2, :]))
            fl = lambda t: t.rearrange("p b t -> p (b t)")
            link(dve.tensor_tensor_scan(fl(E[:, :, :]), fl(eM[:, :, :]), fl(MT[:, :, :]), 0.0, ALU.mult, ALU.add))
            link(dve.tensor_tensor_scan(fl(MT[:, :, :]), fl(aM[:, :, :]), fl(E[:, :, :]), 0.0, ALU.mult, ALU.add))
            link(dve.tensor_tensor(big[:, AQ, :], big[:, Q_, :], big[:, A_, :], ALU.mult))
            link(dve.tensor_tensor(big[:, BQ, :], big[:, Q_, :], big[:, B_, :], ALU.mult))

    release(nc, s)


def release(nc, semaphores):
    nc.clear_and_free_semaphores(list(semaphores.values()))
    nc.all_engine_barrier()


def chunks(nc, ctx0, e):
    big, ident, MT, E, banks = (e[k] for k in ("big", "ident", "MT", "E", "banks"))
    B, WIN, DIM, D, NW, S, C, NC = (e[k] for k in ("B", "WIN", "DIM", "D", "NW", "S", "C", "NC"))
    RT = ctx0.enter_context(nc.sbuf_tensor("RT", [D, NW, P], F32))
    BD = B * D
    with ExitStack() as ctx:
        def sb(name, shape, dt=F32):
            return ctx.enter_context(nc.sbuf_tensor(name, shape, dt))

        def sem(name):
            return nc.alloc_semaphore(name)

        staged = sb("staged", [P, 5, C])
        features = sb("features", [D, 2, B, 7, C])
        mix = sb("mix", [C, 2, B, C])
        eta_tail = sb("eta_tail", [C, 2, B])
        by_token = sb("by_token", [C, 2, 5, BD])
        target02 = sb("target02", [C, BD])
        state = sb("state", [D, 2, 3, B, 2, D])
        base_w = sb("base_w", [D, 3, B, D])
        momentum_in_w = sb("momentum_in_w", [D, 3, B, D])
        base_momentum = sb("base_momentum", [D, 3, B, D])
        z_c, z_e, z_e1, sigmoid, slope, hidden_sigmoid, hidden_plus_sigmoid, dz_raw = (sb(n, [C, BD]) for n in ("z_c", "z_e", "z_e1", "sigmoid", "slope", "hidden_sigmoid", "hidden_plus_sigmoid", "dz_raw"))
        hidden = sb("hidden", [C, 2, BD])
        error = sb("error", [C, BD])
        hidden_t = sb("hidden_t", [D, 2, B, C])
        error_t = sb("error_t", [D, B, C])
        grad_squares = sb("grad_squares", [C, 4, BD])
        norms = sb("norms", [C, 4, B])
        products = sb("products", [C, 2, B])
        grad_sq, grad_log, grad_inv, weight = (sb(n, [C, B]) for n in ("grad_sq", "grad_log", "grad_inv", "weight"))
        weights = sb("weights", [C, B, 2])
        dz_w = sb("dz_w", [C, B, 2, D])
        error_w = sb("error_w", [C, B, 2, D])
        dz_q = sb("dz_q", [C, 2, BD])
        error_q = sb("error_q", [C, 2, BD])
        kq_weighted = sb("kq_weighted", [C, B, C])
        hq_weighted = sb("hq_weighted", [C, B, C])
        zq_c, zq_e, zq_e1, sigmoid_q = (sb(n, [C, BD]) for n in ("zq_c", "zq_e", "zq_e1", "sigmoid_q"))
        hidden_q = sb("hidden_q", [C, 3, BD])
        hidden_q_t = sb("hidden_q_t", [D, 3, B, C])
        names = ("momentum_cleared small_products_issued state_loaded features_loaded0 features_loaded1 "
                 "rows_staged mt_staged ee_staged tokens_transposed tokens_in_sbuf target_scaled z_made z_clamped "
                 "z_exp z_exp_plus_one sigmoid_ready hidden_ready slope_product slope_sum slope_ready "
                 "hidden_transposed hidden_t_in_sbuf prediction_made error_ready error_transposed error_t_in_sbuf "
                 "dhidden_made dz_ready hidden_squared keys_squared error_squared dz_squared norms_but_dz dz_norm "
                 "norm_products grad_norm_summed grad_norm_clamped grad_norm_logged grad_rnorm token_weights "
                 "weights_for_w weights_for_momentum dz_weighted error_weighted dz_for_queries error_for_queries "
                 "update_made decayed_w decayed_momentum_part state_base momentum_base w_updated momentum_updated "
                 "keys_by_queries keys_by_queries_weighted query_z_made query_z_clamped query_z_exp "
                 "query_z_exp_plus_one query_sigmoid query_hidden query_hidden_a query_hidden_b "
                 "query_hidden_transposed query_hidden_t_in_sbuf hidden_by_queries hidden_by_queries_weighted "
                 "read_made read_in_sbuf").split()
        s = {n: sem("c_" + n) for n in names}
        block = ctx.enter_context(nc.Block())
        b4 = lambda t: t.rearrange("p (b d) -> p b d", b=B)
        pN, pZ, pR, pT, pQ0, pQ1, pU0, pU1 = banks
        TAIL = NC - 2

        def drive(eng, body):
            body(-1, 1)
            body(0, 0)
            body(1, 1)
            with eng.Fori(2, TAIL, 2) as c:
                body(c, 0, True)
                body(c + 1, 1, True)
            for c in range(TAIL, NC + 1):
                body(c, c % 2)

        def wait(eng, name, c, loop=True):
            if loop or c >= 0:
                eng.wait_ge(s[name], c + 1)

        def settled(eng):
            eng.wait_ge(s["momentum_cleared"], 1)

        def here(c, loop):
            return loop or 0 <= c < NC

        @block.sync
        def _(sp):
            def body(c, par, loop=False):
                n = c + 1
                if not here(n, loop):
                    return
                wait(sp, "update_made", n - 2, loop)
                wait(sp, "query_z_made", n - 2, loop)
                wait(sp, "keys_by_queries", n - 2, loop)
                wait(sp, "momentum_base", n - 2, loop)
                for b in range(B):
                    sp.dma_start(features[:, 1 - par, b, :, :], big[b * D:(b + 1) * D, K_:EB + 1, bass.ds(n * C, C)]
                                 ).then_inc(s["features_loaded%d" % (1 - par)], 16)
            drive(sp, body)

        @block.gpsimd
        def _(pool):
            pool.memset(state[:, 0, :, :, 1, :], 0.0).then_inc(s["momentum_cleared"], 1)

            def body(c, par, loop=False):
                n, R = c + 1, c - 1
                if here(n, loop):
                    wait(pool, "tokens_transposed", n - 1, loop)
                    pool.tensor_copy(staged[:, :, :], big[:, 0:5, bass.ds(n * C, C)]).then_inc(s["rows_staged"], 1)
                if here(c, loop):
                    wait(pool, "tokens_in_sbuf", c)
                    wait(pool, "norms_but_dz", 2 * c - 1, loop)
                    pool.tensor_tensor(grad_squares[:, 3, :], by_token[:, par, 2, :], by_token[:, par, 2, :], ALU.mult).then_inc(s["keys_squared"], 1)
                    wait(pool, "hidden_ready", c)
                    wait(pool, "dz_ready", c - 1, loop)
                    pool.tensor_tensor(hidden_sigmoid[:, :], hidden[:, par, :], sigmoid[:, :], ALU.mult).then_inc(s["slope_product"], 1)
                    pool.tensor_tensor(hidden_plus_sigmoid[:, :], hidden[:, par, :], sigmoid[:, :], ALU.add).then_inc(s["slope_sum"], 1)
                    wait(pool, "slope_product", c)
                    wait(pool, "slope_sum", c)
                    pool.tensor_tensor(slope[:, :], hidden_plus_sigmoid[:, :], hidden_sigmoid[:, :], ALU.subtract).then_inc(s["slope_ready"], 1)
                    wait(pool, "norms_but_dz", 2 * c - 1, loop)
                    pool.tensor_tensor(grad_squares[:, 2, :], hidden[:, par, :], hidden[:, par, :], ALU.mult).then_inc(s["hidden_squared"], 1)
                    wait(pool, "error_ready", c)
                    pool.tensor_tensor(grad_squares[:, 0, :], error[:, :], error[:, :], ALU.mult).then_inc(s["error_squared"], 1)
                if here(R, loop):
                    wait(pool, "query_hidden", R)
                    wait(pool, "query_hidden_transposed", R - 1, loop)
                    pool.tensor_tensor(hidden_q[:, 1, :], hidden_q[:, 0, :], by_token[:, 1 - par, 3, :], ALU.mult).then_inc(s["query_hidden_a"], 1)
                    pool.tensor_tensor(hidden_q[:, 2, :], hidden_q[:, 0, :], by_token[:, 1 - par, 4, :], ALU.mult).then_inc(s["query_hidden_b"], 1)
                if here(c, loop):
                    wait(pool, "token_weights", c)
                    wait(pool, "query_z_made", c - 2, loop)
                    pool.tensor_tensor(b4(dz_q[:, par, :]), b4(dz_raw[:, :]), weight[:, :].unsqueeze(2).to_broadcast([C, B, D]), ALU.mult).then_inc(s["dz_for_queries"], 1)
                    wait(pool, "read_made", c - 2, loop)
                    pool.tensor_tensor(b4(error_q[:, par, :]), b4(error[:, :]), weight[:, :].unsqueeze(2).to_broadcast([C, B, D]), ALU.mult).then_inc(s["error_for_queries"], 1)
                if here(n, loop):
                    wait(pool, "hidden_by_queries_weighted", n - 2, loop)
                    pool.tensor_copy(mix[:, 1 - par, :, :], MT[:, :, bass.ds(n * C, C)]).then_inc(s["mt_staged"], 1)
                    wait(pool, "weights_for_momentum", n - 2, loop)
                    pool.tensor_copy(eta_tail[:, 1 - par, :].unsqueeze(2), E[:, :, bass.ds(n * C + (C - 1), 1)]).then_inc(s["ee_staged"], 1)
            drive(pool, body)

        @block.tensor
        def _(pe):
            pe.wait_ge(s["momentum_cleared"], 1)
            pe.wait_ge(s["state_loaded"], 16 * 3 * B)
            ZK, ZA, ZB, ZQ, ZAQ, ZBQ, ZE = range(7)

            def nat_t(n, loop):
                wait(pe, "rows_staged", n)
                wait(pe, "tokens_in_sbuf", n - 1, loop)
                wait(pe, "dz_ready", n - 1, loop)
                pe.sem_inc(s["small_products_issued"], 1)
                for i in range(5):
                    out = pN[0:C, i * P:(i + 1) * P] if i < 4 else pZ[0:C, 384:512]
                    mm = pe.transpose(out, staged[:, i, :], ident[:, :])
                mm.then_inc(s["tokens_transposed"], 1)

            def body(c, par, loop=False):
                R = c - 1
                rp = 1 - par
                if here(c, loop):
                    settled(pe)
                    wait(pe, "w_updated", c - 1, loop)
                    wait(pe, "tokens_in_sbuf", c)
                    pe.wait_ge(s["features_loaded%d" % par], (c // 2 + 1) * (16 * B))
                    wait(pe, "dz_ready", c - 1, loop)
                    for b in range(B):
                        mm = pe.matmul(pZ[0:C, b * D:(b + 1) * D], features[:, par, b, ZK, :], state[:, par, 0, b, 0, :],
                                       start=True, stop=True)
                    mm.then_inc(s["z_made"], 1)
                if here(R, loop):
                    settled(pe)
                    wait(pe, "keys_by_queries_weighted", R)
                    wait(pe, "dz_for_queries", R)
                    wait(pe, "hidden_by_queries_weighted", R - 1, loop)
                    for b in range(B):
                        o = pR[0:C, 256 + b * D:256 + (b + 1) * D]
                        pe.matmul(o, features[:, rp, b, ZAQ, :], state[:, rp, 0, b, 0, :], start=True, stop=False)
                        pe.matmul(o, features[:, rp, b, ZBQ, :], state[:, rp, 0, b, 1, :], start=False, stop=False)
                        mm = pe.matmul(o, kq_weighted[:, b, :], dz_q[:, rp, b * D:(b + 1) * D], start=False, stop=True)
                    mm.then_inc(s["query_z_made"], 1)
                if here(c, loop):
                    settled(pe)
                    wait(pe, "hidden_ready", c)
                    wait(pe, "error_t_in_sbuf", c - 1, loop)
                    for b in range(B):
                        mm = pe.transpose(pT[0:D, b * C:(b + 1) * C], hidden[:, par, b * D:(b + 1) * D], ident[0:C, 0:C])
                    mm.then_inc(s["hidden_transposed"], 1)
                    settled(pe)
                    wait(pe, "hidden_t_in_sbuf", c)
                    wait(pe, "z_clamped", c)
                    for b in range(B):
                        mm = pe.matmul(pZ[0:C, BD + b * D:BD + (b + 1) * D], hidden_t[:, par, b, :], state[:, par, 1, b, 0, :],
                                       start=True, stop=True)
                    mm.then_inc(s["prediction_made"], 1)
                if here(c, loop):
                    settled(pe)
                    wait(pe, "error_ready", c)
                    wait(pe, "hidden_t_in_sbuf", c)
                    for b in range(B):
                        mm = pe.transpose(pT[0:D, B * C + b * C:B * C + (b + 1) * C], error[:, b * D:(b + 1) * D], ident[0:C, 0:C])
                    mm.then_inc(s["error_transposed"], 1)
                    settled(pe)
                    wait(pe, "error_t_in_sbuf", c)
                    for b in range(B):
                        mm = pe.matmul(pZ[0:C, 2 * BD + b * D:2 * BD + (b + 1) * D], error_t[:, b, :], state[:, par, 2, b, 0, :],
                                       start=True, stop=True)
                    mm.then_inc(s["dhidden_made"], 1)
                    settled(pe)
                    wait(pe, "momentum_updated", c - 1, loop)
                    for b in range(B):
                        mm = pe.matmul(pU1[0:C, 256 + b * C:256 + (b + 1) * C], features[:, par, b, ZK, :], features[:, par, b, ZQ, :],
                                       start=True, stop=True)
                    mm.then_inc(s["keys_by_queries"], 1)
                if here(R, loop):
                    wait(pe, "query_hidden_a", R)
                    wait(pe, "query_hidden_b", R)
                    wait(pe, "query_hidden", R)
                    wait(pe, "read_in_sbuf", R - 1, loop)
                    pe.sem_inc(s["small_products_issued"], 1)
                    for i in range(3):
                        for b in range(B):
                            bank = (pQ0, pQ1)[i // 2]
                            o = (i % 2) * B * C + b * C
                            mm = pe.transpose(bank[0:D, o:o + C], hidden_q[:, i, b * D:(b + 1) * D], ident[0:C, 0:C])
                    mm.then_inc(s["query_hidden_transposed"], 1)
                if here(c + 1, loop):
                    nat_t(c + 1, loop)
                if here(R, loop):
                    settled(pe)
                    wait(pe, "query_hidden_t_in_sbuf", 2 * R + 1)
                    wait(pe, "query_z_clamped", R)
                    for b in range(B):
                        mm = pe.matmul(pR[0:C, b * C:(b + 1) * C], hidden_t[:, rp, b, :], hidden_q_t[:, 0, b, :], start=True, stop=True)
                    mm.then_inc(s["hidden_by_queries"], 1)
                if here(c, loop):
                    settled(pe)
                    wait(pe, "dz_weighted", c)
                    wait(pe, "error_weighted", c)
                    wait(pe, "keys_by_queries_weighted", c)
                    for b in range(B):
                        d = slice(b * D, (b + 1) * D)
                        o = b * 2 * D
                        pe.matmul(pU0[0:D, o:o + 2 * D], by_token[:, par, 2, d], dz_w[:, b, :, :].rearrange("p a d -> p (a d)"),
                                  start=True, stop=True)
                        pe.matmul(pU0[0:D, 256 + o:256 + o + 2 * D], hidden[:, par, d], error_w[:, b, :, :].rearrange("p a d -> p (a d)"),
                                  start=True, stop=True)
                        pe.matmul(pU1[0:D, o:o + D], error_w[:, b, 0, :], hidden[:, par, d], start=True, stop=True)
                        mm = pe.matmul(pU1[0:D, o + D:o + 2 * D], error_w[:, b, 1, :], hidden[:, par, d], start=True, stop=True)
                    mm.then_inc(s["update_made"], 1)
                if here(R, loop):
                    settled(pe)
                    wait(pe, "hidden_by_queries_weighted", R)
                    wait(pe, "error_for_queries", R)
                    for b in range(B):
                        o = pQ1[0:D, B * C + b * C:B * C + (b + 1) * C]
                        pe.matmul(o, state[:, rp, 1, b, 0, :], hidden_q_t[:, 1, b, :], start=True, stop=False)
                        pe.matmul(o, state[:, rp, 1, b, 1, :], hidden_q_t[:, 2, b, :], start=False, stop=False)
                        mm = pe.matmul(o, error_q[:, rp, b * D:(b + 1) * D], hq_weighted[:, b, :], start=False, stop=True)
                    mm.then_inc(s["read_made"], 1)

            drive(pe, body)

        @block.scalar
        def _(act):
            for m, src in ((0, e["mW1T"]), (1, e["mW2T"]), (2, e["mW2"])):
                for b in range(B):
                    act.dma_start(state[:, 0, m, b, 0, :], src).then_inc(s["state_loaded"], 16)
            act.preload_act_table_set(LN_EXP)

            def body(c, par, loop=False):
                R, n = c - 1, c + 1
                if here(c, loop):
                    wait(act, "z_clamped", c)
                    wait(act, "z_exp_plus_one", c - 1, loop)
                    act.activation(z_e[:, :], z_c[:, :], ACT.Exp, scale=-1.0).then_inc(s["z_exp"], 1)
                if here(R, loop):
                    wait(act, "query_z_clamped", R)
                    wait(act, "query_z_exp_plus_one", R - 1, loop)
                    act.activation(zq_e[:, :], zq_c[:, :], ACT.Exp, scale=-1.0).then_inc(s["query_z_exp"], 1)
                if here(c, loop):
                    wait(act, "hidden_transposed", c)
                    wait(act, "hidden_by_queries", c - 2, loop)
                    act.activation(hidden_t[:, par, :, :].rearrange("p b t -> p (b t)"), pT[0:D, 0:B * C], ACT.Copy).then_inc(s["hidden_t_in_sbuf"], 1)
                    wait(act, "error_transposed", c)
                    wait(act, "dhidden_made", c - 1, loop)
                    act.activation(error_t[:, :, :].rearrange("p b t -> p (b t)"), pT[0:D, B * C:2 * B * C], ACT.Copy).then_inc(s["error_t_in_sbuf"], 1)
                if here(c, loop):
                    wait(act, "grad_norm_clamped", c)
                    act.activation(grad_log[:, :], grad_sq[:, :], ACT.Ln).then_inc(s["grad_norm_logged"], 1)
                    wait(act, "grad_norm_logged", c)
                    wait(act, "token_weights", c - 1, loop)
                    act.activation(grad_inv[:, :], grad_log[:, :], ACT.Exp, scale=-0.5).then_inc(s["grad_rnorm"], 1)
                if here(R, loop):
                    wait(act, "query_hidden_transposed", R)
                    wait(act, "read_made", R - 1, loop)
                    hf = hidden_q_t[:, :, :, :].rearrange("p i b t -> p (i b t)")
                    act.activation(hf[:, 0:512], pQ0[0:D, :], ACT.Copy).then_inc(s["query_hidden_t_in_sbuf"], 1)
                    act.activation(hf[:, 512:768], pQ1[0:D, 0:256], ACT.Copy).then_inc(s["query_hidden_t_in_sbuf"], 1)
                if here(n, loop):
                    wait(act, "tokens_transposed", n)
                    for q in ("keys_squared", "target_scaled", "token_weights", "update_made"):
                        wait(act, q, n - 2, loop)
                    for q in ("query_hidden_a", "query_hidden_b"):
                        wait(act, q, n - 2, loop)
                    act.activation(by_token[:, 1 - par, 0:4, :].rearrange("p i d -> p (i d)"), pN[0:C, :], ACT.Copy)
                    act.activation(by_token[:, 1 - par, 4, :], pZ[0:C, 384:512], ACT.Copy).then_inc(s["tokens_in_sbuf"], 1)
                if here(R, loop):
                    wait(act, "read_made", R)
                    act.activation(RT[:, bass.ds(R * (C // WIN), C // WIN), :].rearrange("p w (b i) -> p w b i", b=B),
                                   pQ1[0:D, B * C:2 * B * C].rearrange("p (b w i) -> p w b i", b=B, i=WIN), ACT.Copy).then_inc(s["read_in_sbuf"], 1)

            drive(act, body)

        @block.vector
        def _(dve):
            def body(c, par, loop=False):
                R = c - 1
                rp = 1 - par
                TT = dve.tensor_tensor
                if here(c, loop):
                    wait(dve, "z_made", c)
                    wait(dve, "hidden_ready", c - 1, loop)
                    dve.tensor_scalar(z_c[:, :], pZ[0:C, 0:BD], -80.0, None, ALU.max).then_inc(s["z_clamped"], 1)
                    wait(dve, "tokens_in_sbuf", c)
                    wait(dve, "error_ready", c - 1, loop)
                    dve.tensor_scalar(target02[:, :], by_token[:, par, 0, :], 0.2, None, ALU.mult).then_inc(s["target_scaled"], 1)
                    wait(dve, "z_exp", c)
                    wait(dve, "sigmoid_ready", c - 1, loop)
                    dve.tensor_scalar(z_e1[:, :], z_e[:, :], 1.0, None, ALU.add).then_inc(s["z_exp_plus_one"], 1)
                    wait(dve, "z_exp_plus_one", c)
                    wait(dve, "slope_sum", c - 1, loop)
                    wait(dve, "slope_product", c - 1, loop)
                    dve.reciprocal(sigmoid[:, :], z_e1[:, :]).then_inc(s["sigmoid_ready"], 1)
                    wait(dve, "sigmoid_ready", c)
                    wait(dve, "update_made", c - 2, loop)
                    wait(dve, "hidden_squared", c - 2, loop)
                    TT(hidden[:, par, :], z_c[:, :], sigmoid[:, :], ALU.mult).then_inc(s["hidden_ready"], 1)
                if here(R, loop):
                    wait(dve, "query_z_made", R)
                    wait(dve, "query_hidden", R - 1, loop)
                    dve.tensor_scalar(zq_c[:, :], pR[0:C, 256:256 + BD], -80.0, None, ALU.max).then_inc(s["query_z_clamped"], 1)
                if here(c, loop):
                    W = lambda k: state[:, par, :, :, k, :]
                    last = lambda i: features[:, par, :, i, C - 1].unsqueeze(1).unsqueeze(3).to_broadcast([D, 3, B, D])
                    wait(dve, "w_updated", c - 1, loop)
                    wait(dve, "momentum_updated", c - 1, loop)
                    TT(base_w[:, :, :, :], W(0), last(1), ALU.mult).then_inc(s["decayed_w"], 1)
                if here(R, loop):
                    wait(dve, "query_z_exp", R)
                    wait(dve, "query_sigmoid", R - 1, loop)
                    dve.tensor_scalar(zq_e1[:, :], zq_e[:, :], 1.0, None, ALU.add).then_inc(s["query_z_exp_plus_one"], 1)
                    wait(dve, "query_z_exp_plus_one", R)
                    dve.reciprocal(sigmoid_q[:, :], zq_e1[:, :]).then_inc(s["query_sigmoid"], 1)
                if here(c, loop):
                    wait(dve, "prediction_made", c)
                    wait(dve, "target_scaled", c)
                    wait(dve, "error_for_queries", c - 1, loop)
                    wait(dve, "error_transposed", c - 1, loop)
                    wait(dve, "error_weighted", c - 1, loop)
                    dve.scalar_tensor_tensor(out=error[:, :], in0=pZ[0:C, BD:2 * BD], scalar=0.2, in1=target02[:, :],
                                             op0=ALU.mult, op1=ALU.subtract).then_inc(s["error_ready"], 1)
                if here(R, loop):
                    wait(dve, "query_sigmoid", R)
                    wait(dve, "query_hidden_transposed", R - 1, loop)
                    wait(dve, "query_hidden_a", R - 1, loop)
                    wait(dve, "query_hidden_b", R - 1, loop)
                    TT(hidden_q[:, 0, :], zq_c[:, :], sigmoid_q[:, :], ALU.mult).then_inc(s["query_hidden"], 1)
                if here(c, loop):
                    TT(momentum_in_w[:, :, :, :], W(1), last(2), ALU.mult).then_inc(s["decayed_momentum_part"], 1)
                    TT(base_momentum[:, :, :, :], W(1), last(6), ALU.mult).then_inc(s["momentum_base"], 1)
                    wait(dve, "decayed_w", c)
                    wait(dve, "decayed_momentum_part", c)
                    TT(base_w[:, :, :, :], base_w[:, :, :, :], momentum_in_w[:, :, :, :], ALU.add).then_inc(s["state_base"], 1)
                    wait(dve, "hidden_squared", c)
                    wait(dve, "keys_squared", c)
                    wait(dve, "error_squared", c)
                    wait(dve, "norm_products", c - 1, loop)
                    dve.tensor_reduce(norms[:, 2:4, :], grad_squares[:, 2:4, :].rearrange("p k (b d) -> p k b d", b=B), AX.X, ALU.add).then_inc(s["norms_but_dz"], 1)
                    dve.tensor_reduce(norms[:, 0, :], b4(grad_squares[:, 0, :]), AX.X, ALU.add).then_inc(s["norms_but_dz"], 1)
                    wait(dve, "dhidden_made", c)
                    wait(dve, "slope_ready", c)
                    wait(dve, "dz_for_queries", c - 1, loop)
                    TT(dz_raw[:, :], pZ[0:C, 2 * BD:3 * BD], slope[:, :], ALU.mult).then_inc(s["dz_ready"], 1)
                    wait(dve, "dz_ready", c)
                    TT(grad_squares[:, 1, :], dz_raw[:, :], dz_raw[:, :], ALU.mult).then_inc(s["dz_squared"], 1)
                    wait(dve, "dz_squared", c)
                    dve.tensor_reduce(norms[:, 1, :], b4(grad_squares[:, 1, :]), AX.X, ALU.add).then_inc(s["dz_norm"], 1)
                    wait(dve, "dz_norm", c)
                    wait(dve, "norms_but_dz", 2 * c + 1)
                    TT(products[:, :, :], norms[:, 0:2, :], norms[:, 2:4, :], ALU.mult).then_inc(s["norm_products"], 1)
                    wait(dve, "norm_products", c)
                    wait(dve, "grad_norm_logged", c - 1, loop)
                    TT(grad_sq[:, :], products[:, 0, :], products[:, 1, :], ALU.add).then_inc(s["grad_norm_summed"], 1)
                    wait(dve, "grad_norm_summed", c)
                    dve.tensor_scalar(grad_sq[:, :], grad_sq[:, :], 1e-12, None, ALU.max).then_inc(s["grad_norm_clamped"], 1)
                if here(c, loop):
                    wait(dve, "grad_rnorm", c)
                    wait(dve, "dz_for_queries", c - 1, loop)
                    wait(dve, "error_for_queries", c - 1, loop)
                    dve.scalar_tensor_tensor(out=weight[:, :], in0=grad_inv[:, :], scalar=1.0, in1=b4(by_token[:, par, 1, :])[:, :, 0],
                                             op0=ALU.min, op1=ALU.mult).then_inc(s["token_weights"], 1)
                    wait(dve, "token_weights", c)
                    wait(dve, "mt_staged", c)
                    wait(dve, "ee_staged", c)
                    wait(dve, "dz_weighted", c - 1, loop)
                    wait(dve, "error_weighted", c - 1, loop)
                    TT(weights[:, :, 0], weight[:, :], mix[:, par, :, C - 1], ALU.mult).then_inc(s["weights_for_w"], 1)
                    TT(weights[:, :, 1], weight[:, :], eta_tail[:, par, :], ALU.mult).then_inc(s["weights_for_momentum"], 1)
                    wait(dve, "weights_for_w", c)
                    wait(dve, "weights_for_momentum", c)
                    wait(dve, "update_made", c - 1, loop)
                    ws = weights[:, :, :].unsqueeze(3).to_broadcast([C, B, 2, D])
                    TT(dz_w[:, :, :, :], b4(dz_raw[:, :]).unsqueeze(2).to_broadcast([C, B, 2, D]), ws, ALU.mult).then_inc(s["dz_weighted"], 1)
                    TT(error_w[:, :, :, :], b4(error[:, :]).unsqueeze(2).to_broadcast([C, B, 2, D]), ws, ALU.mult).then_inc(s["error_weighted"], 1)
                if here(c, loop):
                    wait(dve, "keys_by_queries", c)
                    wait(dve, "mt_staged", c)
                    wait(dve, "query_z_made", c - 1, loop)
                    TT(kq_weighted[:, :, :], pU1[0:C, 256:512].rearrange("p (b t) -> p b t", b=B), mix[:, par, :, :], ALU.mult).then_inc(s["keys_by_queries_weighted"], 1)
                if here(R, loop):
                    wait(dve, "hidden_by_queries", R)
                    wait(dve, "read_made", R - 1, loop)
                    TT(hq_weighted[:, :, :], pR[0:C, 0:B * C].rearrange("p (b t) -> p b t", b=B), mix[:, rp, :, :], ALU.mult).then_inc(s["hidden_by_queries_weighted"], 1)
                if here(c, loop):
                    wait(dve, "update_made", c)
                    wait(dve, "state_base", c)
                    wait(dve, "momentum_base", c)
                    for k, base in ((0, base_w), (1, base_momentum)):
                        mm = TT(state[:, 1 - par, 0, :, k, :], base[:, 0, :, :],
                                pU0[0:D, 0:256].rearrange("p (b k d) -> p b k d", b=B, k=2)[:, :, k, :], ALU.add)
                    mm.then_inc(s["w_updated"], 1)
                    wait(dve, "read_made", c - 1, loop)
                    for k, base in ((0, base_w), (1, base_momentum)):
                        TT(state[:, 1 - par, 1, :, k, :], base[:, 1, :, :],
                           pU0[0:D, 256:512].rearrange("p (b k d) -> p b k d", b=B, k=2)[:, :, k, :], ALU.add)
                        mm = TT(state[:, 1 - par, 2, :, k, :], base[:, 2, :, :],
                                pU1[0:D, 0:256].rearrange("p (b k d) -> p b k d", b=B, k=2)[:, :, k, :], ALU.add)
                    mm.then_inc(s["momentum_updated"], 1)

            drive(dve, body)
    release(nc, s)
    return RT


def output(nc, e):
    Y, hT, banks, RT = e["Y"], e["hT"], e["banks"], e["RT"]
    B, WIN, DIM, D, NW, S = (e[k] for k in ("B", "WIN", "DIM", "D", "NW", "S"))
    G = 4
    GROUPS = NW // G
    N = G * DIM
    with ExitStack() as ctx:
        def sb(name, shape, dt=F32):
            return ctx.enter_context(nc.sbuf_tensor(name, shape, dt))

        def sem(name):
            return nc.alloc_semaphore(name)

        woT = sb("woT", [D, DIM])
        gwT = sb("gwT", [P, DIM])
        ng = sb("ng", [P, DIM])
        gbb = sb("gbb", [P, DIM])
        osq = sb("osq", [P, 2, N])
        ms = sb("ms", [P, GROUPS, G])
        lm = sb("lm", [P, GROUPS, G])
        rm = sb("rm", [P, GROUPS, G])
        on = sb("on", [P, 2, N])
        ga = sb("ga", [P, 2, N])
        ep = sb("ep6", [P, 1])
        s = {n: sem("o_" + n) for n in "w_in ep o_mm g_mm sq ms lm rm on on2 ga ga2 y".split()}
        block = ctx.enter_context(nc.Block())
        w3 = lambda t: t.rearrange("p (w n) -> p w n", n=DIM)
        bc = lambda t: t[:, :].unsqueeze(1).to_broadcast([P, G, DIM])

        @block.sync
        def _(sp):
            sp.dma_start(woT[:, :], e["WoT"]).then_inc(s["w_in"], 16)
            sp.dma_start(gwT[:, :], e["gWT"]).then_inc(s["w_in"], 16)
            sp.dma_start(ng[:, :], e["norm_g"].unsqueeze(0).to_broadcast([P, DIM])).then_inc(s["w_in"], 16)
            sp.dma_start(gbb[:, :], e["gb"].unsqueeze(0).to_broadcast([P, DIM])).then_inc(s["w_in"], 16)

        @block.tensor
        def _(pe):
            pe.wait_ge(s["w_in"], 64)
            for g in range(GROUPS):
                if g >= 2:
                    pe.wait_ge(s["on"], g - 1)
                for j in range(G):
                    w = G * g + j
                    mm = pe.matmul(banks[g % 2][:, j * DIM:(j + 1) * DIM], RT[:, w, :], woT[:, :], start=True, stop=True)
                mm.then_inc(s["o_mm"], 1)
                if g >= 2:
                    pe.wait_ge(s["ga"], g - 1)
                for j in range(G):
                    w = G * g + j
                    mm = pe.matmul(banks[2 + g % 2][:, j * DIM:(j + 1) * DIM], hT[:, w, :], gwT[:, :], start=True, stop=True)
                mm.then_inc(s["g_mm"], 1)

        @block.scalar
        def _(act):
            act.preload_act_table_set(LN_EXP)
            act.wait_ge(s["ep"], 1)
            for g in range(GROUPS):
                act.wait_ge(s["o_mm"], g + 1)
                if g >= 2:
                    act.wait_ge(s["ms"], g - 1)
                act.activation(osq[:, g % 2, :], banks[g % 2][:, :], ACT.Square).then_inc(s["sq"], 1)
                act.wait_ge(s["ms"], g + 1)
                act.activation(lm[:, g, :], ms[:, g, :], ACT.Ln, bias=ep[:, 0:1], scale=1.0 / DIM).then_inc(s["lm"], 1)
                act.wait_ge(s["lm"], g + 1)
                act.activation(rm[:, g, :], lm[:, g, :], ACT.Exp, scale=-0.5).then_inc(s["rm"], 1)

        @block.vector
        def _(dve):
            dve.memset(ep[:, :], 1e-6).then_inc(s["ep"], 1)
            dve.wait_ge(s["w_in"], 64)
            for g in range(GROUPS):
                r = g % 2
                dve.wait_ge(s["sq"], g + 1)
                dve.tensor_reduce(ms[:, g, :], w3(osq[:, r, :]), AX.X, ALU.add).then_inc(s["ms"], 1)
                if g >= 2:
                    dve.wait_ge(s["y"], g - 1)
                dve.wait_ge(s["g_mm"], g + 1)
                dve.tensor_tensor(w3(ga[:, r, :]), w3(banks[2 + r][:, :]), bc(gbb), ALU.add).then_inc(s["ga"], 1)
                dve.wait_ge(s["ga"], g + 1)
                dve.tensor_tensor(w3(ga[:, r, :]), w3(ga[:, r, :]), bc(ng), ALU.mult).then_inc(s["ga2"], 1)
                dve.wait_ge(s["rm"], g + 1)
                dve.tensor_tensor(w3(on[:, r, :]), w3(banks[r][:, :]), rm[:, g, :].unsqueeze(2).to_broadcast([P, G, DIM]),
                                  ALU.mult).then_inc(s["on"], 1)
                dve.wait_ge(s["ga2"], g + 1)
                dve.wait_ge(s["on"], g + 1)
                dve.tensor_tensor(Y[:, g * N:(g + 1) * N], ga[:, r, :], on[:, r, :], ALU.mult).then_inc(s["y"], 1)

def network(nc, hidden, proj, cols, mW1T, mW2T, mW2, WoT, gWT, norm_g, gb, Wqkv, q_scale, k_scale, Wo, ln_g, ln_b,
            W1, b1, W2, b2, rotary, masks, ident_in, center_in, mean_in, out):
    x_mid = nc.dram_tensor("x_mid", hidden.shape, F32, kind="Internal").ap()
    memory(nc, hidden, proj, cols, mW1T, mW2T, mW2, WoT, gWT, norm_g, gb, mean_in, ident_in, x_mid)
    transformer(nc, x_mid, Wqkv, q_scale, k_scale, Wo, ln_g, ln_b, W1, b1, W2, b2, rotary, masks, ident_in, center_in, out,
                DEPTH=Wqkv.shape[0])


def shape_constants(tokens, window, head_dim, batches):
    half = np.arange(0, head_dim, 2, dtype=np.float32)
    inv_freq = (1.0 / 10000.0 ** (half / head_dim)).astype(np.float32)
    t = np.arange(tokens, dtype=np.float32)
    freqs = t[:, None] * inv_freq[None, :]
    base = ((half + 0.4 * head_dim) / (1.4 * head_dim)).astype(np.float32)
    power = ((t - tokens // 2) / (window // 2)).astype(np.float32)
    scale = (base[None, :] ** power[:, None]).astype(np.float32)
    inv = np.float32(1.0) / scale
    tables = np.stack([np.cos(freqs) * scale, np.sin(freqs) * scale, np.cos(freqs) * inv, np.sin(freqs) * inv], 1)
    tables = tables.astype(np.float32).reshape(tokens // window, window, 2 * head_dim).transpose(1, 0, 2)
    tables = np.broadcast_to(tables[None], (batches,) + tables.shape).reshape(batches * window, -1)
    i, j = np.arange(window)[:, None], np.arange(window)[None, :]
    own = np.where(i < j, -1e30, 0.0)
    prev = np.where(i > j, -1e30, 0.0)
    none = np.full((window, window), -1e30)
    masks = np.stack([np.concatenate(pair, 1) for pair in ((own, none), (own, prev), (prev, own))], 1)
    masks = np.broadcast_to(masks[None], (batches,) + masks.shape).reshape(batches * window, 3, 2 * window)
    eye = np.eye(batches * window, dtype=np.float32)
    return dict(rotary=tables, masks=masks.astype(np.float32), ident_in=eye,
                center_in=eye - np.float32(1.0 / (batches * window)),
                mean_in=np.kron(np.eye(batches), np.full((window, window), 1.0 / window)).astype(np.float32))


def kernel(**inputs):
    import concourse.bacc as _bacc
    from concourse.bass_utils import run_bass_kernel_spmd as _run

    attn = lambda name: np.asarray(inputs["L0_attn_" + name])
    ffn = lambda name: np.asarray(inputs["L0_ffn_" + name])
    hidden = attn("hidden")
    batches, tokens, dim = hidden.shape
    window = P // batches
    windows = tokens // window
    arrays = dict(
        hidden=hidden.reshape(batches, windows, window, dim).transpose(0, 2, 1, 3).reshape(P, windows * dim),
        proj=np.stack([attn(n).T for n in ("Wk", "Wv", "Wq", "aW", "eW", "tW")], 1),
        cols=np.tile(np.concatenate([np.concatenate([attn(w), attn(b)[:, None]], 1)
                                     for w, b in (("ckw", "ckb"), ("cvw", "cvb"), ("cqw", "cqb"))]
                                    + [attn(n)[:, None] for n in ("ab", "eb", "tb")], 1), (batches, 1)),
        mW1T=attn("mW1").T, mW2T=attn("mW2").T, mW2=attn("mW2"), WoT=attn("Wo").T, gWT=attn("gW").T,
        norm_g=attn("norm_g"), gb=attn("gb"),
        Wqkv=ffn("Wqkv"), q_scale=ffn("q_scale"), k_scale=ffn("k_scale"), Wo=ffn("Wo"),
        ln_g=ffn("ln_g").T, ln_b=ffn("ln_b").T, W1=ffn("W1"), b1=ffn("b1"), W2=ffn("W2"), b2=ffn("b2"),
        **shape_constants(tokens, window, inputs["L0_ffn_q_scale"].shape[1], batches))
    nc = _bacc.Bacc("TRN2", target_bir_lowering=False, num_devices=1)
    feeds, aps = {}, {}
    for name, a in arrays.items():
        a = np.ascontiguousarray(a)
        feeds["in_" + name] = a
        aps[name] = nc.dram_tensor("in_" + name, a.shape, mybir.dt.from_np(a.dtype), kind="ExternalInput").ap()
    out = nc.dram_tensor("stream_out", (P, windows * dim), F32, kind="ExternalOutput").ap()
    network(nc, out=out, **aps)
    result = _run(nc, [feeds], core_ids=[0]).results[0]["stream_out"]
    return result.reshape(batches, window, windows, dim).transpose(0, 2, 1, 3).reshape(batches, tokens, dim)
```
